# Optimizing a Trainium2 kernel written in Bass

```python
import numpy as np
import jax
import jax.numpy as jnp

def _softmax(x, axis=-1):
    return jax.nn.softmax(x, axis=axis)

def _gelu(x):
    return jax.nn.gelu(x, approximate=True)

def _silu(x):
    return jax.nn.silu(x)

def _sigmoid(x):
    return jax.nn.sigmoid(x)

def _layernorm(x, axis=-1, eps=1e-05):
    m = jnp.mean(x, axis=axis, keepdims=True)
    v = jnp.var(x, axis=axis, keepdims=True)
    return (x - m) / jnp.sqrt(v + eps)

def _scatter_add(tgt, idx, src, axis=0):
    return tgt.at[idx].add(src)

def _segment_sum(src, seg, n):
    return jax.ops.segment_sum(src, seg, n)
kernel_name = 'mk_seq_preln_d2_jaxref_r8_015aed'

def setup_inputs(seed: int=0):
    np.random.seed(seed)
    _w = jnp.asarray

    def _L0_attn_setup():
        import jax, jax.numpy as jnp
        import numpy as np
        key = jax.random.key(seed)
        ks = jax.random.split(key, 8)
        B, L, D = (4, 256, 256)
        H, Dh, S = (24, 64, 64)
        Di = H * Dh
        P = H * (1 + 2 * S)
        return {'hidden_states': jax.random.normal(ks[0], (B, L, D), jnp.float32), 'norm_w': jnp.ones((D,), jnp.float32), 'in_proj_w': jax.random.normal(ks[1], (2 * Di, D), jnp.float32) * 0.02, 'in_proj_b': jnp.zeros((2 * Di,), jnp.float32), 'conv_w': jax.random.normal(ks[2], (Di, 1, 4), jnp.float32) * 0.2, 'conv_b': jnp.zeros((Di,), jnp.float32), 'x_proj_w': jax.random.normal(ks[3], (P, Di), jnp.float32) * 0.02, 'x_proj_b': jnp.zeros((P,), jnp.float32), 'A_log': jnp.full((H,), np.log(0.5), jnp.float32), 'log2_alpha_base': jnp.full((H,), -1.0, jnp.float32), 'log2_beta': jnp.zeros((H,), jnp.float32), 'surprise_ema': jnp.ones((H,), jnp.float32), 'out_proj_w': jax.random.normal(ks[4], (D, Di), jnp.float32) * 0.02, 'out_proj_b': jnp.zeros((D,), jnp.float32), 'res_gate': jnp.full((1,), 1.0 / np.sqrt(2 * 24), jnp.float32)}
    _L0_attn_in = _L0_attn_setup()

    def _L0_ffn_setup():
        import jax, jax.numpy as jnp
        import numpy as np
        H, I, E, K = (256, 512, 8, 2)
        B, S = (1, 256)

        def _silu_mul(gu):
            d = gu.shape[-1] // 2
            return jax.nn.silu(gu[..., :d]) * gu[..., d:]
        key = jax.random.key(seed)
        ks = jax.random.split(key, 6)
        w_scale = 0.02
        return {'x': jax.random.normal(ks[0], (B, S, H), jnp.float32), 'gate_w': jax.random.normal(ks[1], (H, E), jnp.float32) * w_scale, 'base_gate_up': jax.random.normal(ks[2], (H, 2 * I), jnp.float32) * w_scale, 'base_down': jax.random.normal(ks[3], (I, H), jnp.float32) * w_scale, 'expert_gate_up': jax.random.normal(ks[4], (E, H, 2 * I), jnp.float32) * w_scale, 'expert_down': jax.random.normal(ks[5], (E, I, H), jnp.float32) * w_scale}
    _L0_ffn_in = _L0_ffn_setup()

    def _L1_attn_setup():
        import jax, jax.numpy as jnp
        import numpy as np
        import math
        N_EMBD = 256
        N_HEADS = 16
        HEAD_DIM = N_EMBD // N_HEADS
        CTX = 256

        def alibi_bias(seq_len: int, n_heads: int) -> jnp.ndarray:
            i = jnp.arange(seq_len)[:, None]
            j = jnp.arange(seq_len)[None, :]
            pos = jnp.where(j <= i, (j - i).astype(jnp.float32), 0.0)
            slopes = 2.0 ** (-8.0 / jnp.arange(1, n_heads + 1, dtype=jnp.float32))
            return slopes[:, None, None] * pos[None, :, :]

        def causal_mask(seq_len: int) -> jnp.ndarray:
            i = jnp.arange(seq_len)[:, None]
            j = jnp.arange(seq_len)[None, :]
            return jnp.where(j > i, -jnp.inf, 0.0).astype(jnp.float32)
        key = jax.random.key(seed)
        k_x, k_qkv, k_o = jax.random.split(key, 3)
        scale = 1.0 / math.sqrt(N_EMBD)
        x = jax.random.normal(k_x, (2, CTX, N_EMBD), dtype=jnp.float32)
        W_qkv = jax.random.normal(k_qkv, (N_EMBD, 3 * N_EMBD), dtype=jnp.float32) * scale
        W_o = jax.random.normal(k_o, (N_EMBD, N_EMBD), dtype=jnp.float32) * scale
        return {'x': x, 'W_qkv': W_qkv, 'W_o': W_o}
    _L1_attn_in = _L1_attn_setup()

    def _L1_ffn_setup():
        import jax, jax.numpy as jnp
        import numpy as np
        B, T, D = (1, 256, 256)
        E, K, F = (64, 4, 64)
        S, SF = (2, 64 * 4)
        CAP = 32

        def _moe_forward(x, router_w, router_bias, gate_w, up_w, down_w, sh_gate_w, sh_up_w, sh_down_w):
            b, t, d = x.shape
            flat = x.reshape(b * t, d)
            N = flat.shape[0]
            logits = flat @ router_w.T
            scores = jax.nn.softmax(logits, axis=-1)
            _, topk_idx = jax.lax.top_k(logits + router_bias, K)
            topk_w = jnp.take_along_axis(scores, topk_idx, axis=-1)
            topk_w = topk_w / topk_w.sum(axis=-1, keepdims=True)
            P = N * K
            e_flat = topk_idx.reshape(-1)
            t_flat = jnp.repeat(jnp.arange(N), K)
            w_flat = topk_w.reshape(-1)
            order = jnp.argsort(e_flat)
            e_s, t_s, w_s = (e_flat[order], t_flat[order], w_flat[order])
            counts = jnp.bincount(e_s, length=E)
            starts = jnp.concatenate([jnp.zeros((1,), counts.dtype), jnp.cumsum(counts)[:-1]])
            pos = jnp.arange(P) - starts[e_s]
            slot = jnp.where(pos < CAP, pos, CAP)
            tok_table = jnp.zeros((E, CAP + 1), jnp.int32).at[e_s, slot].set(t_s)[:, :CAP]
            w_table = jnp.zeros((E, CAP + 1), w_s.dtype).at[e_s, slot].set(w_s)[:, :CAP]
            xg = flat[tok_table]
            g = jnp.einsum('ecd,efd->ecf', xg, gate_w)
            u = jnp.einsum('ecd,efd->ecf', xg, up_w)
            y = jnp.einsum('ecf,edf->ecd', jax.nn.silu(g) * u, down_w)
            out = jnp.zeros_like(flat).at[tok_table.reshape(-1)].add((y * w_table[..., None]).reshape(-1, d))
            sg = jnp.einsum('nd,sfd->nsf', flat, sh_gate_w)
            su = jnp.einsum('nd,sfd->nsf', flat, sh_up_w)
            out = out + jnp.einsum('nsf,sdf->nd', jax.nn.silu(sg) * su, sh_down_w)
            return out.reshape(b, t, d)
        key = jax.random.key(seed)
        ks = jax.random.split(key, 9)
        s = 0.02
        return {'x': jax.random.normal(ks[0], (B, T, D), jnp.float32), 'router_w': jax.random.normal(ks[1], (E, D), jnp.float32) * s, 'router_bias': jnp.zeros((E,), jnp.float32), 'gate_w': jax.random.normal(ks[2], (E, F, D), jnp.float32) * s, 'up_w': jax.random.normal(ks[3], (E, F, D), jnp.float32) * s, 'down_w': jax.random.normal(ks[4], (E, D, F), jnp.float32) * s, 'sh_gate_w': jax.random.normal(ks[5], (S, SF, D), jnp.float32) * s, 'sh_up_w': jax.random.normal(ks[6], (S, SF, D), jnp.float32) * s, 'sh_down_w': jax.random.normal(ks[7], (S, D, SF), jnp.float32) * s}
    _L1_ffn_in = _L1_ffn_setup()
    _d = {'L0_attn_hidden_states': _L0_attn_in['hidden_states'], 'L0_attn_norm_w': _L0_attn_in['norm_w'], 'L0_attn_in_proj_w': _L0_attn_in['in_proj_w'], 'L0_attn_in_proj_b': _L0_attn_in['in_proj_b'], 'L0_attn_conv_w': _L0_attn_in['conv_w'], 'L0_attn_conv_b': _L0_attn_in['conv_b'], 'L0_attn_x_proj_w': _L0_attn_in['x_proj_w'], 'L0_attn_x_proj_b': _L0_attn_in['x_proj_b'], 'L0_attn_A_log': _L0_attn_in['A_log'], 'L0_attn_log2_alpha_base': _L0_attn_in['log2_alpha_base'], 'L0_attn_log2_beta': _L0_attn_in['log2_beta'], 'L0_attn_surprise_ema': _L0_attn_in['surprise_ema'], 'L0_attn_out_proj_w': _L0_attn_in['out_proj_w'], 'L0_attn_out_proj_b': _L0_attn_in['out_proj_b'], 'L0_attn_res_gate': _L0_attn_in['res_gate'], 'L0_ffn_gate_w': _L0_ffn_in['gate_w'], 'L0_ffn_base_gate_up': _L0_ffn_in['base_gate_up'], 'L0_ffn_base_down': _L0_ffn_in['base_down'], 'L0_ffn_expert_gate_up': _L0_ffn_in['expert_gate_up'], 'L0_ffn_expert_down': _L0_ffn_in['expert_down'], 'L1_attn_W_qkv': _L1_attn_in['W_qkv'], 'L1_attn_W_o': _L1_attn_in['W_o'], 'L1_ffn_router_w': _L1_ffn_in['router_w'], 'L1_ffn_router_bias': _L1_ffn_in['router_bias'], 'L1_ffn_gate_w': _L1_ffn_in['gate_w'], 'L1_ffn_up_w': _L1_ffn_in['up_w'], 'L1_ffn_down_w': _L1_ffn_in['down_w'], 'L1_ffn_sh_gate_w': _L1_ffn_in['sh_gate_w'], 'L1_ffn_sh_up_w': _L1_ffn_in['sh_up_w'], 'L1_ffn_sh_down_w': _L1_ffn_in['sh_down_w']}
    _x0 = _d['L0_attn_hidden_states']
    _d['L0_attn_hidden_states'] = jax.random.normal(jax.random.fold_in(jax.random.key(seed), 1), (4, 512, 256), dtype=_x0.dtype)
    del _x0
    return _d

def reference(L0_attn_hidden_states, L0_attn_norm_w, L0_attn_in_proj_w, L0_attn_in_proj_b, L0_attn_conv_w, L0_attn_conv_b, L0_attn_x_proj_w, L0_attn_x_proj_b, L0_attn_A_log, L0_attn_log2_alpha_base, L0_attn_log2_beta, L0_attn_surprise_ema, L0_attn_out_proj_w, L0_attn_out_proj_b, L0_attn_res_gate, L0_ffn_gate_w, L0_ffn_base_gate_up, L0_ffn_base_down, L0_ffn_expert_gate_up, L0_ffn_expert_down, L1_attn_W_qkv, L1_attn_W_o, L1_ffn_router_w, L1_ffn_router_bias, L1_ffn_gate_w, L1_ffn_up_w, L1_ffn_down_w, L1_ffn_sh_gate_w, L1_ffn_sh_up_w, L1_ffn_sh_down_w):

    def _L0_attn_ref(hidden_states, norm_w, in_proj_w, in_proj_b, conv_w, conv_b, x_proj_w, x_proj_b, A_log, log2_alpha_base, log2_beta, surprise_ema, out_proj_w, out_proj_b, res_gate):
        import jax, jax.numpy as jnp
        import numpy as np
        Bsz, L, D = hidden_states.shape
        H = A_log.shape[0]
        S = (x_proj_b.shape[0] // H - 1) // 2
        Di = in_proj_w.shape[0] // 2
        Dh = Di // H
        eps = jnp.finfo(jnp.float32).eps
        x = hidden_states * jax.lax.rsqrt(jnp.mean(hidden_states ** 2, -1, keepdims=True) + eps) * norm_w
        xz = x @ in_proj_w.T + in_proj_b
        x, z = (xz[..., :Di], xz[..., Di:])
        xc = jax.lax.conv_general_dilated(x.transpose(0, 2, 1), conv_w, (1,), [(3, 0)], dimension_numbers=('NCH', 'OIH', 'NCH'), feature_group_count=Di)
        x = jax.nn.silu((xc + conv_b[None, :, None]).transpose(0, 2, 1))
        xp = (x @ x_proj_w.T + x_proj_b).reshape(Bsz, L, H, 1 + 2 * S)
        dt = xp[..., 0]
        Bs = xp[..., 1:1 + S]
        Cs = xp[..., 1 + S:]
        Bs = Bs / jnp.maximum(jnp.linalg.norm(Bs, axis=-1, keepdims=True), 1e-12)
        Cs = Cs / jnp.maximum(jnp.linalg.norm(Cs, axis=-1, keepdims=True), 1e-12)
        A = jnp.clip(A_log, -2.3, -0.01)[None, None, :] * jax.nn.softplus(dt)
        A_decay = jnp.exp(A)
        X = x.reshape(Bsz, L, H, Dh)
        alpha_base = 1.0 - 2.0 ** jnp.clip(log2_alpha_base, -3.32, -0.015)
        beta = 2.0 ** jnp.clip(log2_beta, -2.0, 2.0)

        def step(carry, xs):
            h, h_red = carry
            x_t, a_t, B_t, C_t = xs
            u_red = B_t * x_t.mean(-1)[..., None]
            diff = (1.0 - a_t)[..., None] * u_red
            pe = jnp.mean(diff ** 2, -1)
            ns = pe / (surprise_ema[None, :] + 1e-06)
            boost = jax.nn.relu(jnp.tanh(beta[None, :] * ns))
            alpha = jnp.clip(alpha_base[None, :] + (1.0 - alpha_base[None, :]) * boost, 0.01, 0.999)
            u_t = B_t[..., None] * x_t[:, :, None, :]
            h = alpha[..., None, None] * h + (1.0 - alpha)[..., None, None] * u_t
            h_red = h.mean(-1)
            y = jnp.einsum('bhs,bhsd->bhd', C_t, h)
            return ((h, h_red), y)
        h0 = jnp.zeros((Bsz, H, S, Dh), jnp.float32)
        hr0 = jnp.zeros((Bsz, H, S), jnp.float32)
        xs = (X.transpose(1, 0, 2, 3), A_decay.transpose(1, 0, 2), Bs.transpose(1, 0, 2, 3), Cs.transpose(1, 0, 2, 3))
        _, Yt = jax.lax.scan(step, (h0, hr0), xs)
        Y = Yt.transpose(1, 0, 2, 3).reshape(Bsz, L, Di)
        Y = Y * jax.nn.silu(z)
        out = Y @ out_proj_w.T + out_proj_b
        return hidden_states + res_gate * out

    def _L0_ffn_ref(x, gate_w, base_gate_up, base_down, expert_gate_up, expert_down):
        import jax, jax.numpy as jnp
        import numpy as np
        H, I, E, K = (256, 512, 8, 2)
        B, S = (1, 256)

        def _silu_mul(gu):
            d = gu.shape[-1] // 2
            return jax.nn.silu(gu[..., :d]) * gu[..., d:]
        base_y = _silu_mul(x @ base_gate_up) @ base_down
        b, s, h = x.shape
        xf = x.reshape(-1, h)
        n = xf.shape[0]
        n_exp = gate_w.shape[1]
        probs = jax.nn.softmax((xf @ gate_w).astype(jnp.float32), axis=-1)
        w, idx = jax.lax.top_k(probs, K)
        w = (w / w.sum(axis=-1, keepdims=True)).astype(x.dtype)
        comb = jnp.zeros((n, n_exp), x.dtype).at[jnp.arange(n)[:, None], idx].add(w)
        out = jnp.zeros_like(xf)
        for e in range(n_exp):
            y = _silu_mul(xf @ expert_gate_up[e]) @ expert_down[e]
            out = out + comb[:, e:e + 1] * y
        return out.reshape(b, s, h) + base_y

    def _L1_attn_ref(x, W_qkv, W_o):
        import jax, jax.numpy as jnp
        import numpy as np
        import math
        N_EMBD = 256
        N_HEADS = 16
        HEAD_DIM = N_EMBD // N_HEADS
        CTX = 256

        def alibi_bias(seq_len: int, n_heads: int) -> jnp.ndarray:
            i = jnp.arange(seq_len)[:, None]
            j = jnp.arange(seq_len)[None, :]
            pos = jnp.where(j <= i, (j - i).astype(jnp.float32), 0.0)
            slopes = 2.0 ** (-8.0 / jnp.arange(1, n_heads + 1, dtype=jnp.float32))
            return slopes[:, None, None] * pos[None, :, :]

        def causal_mask(seq_len: int) -> jnp.ndarray:
            i = jnp.arange(seq_len)[:, None]
            j = jnp.arange(seq_len)[None, :]
            return jnp.where(j > i, -jnp.inf, 0.0).astype(jnp.float32)
        bsz, seq_len, n_embd = x.shape
        qkv = jnp.einsum('bsd,de->bse', x, W_qkv)
        q, k, v = jnp.split(qkv, 3, axis=-1)

        def to_heads(t):
            return t.reshape(bsz, seq_len, N_HEADS, HEAD_DIM).transpose(0, 2, 1, 3)
        q, k, v = (to_heads(q), to_heads(k), to_heads(v))
        attn = jnp.einsum('bhqd,bhkd->bhqk', q, k) / math.sqrt(HEAD_DIM)
        attn = attn + alibi_bias(seq_len, N_HEADS)[None] + causal_mask(seq_len)[None, None]
        attn = jax.nn.softmax(attn, axis=-1)
        y = jnp.einsum('bhqk,bhkd->bhqd', attn, v)
        y = y.transpose(0, 2, 1, 3).reshape(bsz, seq_len, n_embd)
        return jnp.einsum('bsd,de->bse', y, W_o)

    def _L1_ffn_ref(x, router_w, router_bias, gate_w, up_w, down_w, sh_gate_w, sh_up_w, sh_down_w):
        import jax, jax.numpy as jnp
        import numpy as np
        B, T, D = (1, 256, 256)
        E, K, F = (64, 4, 64)
        S, SF = (2, 64 * 4)
        CAP = 32

        def _moe_forward(x, router_w, router_bias, gate_w, up_w, down_w, sh_gate_w, sh_up_w, sh_down_w):
            b, t, d = x.shape
            flat = x.reshape(b * t, d)
            N = flat.shape[0]
            logits = flat @ router_w.T
            scores = jax.nn.softmax(logits, axis=-1)
            _, topk_idx = jax.lax.top_k(logits + router_bias, K)
            topk_w = jnp.take_along_axis(scores, topk_idx, axis=-1)
            topk_w = topk_w / topk_w.sum(axis=-1, keepdims=True)
            P = N * K
            e_flat = topk_idx.reshape(-1)
            t_flat = jnp.repeat(jnp.arange(N), K)
            w_flat = topk_w.reshape(-1)
            order = jnp.argsort(e_flat)
            e_s, t_s, w_s = (e_flat[order], t_flat[order], w_flat[order])
            counts = jnp.bincount(e_s, length=E)
            starts = jnp.concatenate([jnp.zeros((1,), counts.dtype), jnp.cumsum(counts)[:-1]])
            pos = jnp.arange(P) - starts[e_s]
            slot = jnp.where(pos < CAP, pos, CAP)
            tok_table = jnp.zeros((E, CAP + 1), jnp.int32).at[e_s, slot].set(t_s)[:, :CAP]
            w_table = jnp.zeros((E, CAP + 1), w_s.dtype).at[e_s, slot].set(w_s)[:, :CAP]
            xg = flat[tok_table]
            g = jnp.einsum('ecd,efd->ecf', xg, gate_w)
            u = jnp.einsum('ecd,efd->ecf', xg, up_w)
            y = jnp.einsum('ecf,edf->ecd', jax.nn.silu(g) * u, down_w)
            out = jnp.zeros_like(flat).at[tok_table.reshape(-1)].add((y * w_table[..., None]).reshape(-1, d))
            sg = jnp.einsum('nd,sfd->nsf', flat, sh_gate_w)
            su = jnp.einsum('nd,sfd->nsf', flat, sh_up_w)
            out = out + jnp.einsum('nsf,sdf->nd', jax.nn.silu(sg) * su, sh_down_w)
            return out.reshape(b, t, d)
        return _moe_forward(x, router_w, router_bias, gate_w, up_w, down_w, sh_gate_w, sh_up_w, sh_down_w)
    x = L0_attn_hidden_states
    x = x + _L0_attn_ref(_layernorm(x, axis=-1), L0_attn_norm_w, L0_attn_in_proj_w, L0_attn_in_proj_b, L0_attn_conv_w, L0_attn_conv_b, L0_attn_x_proj_w, L0_attn_x_proj_b, L0_attn_A_log, L0_attn_log2_alpha_base, L0_attn_log2_beta, L0_attn_surprise_ema, L0_attn_out_proj_w, L0_attn_out_proj_b, L0_attn_res_gate)
    x = x + _L0_ffn_ref(_layernorm(x, axis=-1), L0_ffn_gate_w, L0_ffn_base_gate_up, L0_ffn_base_down, L0_ffn_expert_gate_up, L0_ffn_expert_down)
    x = x + _L1_attn_ref(_layernorm(x, axis=-1), L1_attn_W_qkv, L1_attn_W_o)
    x = x + _L1_ffn_ref(_layernorm(x, axis=-1), L1_ffn_router_w, L1_ffn_router_bias, L1_ffn_gate_w, L1_ffn_up_w, L1_ffn_down_w, L1_ffn_sh_gate_w, L1_ffn_sh_up_w, L1_ffn_sh_down_w)
    return x

_drawn_inputs = setup_inputs


def setup_inputs(seed=0):
    import zlib

    import numpy as np

    out = dict(_drawn_inputs(seed))
    spreads = {'L0_attn_norm_w': (1.0, 0.6),
     'L0_attn_in_proj_b': (0.0, 0.8),
     'L0_attn_conv_b': (0.0, 0.8),
     'L0_attn_x_proj_b': (0.0, 0.8),
     'L0_attn_A_log': (-0.6931471824645996, 0.6),
     'L0_attn_log2_alpha_base': (-1.0, 0.6),
     'L0_attn_log2_beta': (0.0, 0.8),
     'L0_attn_surprise_ema': (1.0, 0.6),
     'L0_attn_out_proj_b': (0.0, 0.8),
     'L1_ffn_router_bias': (0.0, 0.8)}
    factors = {'L0_attn_in_proj_w': 8.0,
     'L0_attn_conv_w': 8.0,
     'L0_attn_x_proj_w': 8.0,
     'L0_attn_out_proj_w': 8.0,
     'L0_ffn_gate_w': 7.515,
     'L0_ffn_base_gate_up': 4.6,
     'L0_ffn_base_down': 4.597,
     'L0_ffn_expert_gate_up': 6.463,
     'L0_ffn_expert_down': 6.467,
     'L1_ffn_router_w': 8.0,
     'L1_ffn_gate_w': 8.0,
     'L1_ffn_up_w': 8.0,
     'L1_ffn_down_w': 8.0,
     'L1_ffn_sh_gate_w': 4.934,
     'L1_ffn_sh_up_w': 4.879,
     'L1_ffn_sh_down_w': 4.89}
    for name, (base, spread) in spreads.items():
        noise = np.random.default_rng([zlib.crc32(name.encode()), seed]).standard_normal(out[name].shape)
        drawn = base * np.exp(spread * noise) if base else spread * noise
        out[name] = jnp.asarray(drawn.astype(out[name].dtype))
    for name, factor in factors.items():
        out[name] = (out[name] * factor).astype(out[name].dtype)
    return out
```

```python
from contextlib import ExitStack

import numpy as np

import concourse.bass as bass
from concourse import mybir

ACT = mybir.ActivationFunctionType
ALU = mybir.AluOpType
F32 = mybir.dt.float32
I32 = mybir.dt.int32
AX_X = mybir.AxisListType.X

P = 128
D = 256
KD = D // P
BATCH, SEQ = 4, 512
TOK = BATCH * SEQ
NT = TOK // P
CH = SEQ // P
LN_EPS = 1e-5
RMS_EPS = float(np.finfo(np.float32).eps)

NH0, DH, NS = 24, 64, 64
DI = NH0 * DH
KI = DI // P
PAIRS = KI
HC = 2 * CH
LN2 = float(np.log(2.0))


class Chain:

    def __init__(self, eng, sem):
        self.eng, self.sem, self.n = eng, sem, 0

    def __call__(self, ins):
        self.n += 1
        ins.then_inc(self.sem, 1)
        self.eng.wait_ge(self.sem, self.n)

    def restart(self):
        self.eng.sem_clear(self.sem)
        self.n = 0


def rsqrt(ve, link, out, v, tmp):
    link(ve.tensor_scalar(tmp.bitcast(I32), v.bitcast(I32), 1, None, ALU.logical_shift_right))
    link(ve.tensor_scalar(out.bitcast(I32), tmp.bitcast(I32), -1.0, float(0x5F3759DF), ALU.mult, ALU.add))
    for _ in range(3):
        link(ve.tensor_tensor(tmp, out, out, ALU.mult))
        link(ve.scalar_tensor_tensor(tmp, tmp, -0.5, v, ALU.mult, ALU.mult))
        link(ve.scalar_tensor_tensor(out, tmp, 1.5, out, ALU.add, ALU.mult))


def scope(nc, tag):
    ctx = ExitStack()

    def sb(name, shape, dt=F32):
        return ctx.enter_context(nc.sbuf_tensor(f"{tag}_{name}", shape, dt))

    def ps(name, shape, dt=F32):
        return ctx.enter_context(nc.psum_tensor(f"{tag}_{name}", shape, dt))

    def sem(name):
        USED.append(ctx.enter_context(nc.semaphore(f"{tag}_{name}")))
        return USED[-1]

    return ctx, sb, ps, sem


USED = []


def clear_semaphores(nc):
    with nc.Block() as block:
        @block.gpsimd
        def _(pool):
            for s in USED:
                pool.sem_clear(s)
    USED.clear()


def constants(nc, ident, upto, after, ones, pair_rows):
    ctx, sb, ps, sem = scope(nc, "const")
    with ctx:
        filled = sem("filled")
        made = sem("made")
        block = ctx.enter_context(nc.Block())

        @block.gpsimd
        def _(pool):
            pool.memset(ident[:, :], 0.0).then_inc(filled, 1)
            for m in (upto, after, ones, pair_rows):
                pool.memset(m[:, :], 1.0).then_inc(filled, 1)
            pool.wait_ge(filled, 5)
            sel = pool.affine_select
            sel(out=ident[:, :], in_=ident[:, :], compare_op=ALU.not_equal, fill=1.0, base=0,
                pattern=[[-1, P]], channel_multiplier=1).then_inc(made, 1)
            sel(out=upto[:, :], in_=upto[:, :], compare_op=ALU.is_ge, fill=0.0, base=0,
                pattern=[[1, P]], channel_multiplier=-1).then_inc(made, 1)
            sel(out=after[:, :], in_=after[:, :], compare_op=ALU.is_gt, fill=0.0, base=0,
                pattern=[[-1, P]], channel_multiplier=1).then_inc(made, 1)
            sel(out=pair_rows[:, :], in_=pair_rows[:, :], compare_op=ALU.is_ge, fill=0.0, base=0,
                pattern=[[-DH, 2]], channel_multiplier=1).then_inc(made, 1)
            pool.wait_ge(made, 4)
            sel(out=pair_rows[:, :], in_=pair_rows[:, :], compare_op=ALU.is_ge, fill=0.0, base=DH - 1,
                pattern=[[DH, 2]], channel_multiplier=-1).then_inc(made, 1)
            pool.wait_ge(made, 5)


def normalise(nc, tag, x, xT, ident, x_dram=None, rms=None, rows=None):
    ctx, sb, ps, sem = scope(nc, tag)
    with ctx:
        stats = sb("stats", [P, NT, 6])
        mv = sb("mv", [P, NT, 2])
        var = sb("var", [P, NT])
        rstd = sb("rstd", [P, NT])
        rrms = sb("rrms", [P, NT])
        tmp = sb("tmp", [P, NT])
        hrow = sb("hrow", [P, 2, D])
        xrow = sb("xrow", [P, 2, D])
        trans = [ps(f"trans{s}", [P, 512]) for s in range(2)]
        loaded = sem("loaded")
        order = sem("order")
        row_ready = sem("row_ready")
        turned = sem("turned")
        stored = sem("stored")
        block = ctx.enter_context(nc.Block())

        if x_dram is not None:
            @block.sync
            def _(sp):
                for g in range(4):
                    sp.dma_start(x[:, 4 * g:4 * g + 4, :],
                                 x_dram[512 * g:512 * g + 512, :].rearrange("(t p) d -> p t d", p=P)
                                 ).then_inc(loaded, 16)

        @block.vector
        def _(ve):
            link = Chain(ve, order)
            if x_dram is not None:
                ve.wait_ge(loaded, 64)
            with ve.Fori(0, NT) as t:
                ve.bn_stats(stats[:, bass.ds(t, 1), :], x[:, bass.ds(t, 1), :].rearrange("p o d -> p (o d)"))
            link(ve.memset(tmp[:, :], 0.0))
            ve.drain().then_inc(order, 1)
            link.n += 1
            ve.wait_ge(order, link.n)
            for t in range(NT):
                ve.bn_aggr(mv[:, t, :], stats[:, t, :])
            ve.drain().then_inc(order, 1)
            link.n += 1
            ve.wait_ge(order, link.n)
            link(ve.tensor_scalar(var[:, :], mv[:, :, 1], LN_EPS, None, ALU.add))
            rsqrt(ve, link, rstd[:, :], var[:, :], tmp[:, :])
            if rms:
                norm_w, gated_bias = rms
                link(ve.tensor_tensor(var[:, :], mv[:, :, 1], rstd[:, :], ALU.mult))
                link(ve.tensor_tensor(var[:, :], var[:, :], rstd[:, :], ALU.mult))
                link(ve.tensor_scalar(var[:, :], var[:, :], RMS_EPS, None, ALU.add))
                rsqrt(ve, link, rrms[:, :], var[:, :], tmp[:, :])
            with ve.Fori(0, NT // 2) as i:
                link.restart()
                for s in range(2):
                    t = bass.ds(2 * i + s, 1)
                    h = hrow[:, s:s + 1, :]
                    ve.wait_ge(turned, 2 * i + s)
                    if rms:
                        link(ve.tensor_scalar(h, x[:, t, :], mv[:, t, 0:1].rearrange("p o c -> p (o c)"),
                                              rstd[:, t], ALU.subtract, ALU.mult))
                        ve.tensor_scalar(xrow[:, s:s + 1, :], h, rrms[:, t], None, ALU.mult).then_inc(row_ready, 1)
                        link(ve.tensor_tensor(h, h, gated_bias.unsqueeze(1), ALU.add))
                        link(ve.tensor_tensor(x[:, t, :], x[:, t, :], h, ALU.add))
                    else:
                        out = rows[:, t, :] if rows is not None else xrow[:, s:s + 1, :]
                        ve.tensor_scalar(xrow[:, s:s + 1, :], x[:, t, :], mv[:, t, 0:1].rearrange("p o c -> p (o c)"),
                                         rstd[:, t], ALU.subtract, ALU.mult).then_inc(row_ready, 1)
                        if rows is not None:
                            ve.tensor_scalar(rows[:, t, :], x[:, t, :],
                                             mv[:, t, 0:1].rearrange("p o c -> p (o c)"),
                                             rstd[:, t], ALU.subtract, ALU.mult)

        @block.tensor
        def _(pe):
            with pe.Fori(0, NT // 2) as i:
                for s in range(2):
                    pe.wait_ge(row_ready, 2 * i + s + 1)
                    pe.wait_ge(stored, 2 * i + s)
                    for k in range(KD):
                        mm = pe.transpose(trans[s][:, k * P:(k + 1) * P], xrow[:, s, k * P:(k + 1) * P], ident[:, :])
                    mm.then_inc(turned, 1)

        @block.scalar
        def _(act):
            act.preload_act_table_set("natural_log_exp_and_others")
            with act.Fori(0, NT // 2) as i:
                for s in range(2):
                    act.wait_ge(turned, 2 * i + s + 1)
                    for k in range(KD):
                        last = act.activation(xT[:, k, bass.ds((2 * i + s) * P, P)], trans[s][:, k * P:(k + 1) * P],
                                              ACT.Copy, scale=rms[0][:, k:k + 1] if rms else 1.0)
                    last.then_inc(stored, 1)


def mixer(nc, x, xT, ident, upto, after, ones, pair_rows, A):
    ctx, sb, ps, sem = scope(nc, "mix")
    with ctx:
        in_b = sb("in_b", [P, 2 * KI])
        conv_w = sb("conv_w", [P, KI, 4])
        conv_b = sb("conv_b", [P, KI])
        bc_b = sb("bc_b", [P, PAIRS, 2])
        dt_w = sb("dt_w", [P, KI, 2 * NH0])
        out_w = sb("out_w", [P, KI, D])
        par = sb("par", [P, 5 * NH0 + 1])
        kpar = sb("kpar", [P, 4, NH0])
        ab = sb("ab", [P, NH0, CH])
        omab = sb("omab", [P, NH0, CH])
        xc = sb("xc", [P, KI, SEQ])
        zy = sb("zy", [P, KI, SEQ])
        w_in = [sb(f"w_in{s}", [P, 4, P]) for s in range(2)]
        xin = [sb(f"xin{s}", [P, SEQ + 4]) for s in range(2)]
        acc = [sb(f"acc{s}", [P, SEQ]) for s in range(2)]
        gd = sb("gd", [P, NH0, CH])
        ge = sb("ge", [P, NH0, CH])
        gx = sb("gx", [P, NH0, CH])
        gain = sb("gain", [P, NH0, CH])
        w_b = [sb(f"w_b{s}", [P, KI, P]) for s in range(2)]
        w_c = [sb(f"w_c{s}", [P, KI, P]) for s in range(2)]
        bT = [sb(f"bT{s}", [P, SEQ]) for s in range(2)]
        cT = [sb(f"cT{s}", [P, SEQ]) for s in range(2)]
        sq_b = sb("sq_b", [P, SEQ])
        sq_c = sb("sq_c", [P, SEQ])
        nrm = sb("nrm", [P, 2, HC])
        rn = sb("rn", [P, 2, HC])
        nt = sb("nt", [P, 2, HC])
        u = sb("u", [P, HC])
        e2 = sb("e2", [P, HC])
        alpha = sb("alpha", [P, HC])
        lna = sb("lna", [P, HC])
        wj = sb("wj", [P, HC])
        lna_w = sb("lna_w", [P, CH - 1, P])
        rc_w = sb("rc_w", [P, CH, P])
        lsel = sb("lsel", [P, HC, P])
        dec = sb("dec", [P, HC, P])
        ecum = sb("ecum", [P, 2 * HC + 3 * P])
        xst = sb("xst", [P, SEQ])
        xw = sb("xw", [P, CH, P])
        bf = sb("bf", [P, CH - 1, P])
        cs = sb("cs", [P, CH - 1, P])
        prob = sb("prob", [P, HC, P])
        state = sb("state", [P, CH - 1, P])
        zc = sb("zc", [P, SEQ])

        bank = [ps(f"bank{i}", [P, 512]) for i in range(2)]
        seg = ps("seg", [P, HC, P])
        bank4, bank5, bank6, bank7 = (ps(f"bank{i}", [P, 512]) for i in range(4, 8))

        names = ("params", "kready", "order", "orderp", "ordera", "w_in_ld0", "w_in_ld1", "inproj", "xin_ready",
                 "conv_done", "xc_ready", "gate_mm", "gate_d", "gate_e", "gate_l", "gate_a", "gate_ready", "a_order",
                 "w_b_ld0", "w_b_ld1", "w_c_ld0", "w_c_ld1",
                 "b_proj", "c_proj", "b_out", "c_out", "ssq_mm", "tanh_in", "tanh_out", "alpha_ready",
                 "lna_ready", "lsel_ready", "cum_mm", "cum_out", "seg_mm", "seg_out", "dec_ready", "xst_ready",
                 "xt_mm", "xw_ready", "bt_mm", "bf_ready", "s_mm", "prob_ready", "ds_mm", "state_ready",
                 "cs_ready", "cbc_mm", "zc_ready", "y_mm", "y_out", "o_mm", "o_out", "lna_w_ready", "rc_w_ready", "zpad", "loopa")
        S = {n: sem(n) for n in names}
        block = ctx.enter_context(nc.Block())

        @block.sync
        def _(sp):
            for dst, src in ((in_b, "in_b"), (conv_w, "conv_w"), (conv_b, "conv_b"), (bc_b, "bc_b"), (dt_w, "dt_w"),
                             (out_w, "out_w")):
                sp.dma_start(dst.ap() if hasattr(dst, "ap") and callable(dst.ap) else dst[:], A[src]).then_inc(S["params"], 16)
            sp.dma_start(par[:, :], A["par"].to_broadcast([P, 5 * NH0 + 1])).then_inc(S["params"], 16)

            def load_pair(n, i, s):
                sp.wait_ge(S["b_proj"], 2 * n + s - 1 if s else 2 * n)
                sp.dma_start(w_b[s][:, :, :], A["bc_w"][bass.ds(4 * i + 2 * s, 1)].rearrange("o p k m -> p (o k) m")
                             ).then_inc(S[f"w_b_ld{s}"], 16)
                sp.wait_ge(S["c_proj"], 2 * n + s - 1 if s else 2 * n)
                sp.dma_start(w_c[s][:, :, :], A["bc_w"][bass.ds(4 * i + 2 * s + 1, 1)].rearrange("o p k m -> p (o k) m")
                             ).then_inc(S[f"w_c_ld{s}"], 16)

            with sp.Fori(0, BATCH) as b:
                with sp.Fori(0, KI // 2) as i:
                    for s in range(2):
                        n = b * (KI // 2) + i
                        sp.wait_ge(S["inproj"], 2 * n + s - 1 if s else 2 * n)
                        sp.dma_start(w_in[s][:, :, :], A["in_w"][bass.ds(2 * i + s, 1)].rearrange("o p k m -> p (o k) m")
                                     ).then_inc(S[f"w_in_ld{s}"], 16)
                with sp.Fori(0, PAIRS // 2) as i:
                    for s in range(2):
                        load_pair(b * (PAIRS // 2) + i, i, s)

        @block.tensor
        def _(pe):
            def project(n, s, w, ld, out, done, freed, ks):
                if 0 in ks:
                    pe.wait_ge(S[ld], 16 * n + 16)
                    pe.wait_ge(S[freed], 2 * n + s)
                for k in ks:
                    mm = pe.matmul(out[:, :], w[s][:, k, :], xc[:, k, :], start=(k == 0), stop=(k == KI - 1))
                if KI - 1 in ks:
                    mm.then_inc(S[done], 1)

            def project_b(n, s):
                project(n, s, w_b, f"w_b_ld{s}", bank[0], "b_proj", "b_out", range(KI))

            def project_c(n, s, ks):
                project(n, s, w_c, f"w_c_ld{s}", bank[1], "c_proj", "c_out", ks)

            def scan(n, s, nxt):
                g = 2 * n + s
                pe.wait_ge(S["xst_ready"], g + 1)
                pe.wait_ge(S["zc_ready"], g)
                for c in range(CH):
                    mm = pe.transpose(bank4[:, c * P:(c + 1) * P], xst[:, c * P:(c + 1) * P], ident[:, :])
                mm.then_inc(S["xt_mm"], 1)
                pe.wait_ge(S["c_out"], g + 1)
                pe.wait_ge(S["b_out"], g + 1)
                pe.wait_ge(S["state_ready"], g)
                for c in range(CH - 1):
                    mm = pe.transpose(bank5[:, c * P:(c + 1) * P], bT[s][:, c * P:(c + 1) * P], ident[:, :])
                mm.then_inc(S["bt_mm"], 1)
                pe.wait_ge(S["cum_out"], g)
                for w, sq in enumerate((sq_b, sq_c)):
                    for c in range(CH):
                        mm = pe.matmul(bank6[:, w * HC + c:w * HC + c + CH + 1:CH], sq[:, c * P:(c + 1) * P],
                                       pair_rows[:, :], start=True, stop=True)
                mm.then_inc(S["ssq_mm"], 1)
                if nxt:
                    project_b(*nxt)
                pe.wait_ge(S["lna_w_ready"], g + 1)
                pe.matmul(bank6[:, 0:HC], after[:, :], lna[:, :], start=True, stop=True)
                pe.matmul(bank6[:, HC:2 * HC], ones[:, :], lna[:, :], start=True, stop=True)
                for c in range(1, CH):
                    mm = pe.matmul(bank6[:, 2 * HC + (c - 1) * P:2 * HC + c * P], lna_w[:, c - 1, :], upto[:, :],
                                   start=True, stop=True)
                mm.then_inc(S["cum_mm"], 1)
                pe.wait_ge(S["lsel_ready"], g + 1)
                pe.wait_ge(S["prob_ready"], g)
                for m in range(HC):
                    mm = pe.matmul(seg[:, m, :], lsel[:, m, :], upto[:, :], start=True, stop=True)
                mm.then_inc(S["seg_mm"], 1)
                if nxt:
                    project_c(*nxt, range(KI // 2))
                pe.wait_ge(S["seg_out"], g + 1)
                for h in range(2):
                    for c in range(CH):
                        r = slice(h * DH, (h + 1) * DH)
                        mm = pe.matmul(seg[:, h * CH + c, :], bT[s][r, c * P:(c + 1) * P],
                                       cT[s][r, c * P:(c + 1) * P], start=True, stop=True)
                mm.then_inc(S["s_mm"], 1)
                pe.wait_ge(S["bf_ready"], g + 1)
                pe.wait_ge(S["xw_ready"], g + 1)
                for c in range(CH - 1):
                    mm = pe.matmul(bank5[:, c * P:(c + 1) * P], bf[:, c, :], xw[:, c, :], start=True, stop=True)
                mm.then_inc(S["ds_mm"], 1)
                pe.wait_ge(S["rc_w_ready"], g + 1)
                for c in range(CH):
                    mm = pe.matmul(bank4[:, c * P:(c + 1) * P], rc_w[:, c, :], ident[:, :], start=True, stop=True)
                mm.then_inc(S["cbc_mm"], 1)
                if nxt:
                    project_c(*nxt, range(KI // 2, KI))
                pe.wait_ge(S["y_out"], g)
                pe.wait_ge(S["prob_ready"], g + 1)
                pe.wait_ge(S["state_ready"], g + 1)
                pe.wait_ge(S["cs_ready"], g + 1)
                for c in range(CH):
                    col = slice(c * P, (c + 1) * P)
                    if c:
                        pe.matmul(bank7[:, col], state[:, c - 1, :], cs[:, c - 1, :], start=True, stop=True,
                                  skip_group_check=True)
                    for h in range(2):
                        mm = pe.matmul(bank7[h * DH:(h + 1) * DH, col], xw[:, c, h * DH:(h + 1) * DH],
                                       prob[:, h * CH + c, :], start=(c == 0), stop=True, skip_group_check=True)
                mm.then_inc(S["y_mm"], 1)

            pe.wait_ge(S["params"], 16 * 7)
            with pe.Fori(0, BATCH) as b:
                with pe.Fori(0, KI // 2) as i:
                    for s in range(2):
                        n = b * (KI // 2) + i
                        pe.wait_ge(S[f"w_in_ld{s}"], 16 * n + 16)
                        pe.wait_ge(S["xin_ready"], 2 * n + s - 1 if s else 2 * n)
                        for half in range(2):
                            out = (bank4, bank5, bank6, bank7)[2 * s + half]
                            for k in range(KD):
                                mm = pe.matmul(out[:, :], w_in[s][:, 2 * half + k, :],
                                               xT[:, k, bass.ds(b * SEQ, SEQ)], start=(k == 0), stop=(k == KD - 1))
                        mm.then_inc(S["inproj"], 1)
                pe.wait_ge(S["xc_ready"], (b + 1) * KI)
                for c in range(CH):
                    for k in range(KI):
                        mm = pe.matmul(seg[:, 0, :].unsqueeze(1)[:, 0, 0:1] if False else bank[0][:, c * 2 * NH0:(c + 1) * 2 * NH0],
                                       xc[:, k, c * P:(c + 1) * P], dt_w[:, k, :], start=(k == 0), stop=(k == KI - 1))
                mm.then_inc(S["gate_mm"], 1)
                n0 = b * (PAIRS // 2)
                pe.wait_ge(S["gate_d"], b + 1)
                project_b(n0, 0)
                project_c(n0, 0, range(KI))
                with pe.Fori(0, PAIRS // 2 - 1) as i:
                    scan(n0 + i, 0, (n0 + i, 1))
                    scan(n0 + i, 1, (n0 + i + 1, 0))
                n1 = n0 + PAIRS // 2 - 1
                scan(n1, 0, (n1, 1))
                scan(n1, 1, None)
                pe.wait_ge(S["y_out"], (b + 1) * PAIRS)
                for c in range(CH):
                    out = seg[:, 4 * (c // 2):4 * (c // 2) + 4, :].rearrange("p m t -> p (m t)")[:, (c % 2) * D:(c % 2 + 1) * D]
                    for k in range(KI):
                        mm = pe.matmul(out, zy[:, k, c * P:(c + 1) * P], out_w[:, k, :],
                                       start=(k == 0), stop=(k == KI - 1))
                mm.then_inc(S["o_mm"], 1)

        @block.scalar
        def _(act):
            def evacuate(n, i, s, w):
                g = 2 * n + s
                src, dst, sq = ((bank[0], bT, sq_b), (bank[1], cT, sq_c))[w]
                act.wait_ge(S[("b_proj", "c_proj")[w]], g + 1)
                bias = bc_b[:, bass.ds(2 * i + s, 1), w]
                act.activation(dst[s][:, :], src[:, :], ACT.Identity, bias=bias)
                act.activation(sq[:, :], src[:, :], ACT.Square, bias=bias).then_inc(S[("b_out", "c_out")[w]], 1)

            def scan(n, i, s, nxt):
                g = 2 * n + s
                act.wait_ge(S["tanh_in"], g + 1)
                act.activation(e2[:, :], u[:, :], ACT.Exp).then_inc(S["tanh_out"], 1)
                act.wait_ge(S["alpha_ready"], g + 1)
                act.activation(lna[:, :], alpha[:, :], ACT.Ln).then_inc(S["lna_ready"], 1)
                if nxt:
                    evacuate(*nxt, 0)
                act.wait_ge(S["cum_mm"], g + 1)
                act.activation(ecum[:, :], bank6[:, 0:2 * HC + 3 * P], ACT.Exp).then_inc(S["cum_out"], 1)
                act.wait_ge(S["seg_mm"], g + 1)
                act.activation(dec[:, :, :], seg[:, :, :], ACT.Exp).then_inc(S["seg_out"], 1)
                if nxt:
                    evacuate(*nxt, 1)

            act.wait_ge(S["params"], 16 * 7)
            act.preload_act_table_set("natural_log_exp_and_others")
            act.wait_ge(S["kready"], 1)
            act.activation(kpar[:, 1:3, :], kpar[:, 1:3, :], ACT.Exp, scale=LN2).then_inc(S["a_order"], 1)
            with act.Fori(0, BATCH) as b:
                act.preload_act_table_set("silu_and_others")
                act.wait_ge(S["o_mm"], b)
                with act.Fori(0, KI // 2) as i:
                    for s in range(2):
                        n = b * (KI // 2) + i
                        f = 2 * i + s
                        act.wait_ge(S["inproj"], 2 * n + s + 1)
                        act.wait_ge(S["conv_done"], 2 * n + s - 1 if s else 2 * n)
                        act.activation(xin[s][:, 3:3 + SEQ], (bank4, bank6)[s][:, :], ACT.Identity,
                                       bias=in_b[:, bass.ds(f, 1)])
                        act.activation(zy[:, bass.ds(f, 1), :], (bank5, bank7)[s][:, :].unsqueeze(1), ACT.Silu,
                                       bias=in_b[:, bass.ds(f + KI, 1)]).then_inc(S["xin_ready"], 1)
                        act.wait_ge(S["conv_done"], 2 * n + s + 1)
                        act.activation(xc[:, bass.ds(f, 1), :], acc[s][:, :].unsqueeze(1), ACT.Silu,
                                       bias=conv_b[:, bass.ds(f, 1)]).then_inc(S["xc_ready"], 1)
                act.preload_act_table_set("natural_log_exp_and_others")
                act.wait_ge(S["gate_e"], b + 1)
                act.activation(ge[:, :, :], ge[:, :, :], ACT.Exp, scale=-1.0).then_inc(S["a_order"], 1)
                act.wait_ge(S["a_order"], 2 * b + 2)
                act.activation(ge[:, :, :], ge[:, :, :], ACT.Ln, bias=1.0).then_inc(S["gate_l"], 1)
                act.wait_ge(S["gate_a"], b + 1)
                act.activation(gd[:, :, :], gd[:, :, :], ACT.Exp).then_inc(S["a_order"], 1)
                n0 = b * (PAIRS // 2)
                evacuate(n0, 0, 0, 0)
                evacuate(n0, 0, 0, 1)
                with act.Fori(0, PAIRS // 2 - 1) as i:
                    scan(n0 + i, i, 0, (n0 + i, i, 1))
                    scan(n0 + i, i, 1, (n0 + i + 1, i + 1, 0))
                i1 = PAIRS // 2 - 1
                scan(n0 + i1, i1, 0, (n0 + i1, i1, 1))
                scan(n0 + i1, i1, 1, None)

        @block.gpsimd
        def _(pool):
            def scan(b, n, i, s):
                g = 2 * n + s
                pool.wait_ge(S["xc_ready"], (b + 1) * KI)
                pool.wait_ge(S["xt_mm"], g)
                pool.tensor_copy(xst[:, :].unsqueeze(1), xc[:, bass.ds(2 * i + s, 1), :]).then_inc(S["xst_ready"], 1)
                pool.wait_ge(S["lna_ready"], g + 1)
                pool.tensor_tensor(lsel[:, :, :], after[:, :].unsqueeze(1).to_broadcast([P, HC, P]),
                                   lna[:, :].unsqueeze(2).to_broadcast([P, HC, P]), ALU.mult
                                   ).then_inc(S["lsel_ready"], 1)
                pool.tensor_copy(rc_w[:, :, :].rearrange("p c (h d) -> p c h d", h=2),
                                 rn[:, 1, :].rearrange("p (h c) -> p c h", h=2).unsqueeze(3).to_broadcast([P, CH, 2, DH])
                                 ).then_inc(S["rc_w_ready"], 1)
                pool.wait_ge(S["seg_out"], g + 1)
                pool.tensor_tensor(dec[:, :, :], dec[:, :, :], upto[:, :].unsqueeze(1).to_broadcast([P, HC, P]),
                                   ALU.mult).then_inc(S["dec_ready"], 1)

            with pool.Fori(0, BATCH) as b:
                with pool.Fori(0, PAIRS // 2) as i:
                    for s in range(2):
                        scan(b, b * (PAIRS // 2) + i, i, s)

        @block.vector
        def _(ve):
            link = Chain(ve, S["order"])

            def scan(n, i, s):
                g = 2 * n + s
                heads = bass.ds(4 * i + 2 * s, 2)
                link.restart()
                ve.wait_ge(S["ssq_mm"], g + 1)
                link(ve.tensor_scalar(nrm[:, :, :], bank6[:, 0:2 * HC].rearrange("p (w m) -> p w m", w=2), 1e-24, None, ALU.max))
                link(ve.tensor_copy(u[:, :], bank6[:, 0:HC]))
                rsqrt(ve, link, rn[:, :, :], nrm[:, :, :], nt[:, :, :])
                link(ve.tensor_tensor(u[:, :], u[:, :], rn[:, 0, :], ALU.mult))
                link(ve.tensor_tensor(u[:, :], u[:, :], rn[:, 0, :], ALU.mult))
                link(ve.tensor_tensor(u[:, :].rearrange("p (h c) -> p h c", h=2), u[:, :].rearrange("p (h c) -> p h c", h=2),
                                      gain[:, heads, :], ALU.mult))
                ve.tensor_scalar(u[:, :], u[:, :], 60.0, None, ALU.min).then_inc(S["tanh_in"], 1)
                ve.wait_ge(S["tanh_out"], g + 1)
                link(ve.tensor_scalar(e2[:, :], e2[:, :], 1.0, None, ALU.add))
                link(ve.reciprocal(e2[:, :], e2[:, :]))
                link(ve.tensor_scalar(e2[:, :], e2[:, :], -2.0, 1.0, ALU.mult, ALU.add))
                v = lambda t: t[:, :].rearrange("p (h c) -> p h c", h=2)
                link(ve.scalar_tensor_tensor(v(e2), v(e2), 0.0, omab[:, heads, :], ALU.max, ALU.mult))
                link(ve.tensor_tensor(v(e2), v(e2), ab[:, heads, :], ALU.add))
                ve.tensor_scalar(alpha[:, :], e2[:, :], 0.01, 0.999, ALU.max, ALU.min).then_inc(S["alpha_ready"], 1)
                ve.wait_ge(S["alpha_ready"], g + 1)
                link(ve.tensor_scalar(wj[:, :], alpha[:, :], -1.0, 1.0, ALU.mult, ALU.add))
                link(ve.tensor_tensor(wj[:, :], wj[:, :], rn[:, 0, :], ALU.mult))
                wide = lambda t, c: t.rearrange("p (h c) -> p c h", h=2)[:, c, :].unsqueeze(3).to_broadcast(
                    [P, c.stop - c.start, 2, DH])
                four = lambda t: t.rearrange("p c (h d) -> p c h d", h=2)
                ve.wait_ge(S["lna_ready"], g + 1)
                ve.tensor_copy(four(lna_w[:, :, :]), wide(lna[:, :], slice(1, CH))).then_inc(S["lna_w_ready"], 1)
                ve.wait_ge(S["xt_mm"], g + 1)
                ve.tensor_tensor(four(xw[:, :, :]), four(bank4[:, :].rearrange("p (c q) -> p c q", c=CH)),
                                 wide(wj[:, :], slice(0, CH)), ALU.mult).then_inc(S["xw_ready"], 1)
                ve.wait_ge(S["bt_mm"], g + 1)
                ve.wait_ge(S["cum_out"], g + 1)
                ve.tensor_tensor(four(bf[:, :, :]), four(bank5[:, 0:3 * P].rearrange("p (c q) -> p c q", c=CH - 1)),
                                 wide(ecum[:, 0:HC], slice(0, CH - 1)), ALU.mult).then_inc(S["bf_ready"], 1)
                ve.tensor_tensor(cs[:, :, :].rearrange("p c q -> p (c q)"), cT[s][:, P:], ecum[:, 2 * HC:],
                                 ALU.mult).then_inc(S["cs_ready"], 1)
                ve.wait_ge(S["dec_ready"], g + 1)
                ve.wait_ge(S["s_mm"], g + 1)
                ve.tensor_tensor(prob[:, :, :], seg[:, :, :], dec[:, :, :], ALU.mult).then_inc(S["prob_ready"], 1)
                ve.wait_ge(S["ds_mm"], g + 1)
                for c in range(CH - 1):
                    for h in range(2):
                        r = slice(h * DH, (h + 1) * DH)
                        new = bank5[r, c * P + h * DH:c * P + (h + 1) * DH]
                        if c == 0:
                            ins = ve.tensor_copy(state[r, 0, r], new)
                        else:
                            m = HC + h * CH + c
                            ins = ve.scalar_tensor_tensor(state[r, c, r], state[r, c - 1, r], ecum[r, m:m + 1],
                                                          new, ALU.mult, ALU.add)
                        if c == CH - 2 and h == 1:
                            ins.then_inc(S["state_ready"], 1)
                        elif c == CH - 2:
                            pass
                        else:
                            link(ins)
                ve.wait_ge(S["cbc_mm"], g + 1)
                ve.tensor_tensor(zc[:, :].unsqueeze(1), zy[:, bass.ds(2 * i + s, 1), :], bank4[:, :].unsqueeze(1),
                                 ALU.mult).then_inc(S["zc_ready"], 1)
                ve.wait_ge(S["zc_ready"], g + 1)
                ve.wait_ge(S["y_mm"], g + 1)
                ve.tensor_tensor(zy[:, bass.ds(2 * i + s, 1), :], bank7[:, :].unsqueeze(1), zc[:, :].unsqueeze(1),
                                 ALU.mult).then_inc(S["y_out"], 1)

            for s in range(2):
                link(ve.memset(xin[s][:, 0:3], 0.0))
            link(ve.memset(state[:, :, :], 0.0))
            ve.wait_ge(S["params"], 16 * 7)
            row = lambda r: par[:, r * NH0:(r + 1) * NH0]
            link(ve.tensor_scalar(kpar[:, 0, :], row(0), -2.3, -0.01, ALU.max, ALU.min))
            link(ve.tensor_scalar(kpar[:, 1, :], row(1), -3.32, -0.015, ALU.max, ALU.min))
            link(ve.tensor_scalar(kpar[:, 3, :], row(3), 1e-6, None, ALU.add))
            link(ve.reciprocal(kpar[:, 3, :], kpar[:, 3, :]))
            ve.tensor_scalar(kpar[:, 2, :], row(2), -2.0, 2.0, ALU.max, ALU.min).then_inc(S["kready"], 1)
            ve.wait_ge(S["a_order"], 1)
            link(ve.tensor_scalar(kpar[:, 1, :], kpar[:, 1, :], -1.0, 1.0, ALU.mult, ALU.add))
            link(ve.tensor_tensor(kpar[:, 2, :], kpar[:, 2, :], kpar[:, 3, :], ALU.mult))
            link(ve.tensor_scalar(kpar[:, 2, :], kpar[:, 2, :], 2.0 / NS, None, ALU.mult))
            for c in range(CH):
                link(ve.tensor_copy(ab[:, :, c], kpar[:, 1, :]))
                link(ve.tensor_scalar(omab[:, :, c], kpar[:, 1, :], -1.0, 1.0, ALU.mult, ALU.add))

            with ve.Fori(0, BATCH) as b:
                with ve.Fori(0, KI // 2) as i:
                    link.restart()
                    for s in range(2):
                        n = b * (KI // 2) + i
                        f = bass.ds(2 * i + s, 1)
                        ve.wait_ge(S["xin_ready"], 2 * n + s + 1)
                        ve.wait_ge(S["xc_ready"], 2 * n + s - 1 if s else 2 * n)
                        tap = lambda j: conv_w[:, f, j]
                        link(ve.tensor_scalar(acc[s][:, :], xin[s][:, 0:SEQ], tap(0), None, ALU.mult))
                        for j in range(1, 4):
                            ins = ve.scalar_tensor_tensor(acc[s][:, :], xin[s][:, j:j + SEQ], tap(j), acc[s][:, :],
                                                          ALU.mult, ALU.add)
                            if j < 3:
                                link(ins)
                        ins.then_inc(S["conv_done"], 1)
                link.restart()
                chunked = bank[0][:, 0:CH * 2 * NH0].rearrange("p (c q) -> p q c", c=CH)
                ve.wait_ge(S["gate_mm"], b + 1)
                link(ve.tensor_tensor(gd[:, :, :], chunked[:, 0:NH0, :],
                                      row(4).unsqueeze(2).to_broadcast([P, NH0, CH]), ALU.add))
                ve.tensor_copy(gx[:, :, :], chunked[:, NH0:, :]).then_inc(S["gate_d"], 1)
                ve.scalar_tensor_tensor(ge[:, :, :], gd[:, :, :], -1.0, gd[:, :, :], ALU.mult, ALU.max
                                        ).then_inc(S["gate_e"], 1)
                ve.wait_ge(S["gate_l"], b + 1)
                link(ve.scalar_tensor_tensor(gd[:, :, :], gd[:, :, :], 0.0, ge[:, :, :], ALU.max, ALU.add))
                ve.tensor_tensor(gd[:, :, :], gd[:, :, :], kpar[:, 0, :].unsqueeze(2).to_broadcast([P, NH0, CH]),
                                 ALU.mult).then_inc(S["gate_a"], 1)
                ve.wait_ge(S["a_order"], 2 * b + 3)
                ve.wait_ge(S["gate_d"], b + 1)
                link(ve.tensor_scalar(gd[:, :, :], gd[:, :, :], -1.0, 1.0, ALU.mult, ALU.add))
                link(ve.tensor_tensor(gx[:, :, :], gx[:, :, :], gd[:, :, :], ALU.mult))
                link(ve.tensor_tensor(gx[:, :, :], gx[:, :, :], gx[:, :, :], ALU.mult))
                link(ve.tensor_tensor(gain[:, :, :], gx[:, :, :],
                                      kpar[:, 2, :].unsqueeze(2).to_broadcast([P, NH0, CH]), ALU.mult))
                with ve.Fori(0, PAIRS // 2) as i:
                    for s in range(2):
                        scan(b * (PAIRS // 2) + i, i, s)
                ve.wait_ge(S["o_mm"], b + 1)
                for h in range(2):
                    xs = x[:, bass.ds(b * CH + 2 * h, 2), :]
                    ins = ve.scalar_tensor_tensor(xs, seg[:, 4 * h:4 * h + 4, :].rearrange("p m t -> p (m t)").rearrange("p (c d) -> p c d", c=2),
                                                  par[:, 5 * NH0:], xs, ALU.mult, ALU.add)
                ins.then_inc(S["o_out"], 1)
                ve.wait_ge(S["o_out"], b + 1)


E0, I0 = 8, 512
KH = I0 // P


def gate0(nc, xT, comb, A):
    ctx, sb, ps, sem = scope(nc, "gate0")
    with ctx:
        w = sb("w", [P, KD, E0])
        p = sb("p", [P, NT, E0])
        one = sb("one", [P, NT])
        top = sb("top", [P, NT, 8])
        idx = sb("idx", [P, NT, 8], mybir.dt.uint32)
        idf = sb("idf", [P, NT, 8])
        col = sb("col", [P, E0])
        hit = sb("hit", [P, NT, E0])
        hit2 = sb("hit2", [P, NT, E0])
        logits = ps("logits", [P, NT, E0])
        S = {n: sem(n) for n in ("w", "mm", "order", "shifted", "exp", "col")}
        block = ctx.enter_context(nc.Block())

        @block.sync
        def _(sp):
            sp.dma_start(w[:, :, :], A["gate0_w"]).then_inc(S["w"], 16)

        @block.gpsimd
        def _(pool):
            pool.iota(col[:, :], pattern=[[1, E0]], base=0, channel_multiplier=0,
                      allow_small_or_imprecise_dtypes=True).then_inc(S["col"], 1)

        @block.tensor
        def _(pe):
            pe.wait_ge(S["w"], 16)
            for t in range(NT):
                for k in range(KD):
                    mm = pe.matmul(logits[:, t, :], xT[:, k, t * P:(t + 1) * P], w[:, k, :],
                                   start=(k == 0), stop=(k == KD - 1))
            mm.then_inc(S["mm"], 1)

        @block.scalar
        def _(act):
            act.wait_ge(S["shifted"], 1)
            act.activation(p[:, :, :], p[:, :, :], ACT.Exp).then_inc(S["exp"], 1)

        @block.vector
        def _(ve):
            link = Chain(ve, S["order"])
            wide = lambda t, n: t.unsqueeze(2).to_broadcast([P, NT, n])
            ve.wait_ge(S["mm"], 1)
            link(ve.tensor_reduce(one[:, :], logits[:, :, :], AX_X, ALU.max))
            ve.tensor_tensor(p[:, :, :], logits[:, :, :], wide(one[:, :], E0), ALU.subtract).then_inc(S["shifted"], 1)
            ve.wait_ge(S["exp"], 1)
            link(ve.tensor_reduce(one[:, :], p[:, :, :], AX_X, ALU.add))
            link(ve.reciprocal(one[:, :], one[:, :]))
            link(ve.tensor_tensor(p[:, :, :], p[:, :, :], wide(one[:, :], E0), ALU.mult))
            for t in range(NT):
                ins = ve.max(top[:, t, :], p[:, t, :])
            link(ins)
            for t in range(NT):
                ins = ve.max_index(idx[:, t, :], top[:, t, :], p[:, t, :])
            link(ins)
            link(ve.tensor_tensor(one[:, :], top[:, :, 0], top[:, :, 1], ALU.add))
            link(ve.reciprocal(one[:, :], one[:, :]))
            link(ve.tensor_copy(idf[:, :, :], idx[:, :, :]))
            ve.wait_ge(S["col"], 1)
            cols = col[:, :].unsqueeze(1).to_broadcast([P, NT, E0])
            for n, h in enumerate((hit, hit2)):
                link(ve.tensor_tensor(h[:, :, :], cols, wide(idf[:, :, n], E0), ALU.is_equal))
            link(ve.tensor_tensor(hit[:, :, :], hit[:, :, :], hit2[:, :, :], ALU.add))
            link(ve.tensor_tensor(hit[:, :, :], hit[:, :, :], p[:, :, :], ALU.mult))
            link(ve.memset(comb[:, :, E0:], 1.0))
            link(ve.tensor_tensor(comb[:, :, 0:E0], hit[:, :, :], wide(one[:, :], E0), ALU.mult))


def ffn(nc, tag, x, xT, up_w, down_w, n_exp, comb):
    ctx, sb, ps, sem = scope(nc, tag)
    G = TOK // SEQ
    loops = n_exp // 2
    with ctx:
        wu = [sb(f"wu{s}", [P, KD, 2 * I0]) for s in range(2)]
        wd = [sb(f"wd{s}", [P, KH, D]) for s in range(2)]
        sg = [sb(f"sg{s}", [P, SEQ]) for s in range(2)]
        hT = [sb(f"hT{s}", [P, KH, SEQ]) for s in range(2)]
        gp = [ps(f"g{s}", [P, SEQ]) for s in range(2)]
        up = [ps(f"u{s}", [P, SEQ]) for s in range(2)]
        yp = [ps(f"y{s}", [P, CH, D]) for s in range(2)]
        S = {n: sem(n) for n in ("wu0", "wu1", "wd0", "wd1", "gu_mm", "sg_ready", "h_ready0", "h_ready1",
                                 "y_mm0", "y_mm1", "added0", "added1")}
        block = ctx.enter_context(nc.Block())

        @block.sync
        def _(sp):
            def load(e, s, first):
                if not first:
                    sp.wait_ge(S["gu_mm"], 16 * e - 16)
                sp.dma_start(wu[s][:, :, :], up_w[bass.ds(e, 1)].rearrange("o p k m -> p (o k) m")
                             ).then_inc(S[f"wu{s}"], 16)
                if not first:
                    sp.wait_ge(S["y_mm1"], 2 * e - 2)
                sp.dma_start(wd[s][:, :, :], down_w[bass.ds(e, 1)].rearrange("o p k m -> p (o k) m")
                             ).then_inc(S[f"wd{s}"], 16)

            load(0, 0, True)
            if loops:
                load(1, 1, True)
                with sp.Fori(1, loops) as i:
                    load(2 * i, 0, False)
                    load(2 * i + 1, 1, False)
                load(n_exp - 1, 0, False)

        @block.tensor
        def _(pe):
            def project_up(i, s, j):
                half = 4 * i + 2 * s + j // 2
                q2 = 2 * (8 * i + 4 * s + j)
                if j == 0:
                    pe.wait_ge(S[f"wu{s}"], 16 * i + 16)
                for m in range(KH):
                    pe.wait_ge(S[f"h_ready{m % 2}"], q2 + m // 2)
                    for out, o in ((gp[m % 2], 0), (up[m % 2], I0)):
                        for k in range(KD):
                            mm = pe.matmul(out[:, :], wu[s][:, k, o + m * P:o + (m + 1) * P],
                                           xT[:, k, j * SEQ:(j + 1) * SEQ], start=(k == 0), stop=(k == KD - 1))
                    mm.then_inc(S["gu_mm"], 1)

            def project_down(i, s, j):
                half = 4 * i + 2 * s + j // 2
                q2 = 2 * (8 * i + 4 * s + j)
                if j == 0:
                    pe.wait_ge(S[f"wd{s}"], 16 * i + 16)
                pe.wait_ge(S["h_ready0"], q2 + 2)
                pe.wait_ge(S["h_ready1"], q2 + 2)
                pe.wait_ge(S[f"added{j % 2}"], half)
                for c in range(CH):
                    for k in range(KH):
                        mm = pe.matmul(yp[j % 2][:, c, :], hT[j % 2][:, k, c * P:(c + 1) * P], wd[s][:, k, :],
                                       start=(k == 0), stop=(k == KH - 1))
                mm.then_inc(S[f"y_mm{j % 2}"], 1)

            project_up(0, 0, 0)
            if loops:
                with pe.Fori(0, loops) as i:
                    for n in range(8):
                        project_up(i + (n == 7), (n + 1) // 4 % 2, (n + 1) % 4)
                        project_down(i, n // 4, n % 4)
            for j in range(G):
                if j < G - 1:
                    project_up(loops, 0, j + 1)
                project_down(loops, 0, j)

        @block.scalar
        def _(act):
            def step(i, s, j):
                q = 8 * i + 4 * s + j
                for m in range(KH):
                    act.wait_ge(S["gu_mm"], 4 * q + m + 1)
                    act.wait_ge(S[f"h_ready{m % 2}"], 2 * q + m // 2)
                    act.activation(sg[m % 2][:, :], gp[m % 2][:, :], ACT.Silu).then_inc(S["sg_ready"], 1)

            act.preload_act_table_set("silu_and_others")
            if loops:
                with act.Fori(0, loops) as i:
                    for n in range(8):
                        step(i, n // 4, n % 4)
            for j in range(G):
                step(loops, 0, j)

        @block.vector
        def _(ve):
            def hidden(i, s, j):
                q = 8 * i + 4 * s + j
                ve.wait_ge(S[f"y_mm{j % 2}"], 4 * i + 2 * s + j // 2)
                for m in range(KH):
                    ve.wait_ge(S["sg_ready"], 4 * q + m + 1)
                    ve.tensor_tensor(hT[j % 2][:, m, :], sg[m % 2][:, :], up[m % 2][:, :], ALU.mult
                                     ).then_inc(S[f"h_ready{m % 2}"], 1)

            def add(i, s, j):
                ve.wait_ge(S[f"y_mm{j % 2}"], 4 * i + 2 * s + j // 2 + 1)
                for c in range(CH):
                    t = j * CH + c
                    if comb is None:
                        ins = ve.tensor_tensor(x[:, t, :], yp[j % 2][:, c, :], x[:, t, :], ALU.add)
                    else:
                        ins = ve.scalar_tensor_tensor(x[:, t, :], yp[j % 2][:, c, :],
                                                      comb[:, t, bass.ds(2 * i + s, 1)], x[:, t, :],
                                                      ALU.mult, ALU.add)
                ins.then_inc(S[f"added{j % 2}"], 1)

            hidden(0, 0, 0)
            if loops:
                with ve.Fori(0, loops) as i:
                    for n in range(8):
                        hidden(i + (n == 7), (n + 1) // 4 % 2, (n + 1) % 4)
                        add(i, n // 4, n % 4)
            for j in range(G):
                if j < G - 1:
                    hidden(loops, 0, j + 1)
                add(loops, 0, j)


NH1, DH1 = 16, 16
QG = 4
MASKED = 1e30


def attention(nc, x, xT, ident, A):
    ctx, sb, ps, sem = scope(nc, "attn")
    STEPS = NH1 * CH
    with ctx:
        wqk = sb("wqk", [P, KD, 2 * QG, P])
        wv = sb("wv", [P, KD, D])
        wo = sb("wo", [P, KD, D])
        far = sb("far", [P, SEQ])
        bias = sb("bias", [P, NH1, SEQ])
        xb = sb("xb", [P, KD, SEQ])
        qT = sb("qT", [P, QG, SEQ])
        kT = sb("kT", [P, QG, SEQ])
        v = sb("v", [P, CH, D])
        T = [sb(f"T{i}", [P, SEQ]) for i in range(3)]
        E = [sb(f"E{i}", [P, SEQ]) for i in range(2)]
        ET = [sb(f"ET{i}", [P, SEQ]) for i in range(2)]
        low = sb("low", [P, STEPS])
        rows = sb("rows", [P, QG, CH, 4])
        y = sb("y", [P, CH, D])
        yT = sb("yT", [P, KD, SEQ])
        sc = [ps(f"sc{i}", [P, SEQ]) for i in range(3)]
        tp = [ps(f"tp{i}", [P, SEQ]) for i in range(2)]
        yp = ps("yp", [P, CH, P])
        pj = [ps(f"pj{i}", [P, SEQ]) for i in range(2)]
        names = ("w", "far", "bias", "xb", "pj_mm", "pj_out", "sc_mm", "T_ready", "E_ready", "tp_mm", "ET_ready",
                 "y_mm", "y_out", "yt_mm", "yt_out", "o_mm", "added", "order")
        S = {n: sem(n) for n in names}
        block = ctx.enter_context(nc.Block())

        def step(u):
            g, r, t = u // 16, u % 16 // CH, u % CH
            return g, r, 4 * g + r, t, (t + 1) * P

        NPJ = 2 * QG + CH

        @block.sync
        def _(sp):
            sp.dma_start(wqk[:, :, :, :], A["qk_w"]).then_inc(S["w"], 16)
            sp.dma_start(wv[:, :, :], A["v_w"]).then_inc(S["w"], 16)
            sp.dma_start(wo[:, :, :], A["o_w"]).then_inc(S["w"], 16)

        @block.gpsimd
        def _(pool):
            pool.iota(far[:, :], pattern=[[-1, SEQ]], base=(CH - 1) * P, channel_multiplier=1,
                      allow_small_or_imprecise_dtypes=True).then_inc(S["far"], 1)
            pool.wait_ge(S["far"], 1)
            pool.affine_select(out=far[:, :], in_=far[:, :], compare_op=ALU.is_ge, fill=2 * MASKED * 256.0,
                               base=(CH - 1) * P, pattern=[[-1, SEQ]], channel_multiplier=1).then_inc(S["far"], 1)

        @block.tensor
        def _(pe):
            pe.wait_ge(S["w"], 48)
            with pe.Fori(0, BATCH) as b:
                u0 = b * STEPS

                def project(n):
                    out = pj[n % 2]
                    pe.wait_ge(S[f"pj_out"], b * NPJ + n - 1 if n > 1 else b * NPJ)
                    if n < 2 * QG:
                        for k in range(KD):
                            mm = pe.matmul(out[:, :], wqk[:, k, n, :], xb[:, k, :], start=(k == 0), stop=(k == KD - 1))
                    else:
                        c = n - 2 * QG
                        for k in range(KD):
                            mm = pe.matmul(out[:, 0:D], xb[:, k, c * P:(c + 1) * P], wv[:, k, :],
                                           start=(k == 0), stop=(k == KD - 1))
                    mm.then_inc(S["pj_mm"], 1)

                def scores(u):
                    g, r, h, t, n = step(u)
                    if u > 2:
                        pe.wait_ge(S["T_ready"], u0 + u - 2)
                    rows_ = slice(32 * r, 32 * r + DH1)
                    pe.matmul(sc[u % 3][:, 0:n], qT[rows_, g, t * P:(t + 1) * P], kT[rows_, g, 0:n],
                              start=True, stop=True).then_inc(S["sc_mm"], 1)

                def turn(u):
                    g, r, h, t, n = step(u)
                    pe.wait_ge(S["E_ready"], u0 + u + 1)
                    if u > 1:
                        pe.wait_ge(S["ET_ready"], u0 + u - 1)
                    for j in range(t + 1):
                        mm = pe.transpose(tp[u % 2][:, j * P:(j + 1) * P], E[u % 2][:, j * P:(j + 1) * P], ident[:, :])
                    mm.then_inc(S["tp_mm"], 1)

                def mix(u):
                    g, r, h, t, n = step(u)
                    pe.wait_ge(S["ET_ready"], u0 + u + 1)
                    if u % 16 == 0 and u:
                        pe.wait_ge(S["y_out"], b * QG + g)
                    for j in range(t + 1):
                        mm = pe.matmul(yp[:, t, r * DH1:(r + 1) * DH1], ET[u % 2][:, j * P:(j + 1) * P],
                                       v[:, j, h * DH1:(h + 1) * DH1], start=(j == 0), stop=(j == t))
                    mm.then_inc(S["y_mm"], 1)

                pe.wait_ge(S["xb"], b + 1)
                for n in range(NPJ):
                    project(n)
                pe.wait_ge(S["pj_out"], (b + 1) * NPJ)
                for u in range(3):
                    scores(u)
                for u in range(STEPS):
                    if u + 3 < STEPS:
                        scores(u + 3)
                    turn(u)
                    if u:
                        mix(u - 1)
                mix(STEPS - 1)
                pe.wait_ge(S["y_out"], (b + 1) * QG)
                for k in range(KD):
                    for c in range(CH):
                        mm = pe.transpose(tp[k][:, c * P:(c + 1) * P], y[:, c, k * P:(k + 1) * P], ident[:, :])
                mm.then_inc(S["yt_mm"], 1)
                pe.wait_ge(S["yt_out"], b + 1)
                for c in range(CH):
                    out = pj[c // 2][:, (c % 2) * D:(c % 2 + 1) * D]
                    for k in range(KD):
                        mm = pe.matmul(out, yT[:, k, c * P:(c + 1) * P], wo[:, k, :], start=(k == 0), stop=(k == KD - 1))
                mm.then_inc(S["o_mm"], 1)

        @block.scalar
        def _(act):
            act.preload_act_table_set("natural_log_exp_and_others")
            act.wait_ge(S["w"], 48)
            with act.Fori(0, BATCH) as b:
                u0 = b * STEPS
                act.wait_ge(S["o_mm"], b)
                for n in range(NPJ):
                    act.wait_ge(S["pj_mm"], b * NPJ + n + 1)
                    if n < QG:
                        ins = act.activation(qT[:, n, :], pj[n % 2][:, :], ACT.Copy, scale=-float(DH1) ** -0.5)
                    elif n < 2 * QG:
                        ins = act.activation(kT[:, n - QG, :], pj[n % 2][:, :], ACT.Copy)
                    else:
                        ins = act.activation(v[:, n - 2 * QG, :], pj[n % 2][:, 0:D], ACT.Copy)
                    ins.then_inc(S["pj_out"], 1)
                for u in range(STEPS):
                    g, r, h, t, n = step(u)
                    act.wait_ge(S["T_ready"], u0 + u + 1)
                    if u > 1:
                        act.wait_ge(S["tp_mm"], u0 + u - 1)
                    if u % 16 == 0 and u:
                        act.wait_ge(S["y_out"], b * QG + g - 1 if g > 1 else b * QG)
                    act.activation(E[u % 2][:, 0:n], T[u % 3][:, 0:n], ACT.Exp, bias=low[:, u:u + 1], scale=-1.0,
                                   accum_out=rows[:, g, t, r:r + 1]).then_inc(S["E_ready"], 1)
                act.wait_ge(S["yt_mm"], b + 1)
                for k in range(KD):
                    last = act.activation(yT[:, k, :], tp[k][:, :], ACT.Copy)
                last.then_inc(S["yt_out"], 1)

        @block.vector
        def _(ve):
            link = Chain(ve, S["order"])
            ve.wait_ge(S["far"], 2)
            for h in range(NH1):
                ins = ve.tensor_scalar(bias[:, h, :], far[:, :], 2.0 ** (-8.0 / (h + 1)), None, ALU.mult)
            link(ins)
            with ve.Fori(0, BATCH) as b:
                link.restart()
                u0 = b * STEPS
                ve.wait_ge(S["pj_mm"], b * NPJ)
                ve.tensor_copy(xb[:, :, :], xT[:, :, bass.ds(b * SEQ, SEQ)]).then_inc(S["xb"], 1)

                def negated(u):
                    g, r, h, t, n = step(u)
                    ve.tensor_tensor_reduce(T[u % 3][:, 0:n], sc[u % 3][:, 0:n], bias[:, h, SEQ - n:], 1.0, 3e38,
                                            ALU.add, ALU.min, low[:, u:u + 1]).then_inc(S["T_ready"], 1)

                def copied(u):
                    g, r, h, t, n = step(u)
                    if u + 2 < STEPS:
                        ve.wait_ge(S["sc_mm"], u0 + u + 3)
                    ve.wait_ge(S["tp_mm"], u0 + u + 1)
                    if u > 1:
                        ve.wait_ge(S["y_mm"], u0 + u - 1)
                    ve.tensor_copy(ET[u % 2][:, 0:n], tp[u % 2][:, 0:n]).then_inc(S["ET_ready"], 1)

                def divided(g):
                    ve.wait_ge(S["y_mm"], u0 + 16 * (g + 1))
                    link(ve.reciprocal(rows[:, g, :, :], rows[:, g, :, :]))
                    ve.tensor_tensor(y[:, :, g * 64:(g + 1) * 64].rearrange("p c (r d) -> p c r d", r=4),
                                     yp[:, :, 0:64].rearrange("p c (r d) -> p c r d", r=4),
                                     rows[:, g, :, :].unsqueeze(3).to_broadcast([P, CH, 4, DH1]), ALU.mult
                                     ).then_inc(S["y_out"], 1)

                ve.wait_ge(S["sc_mm"], u0 + 2)
                link(ve.memset(low[:, 0:2], 0.0))
                negated(0)
                negated(1)
                for u in range(STEPS):
                    copied(u)
                    if u + 2 < STEPS:
                        negated(u + 2)
                    if u % 16 == 0 and u:
                        divided(u // 16 - 1)
                divided(QG - 1)
                ve.wait_ge(S["o_mm"], b + 1)
                for c in range(2):
                    xs = x[:, bass.ds(b * CH + 2 * c, 2), :]
                    ins = ve.tensor_tensor(xs, pj[c][:, :].rearrange("p (c d) -> p c d", c=2), xs, ALU.add)
                ins.then_inc(S["added"], 1)


E1, F1, TOP, CAP = 64, 64, 4, 32
SLOTS = E1 * CAP
EG = P // CAP
NG = E1 // EG


def route1(nc, xT, xn, slots, reads, wk, before, ones, xg, A):
    ctx, sb, ps, sem = scope(nc, "route")
    U32 = mybir.dt.uint32
    with ctx:
        w = sb("w", [P, KD, E1])
        rb = sb("rb", [P, E1])
        lg = sb("lg", [P, NT, E1])
        score = sb("score", [P, NT, E1])
        one = sb("one", [P, NT])
        top = sb("top", [P, NT, 8])
        idx = sb("idx", [P, NT, 8], U32)
        idf = sb("idf", [P, NT, 8])
        col = sb("col", [P, E1])
        first = sb("first", [P, E1])
        hit = [sb(f"hit{k}", [P, NT, E1]) for k in range(TOP)]
        mask = sb("mask", [P, NT, E1])
        prior = sb("prior", [P, NT, E1])
        place = sb("place", [P, NT, E1])
        tmp = sb("tmp", [P, NT, E1])
        sf = sb("sf", [P, NT, TOP])
        zero = sb("zero", [P, 4 * D])
        logits = ps("logits", [P, NT, E1])
        rank = ps("rank", [P, NT, E1])
        S = {n: sem(n) for n in ("w", "mm", "order", "shifted", "exp", "col", "zero", "filled", "mask", "rank",
                                 "slots", "sent")}
        block = ctx.enter_context(nc.Block())

        @block.sync
        def _(sp):
            sp.dma_start(w[:, :, :], A["router_w"]).then_inc(S["w"], 16)
            sp.dma_start(rb[:, :], A["router_b"].to_broadcast([P, E1])).then_inc(S["w"], 16)
            sp.wait_ge(S["zero"], 1)
            for g in range(4):
                sp.dma_start(xg[512 * g:512 * g + 512, :].rearrange("(p c) d -> p (c d)", p=P), zero[:, :]
                             ).then_inc(S["filled"], 16)

        @block.gpsimd
        def _(pool):
            pool.memset(zero[:, :], 0.0).then_inc(S["zero"], 1)
            pool.iota(col[:, :], pattern=[[1, E1]], base=0, channel_multiplier=0,
                      allow_small_or_imprecise_dtypes=True).then_inc(S["col"], 1)
            pool.iota(first[:, :], pattern=[[CAP, E1]], base=0, channel_multiplier=0,
                      allow_small_or_imprecise_dtypes=True).then_inc(S["col"], 1)
            pool.wait_ge(S["filled"], 64)
            pool.wait_ge(S["slots"], 1)
            for t in range(NT):
                for k in range(TOP):
                    pool.indirect_dma_start(xg[:, :], bass.IndirectOffsetOnAxis(slots[:, t, k:k + 1], 0), xn[:, t, :], None,
                                            bounds_check=SLOTS - 1, oob_is_err=False).then_inc(S["sent"], 16)
            pool.wait_ge(S["sent"], 16 * NT * TOP)

        @block.tensor
        def _(pe):
            pe.wait_ge(S["w"], 32)
            for t in range(NT):
                for k in range(KD):
                    mm = pe.matmul(logits[:, t, :], xT[:, k, t * P:(t + 1) * P], w[:, k, :],
                                   start=(k == 0), stop=(k == KD - 1))
            mm.then_inc(S["mm"], 1)
            pe.wait_ge(S["mask"], NT - 1)
            for t in range(NT):
                pe.matmul(rank[:, t, :], before[:, :], mask[:, t, :], start=True, stop=False)
                mm = pe.matmul(rank[:, t, :], ones[:, :], prior[:, t, :], start=False, stop=True)
            mm.then_inc(S["rank"], 1)

        @block.scalar
        def _(act):
            act.wait_ge(S["shifted"], 1)
            act.activation(score[:, :, :], score[:, :, :], ACT.Exp).then_inc(S["exp"], 1)

        @block.vector
        def _(ve):
            link = Chain(ve, S["order"])
            wide = lambda t: t.unsqueeze(2).to_broadcast([P, NT, E1])
            tall = lambda t: t[:, :].unsqueeze(1).to_broadcast([P, NT, E1])
            ve.wait_ge(S["mm"], 1)
            ve.wait_ge(S["w"], 32)
            link(ve.tensor_reduce(one[:, :], logits[:, :, :], AX_X, ALU.max))
            ve.tensor_tensor(score[:, :, :], logits[:, :, :], wide(one[:, :]), ALU.subtract).then_inc(S["shifted"], 1)
            link(ve.tensor_tensor(lg[:, :, :], logits[:, :, :], tall(rb), ALU.add))
            for t in range(NT):
                ins = ve.max(top[:, t, :], lg[:, t, :])
            link(ins)
            for t in range(NT):
                ins = ve.max_index(idx[:, t, :], top[:, t, :], lg[:, t, :])
            link(ins)
            link(ve.tensor_copy(idf[:, :, :], idx[:, :, :]))
            ve.wait_ge(S["col"], 2)
            for k in range(TOP):
                link(ve.tensor_tensor(hit[k][:, :, :], tall(col), wide(idf[:, :, k]), ALU.is_equal))
            link(ve.tensor_tensor(mask[:, :, :], hit[0][:, :, :], hit[1][:, :, :], ALU.add))
            link(ve.tensor_tensor(mask[:, :, :], mask[:, :, :], hit[2][:, :, :], ALU.add))
            link(ve.tensor_tensor(mask[:, :, :], mask[:, :, :], hit[3][:, :, :], ALU.add))
            link(ve.memset(prior[:, 0, :], 0.0))
            for t in range(1, NT):
                ve.tensor_tensor(prior[:, t, :], prior[:, t - 1, :], mask[:, t - 1, :], ALU.add
                                 ).then_inc(S["mask"], 1)
                ve.wait_ge(S["mask"], t)
            ve.wait_ge(S["exp"], 1)
            link(ve.tensor_reduce(one[:, :], score[:, :, :], AX_X, ALU.add))
            link(ve.reciprocal(one[:, :], one[:, :]))
            link(ve.tensor_tensor(score[:, :, :], score[:, :, :], wide(one[:, :]), ALU.mult))
            for k in range(TOP):
                link(ve.tensor_tensor(tmp[:, :, :], hit[k][:, :, :], score[:, :, :], ALU.mult))
                link(ve.tensor_reduce(wk[:, :, k], tmp[:, :, :], AX_X, ALU.add))
            link(ve.tensor_reduce(one[:, :], wk[:, :, :], AX_X, ALU.add))
            link(ve.reciprocal(one[:, :], one[:, :]))
            link(ve.tensor_tensor(wk[:, :, :], wk[:, :, :], one[:, :].unsqueeze(2).to_broadcast([P, NT, TOP]), ALU.mult))
            ve.wait_ge(S["rank"], 1)
            link(ve.tensor_scalar(tmp[:, :, :], rank[:, :, :], float(CAP), float(4 * SLOTS), ALU.is_ge, ALU.mult))
            link(ve.tensor_tensor(place[:, :, :], rank[:, :, :], tmp[:, :, :], ALU.add))
            link(ve.tensor_tensor(place[:, :, :], place[:, :, :], tall(first), ALU.add))
            for k in range(TOP):
                link(ve.tensor_tensor(tmp[:, :, :], hit[k][:, :, :], place[:, :, :], ALU.mult))
                link(ve.tensor_reduce(sf[:, :, k], tmp[:, :, :], AX_X, ALU.add))
            ve.tensor_copy(slots[:, :, :], sf[:, :, :]).then_inc(S["slots"], 1)
            kept = tmp[:, :, 0:TOP]
            link(ve.tensor_scalar(kept, sf[:, :, :], float(SLOTS), None, ALU.is_lt))
            link(ve.tensor_tensor(wk[:, :, :], wk[:, :, :], kept, ALU.mult))
            link(ve.tensor_scalar(sf[:, :, :], sf[:, :, :], float(SLOTS - 1), None, ALU.min))
            link(ve.tensor_copy(reads[:, :, :], sf[:, :, :]))


def experts1(nc, ident, xg, yg, A):
    ctx, sb, ps, sem = scope(nc, "exp1")
    with ctx:
        rows = [sb(f"rows{s}", [P, D]) for s in range(2)]
        up_w = [sb(f"up_w{s}", [P, KD, EG, 2 * F1]) for s in range(2)]
        down_w = [sb(f"down_w{s}", [P, EG, D]) for s in range(2)]
        xgT = [sb(f"xgT{s}", [P, D]) for s in range(2)]
        sg = [sb(f"sg{s}", [P, F1]) for s in range(2)]
        h = [sb(f"h{s}", [P, P]) for s in range(2)]
        hT = [sb(f"hT{s}", [P, P]) for s in range(2)]
        y = [sb(f"y{s}", [P, D]) for s in range(2)]
        xtp = [ps(f"xtp{s}", [P, 512]) for s in range(2)]
        gup = [ps(f"gup{s}", [P, 512]) for s in range(2)]
        htp = [ps(f"htp{s}", [P, 512]) for s in range(2)]
        yp = [ps(f"yp{s}", [P, 512]) for s in range(2)]
        names = ("rows", "up_w", "down_w", "xtp", "xgT", "gup", "sg", "h", "htp", "hT", "yp", "y", "stored")
        S = {f"{n}{s}": sem(f"{n}{s}") for n in names for s in range(2)}
        S["padded"] = sem("padded")
        block = ctx.enter_context(nc.Block())

        @block.sync
        def _(sp):
            with sp.Fori(0, NG // 2) as i:
                for s in range(2):
                    g = bass.ds(2 * i + s, 1)
                    sp.wait_ge(S[f"xtp{s}"], i)
                    sp.dma_start(rows[s][:, :], xg[bass.ds((2 * i + s) * P, P), :]).then_inc(S[f"rows{s}"], 16)
                    sp.wait_ge(S[f"gup{s}"], i)
                    sp.dma_start(up_w[s][:, :, :, :], A["up1_w"][g].rearrange("o p k e f -> p (o k) e f")
                                 ).then_inc(S[f"up_w{s}"], 16)
                    sp.wait_ge(S[f"yp{s}"], i)
                    sp.dma_start(down_w[s][0:F1, :, :], A["down1_w"][g].rearrange("o f e d -> f (o e) d")
                                 ).then_inc(S[f"down_w{s}"], 16)

        @block.gpsimd
        def _(pool):
            with pool.Fori(0, NG // 2) as i:
                for s in range(2):
                    pool.wait_ge(S[f"y{s}"], i + 1)
                    pool.wait_ge(S["rows0"], 16)
                    pool.dma_start(yg[bass.ds((2 * i + s) * P, P), :], y[s][:, :]).then_inc(S[f"stored{s}"], 16)
            for s in range(2):
                pool.wait_ge(S[f"stored{s}"], 16 * (NG // 2))

        @block.tensor
        def _(pe):
            def head(n, s):
                pe.wait_ge(S[f"rows{s}"], 16 * n + 16)
                pe.wait_ge(S[f"xgT{s}"], n)
                for k in range(KD):
                    mm = pe.transpose(xtp[s][:, k * P:(k + 1) * P], rows[s][:, k * P:(k + 1) * P], ident[:, :])
                mm.then_inc(S[f"xtp{s}"], 1)
                pe.wait_ge(S[f"up_w{s}"], 16 * n + 16)
                pe.wait_ge(S[f"h{s}"], n)
                pe.wait_ge(S[f"xgT{s}"], n + 1)
                for e in range(EG):
                    r = slice(e * CAP, (e + 1) * CAP)
                    for k in range(KD):
                        mm = pe.matmul(gup[s][r, 0:2 * F1], xgT[s][:, k * P + e * CAP:k * P + (e + 1) * CAP],
                                       up_w[s][:, k, e, :], start=(k == 0), stop=(k == KD - 1))
                mm.then_inc(S[f"gup{s}"], 1)

            def tail(n, s):
                pe.wait_ge(S[f"hT{s}"], n)
                pe.wait_ge(S[f"h{s}"], n + 1)
                pe.transpose(htp[s][:, 0:P], h[s][:, :], ident[:, :]).then_inc(S[f"htp{s}"], 1)
                pe.wait_ge(S[f"hT{s}"], n + 1)
                pe.wait_ge(S[f"y{s}"], n)
                pe.wait_ge(S[f"down_w{s}"], 16 * n + 16)
                for e in range(EG):
                    r = slice(e * CAP, (e + 1) * CAP)
                    mm = pe.matmul(yp[s][r, 0:D], hT[s][:, r], down_w[s][:, e, :], start=True, stop=True)
                mm.then_inc(S[f"yp{s}"], 1)

            pe.wait_ge(S["padded"], 4)
            head(0, 0)
            with pe.Fori(0, NG // 2 - 1) as i:
                head(i, 1)
                tail(i, 0)
                head(i + 1, 0)
                tail(i, 1)
            n = NG // 2 - 1
            head(n, 1)
            tail(n, 0)
            tail(n, 1)

        @block.scalar
        def _(act):
            act.preload_act_table_set("silu_and_others")

            def head(n, s):
                act.wait_ge(S[f"xtp{s}"], n + 1)
                act.wait_ge(S[f"gup{s}"], n)
                act.activation(xgT[s][:, :], xtp[s][:, 0:D], ACT.Copy).then_inc(S[f"xgT{s}"], 1)
                act.wait_ge(S[f"gup{s}"], n + 1)
                act.wait_ge(S[f"h{s}"], n)
                act.activation(sg[s][:, :], gup[s][:, 0:F1], ACT.Silu).then_inc(S[f"sg{s}"], 1)

            with act.Fori(0, NG // 2) as i:
                head(i, 0)
                head(i, 1)

        @block.vector
        def _(ve):
            def head(n, s):
                ve.wait_ge(S[f"htp{s}"], n)
                ve.wait_ge(S[f"sg{s}"], n + 1)
                ve.tensor_tensor(h[s][:, 0:F1], gup[s][:, F1:2 * F1], sg[s][:, :], ALU.mult).then_inc(S[f"h{s}"], 1)

            def tail(n, s):
                ve.wait_ge(S[f"htp{s}"], n + 1)
                ve.wait_ge(S[f"yp{s}"], n)
                ve.tensor_copy(hT[s][:, :], htp[s][:, 0:P]).then_inc(S[f"hT{s}"], 1)
                ve.wait_ge(S[f"yp{s}"], n + 1)
                ve.wait_ge(S[f"stored{s}"], 16 * n)
                ve.tensor_copy(y[s][:, :], yp[s][:, 0:D]).then_inc(S[f"y{s}"], 1)

            for s in range(2):
                ve.memset(h[s][:, F1:], 0.0).then_inc(S["padded"], 1)
                ve.memset(down_w[s][F1:, :, :], 0.0).then_inc(S["padded"], 1)
            ve.wait_ge(S["padded"], 4)
            head(0, 0)
            with ve.Fori(0, NG // 2 - 1) as i:
                head(i, 1)
                tail(i, 0)
                head(i + 1, 0)
                tail(i, 1)
            n = NG // 2 - 1
            head(n, 1)
            tail(n, 0)
            tail(n, 1)


def combine1(nc, x, reads, wk, yg):
    ctx, sb, ps, sem = scope(nc, "comb1")
    R = 8
    with ctx:
        row = [sb(f"row{i}", [P, D]) for i in range(R)]
        come = [sem(f"come{i}") for i in range(R)]
        used = sem("used")
        block = ctx.enter_context(nc.Block())

        @block.gpsimd
        def _(pool):
            for n in range(NT * TOP):
                t, k = n // TOP, n % TOP
                if n >= R:
                    pool.wait_ge(used, n - R + 1)
                pool.indirect_dma_start(row[n % R][:, :], None, yg[:, :], bass.IndirectOffsetOnAxis(reads[:, t, k:k + 1], 0)
                                        ).then_inc(come[n % R], 16)

        @block.vector
        def _(ve):
            for n in range(NT * TOP):
                t, k = n // TOP, n % TOP
                ve.wait_ge(come[n % R], 16 * (n // R) + 16)
                if n:
                    ve.wait_ge(used, n)
                ve.scalar_tensor_tensor(x[:, t, :], row[n % R][:, :], wk[:, t, k:k + 1], x[:, t, :],
                                        ALU.mult, ALU.add).then_inc(used, 1)


def gated_bias_setup(nc, norm_w, gb, gate, A):
    ctx, sb, ps, sem = scope(nc, "gb")
    with ctx:
        ld = sem("ld")
        done = sem("done")
        block = ctx.enter_context(nc.Block())

        @block.sync
        def _(sp):
            sp.dma_start(norm_w[:, :], A["norm_w"]).then_inc(ld, 16)
            sp.dma_start(gb[:, :], A["out_b"].to_broadcast([P, D])).then_inc(ld, 16)
            sp.dma_start(gate[:, :], A["res_gate"].to_broadcast([P, 1])).then_inc(ld, 16)

        @block.vector
        def _(ve):
            ve.wait_ge(ld, 48)
            ve.tensor_scalar(gb[:, :], gb[:, :], gate[:, 0:1], None, ALU.mult).then_inc(done, 1)
            ve.wait_ge(done, 1)


def store(nc, x, out):
    ctx, sb, ps, sem = scope(nc, "st")
    with ctx:
        done = sem("done")
        block = ctx.enter_context(nc.Block())

        @block.sync
        def _(sp):
            sp.dma_start(out.rearrange("(t p) d -> p t d", p=P), x[:, :, :]).then_inc(done, 16)
            sp.wait_ge(done, 16)


def program(nc, A):
    USED.clear()
    with ExitStack() as ctx:
        sb = lambda name, shape: ctx.enter_context(nc.sbuf_tensor(name, shape, F32))
        x = sb("x", [P, NT, D])
        xT = sb("xT", [P, KD, TOK])
        ident, tri, after, ones = (sb(n, [P, P]) for n in ("ident", "upto", "after", "ones"))
        pair_rows = sb("pair_rows", [P, 2])
        norm_w = sb("norm_w", [P, KD])
        gb = sb("gb", [P, D])
        gate = sb("gate", [P, 1])
        constants(nc, ident, tri, after, ones, pair_rows)
        gated_bias_setup(nc, norm_w, gb, gate, A)
        normalise(nc, "n0", x, xT, ident, x_dram=A["x"], rms=(norm_w[:, :], gb[:, :]))
        mixer(nc, x, xT, ident, tri, after, ones, pair_rows, A)
        clear_semaphores(nc)
        normalise(nc, "n1", x, xT, ident)
        with nc.sbuf_tensor("comb", [P, NT, E0 + 1], F32) as comb:
          gate0(nc, xT, comb, A)
          ffn(nc, "exp0", x, xT, A["up0_w"], A["down0_w"], E0 + 1, comb)
        normalise(nc, "n2", x, xT, ident)
        attention(nc, x, xT, ident, A)
        xg = nc.dram_tensor("slot_rows", [SLOTS, D], F32).ap()
        yg = nc.dram_tensor("slot_results", [SLOTS, D], F32).ap()
        xn = sb("xn", [P, NT, D])
        before = sb("before", [P, P])
        slots = ctx.enter_context(nc.sbuf_tensor("slots", [P, NT, TOP], mybir.dt.uint32))
        reads = ctx.enter_context(nc.sbuf_tensor("reads", [P, NT, TOP], mybir.dt.uint32))
        wk = sb("wk", [P, NT, TOP])
        strict(nc, before, tri, ident)
        normalise(nc, "n3", x, xT, ident, rows=xn)
        route1(nc, xT, xn, slots, reads, wk, before, ones, xg, A)
        ffn(nc, "shared", x, xT, A["shup_w"], A["shdown_w"], 1, None)
        experts1(nc, ident, xg, yg, A)
        combine1(nc, x, reads, wk, yg)
        store(nc, x, A["out"])


def strict(nc, before, upto, ident):
    ctx, sb, ps, sem = scope(nc, "strict")
    with ctx:
        done = sem("done")
        block = ctx.enter_context(nc.Block())

        @block.vector
        def _(ve):
            ve.tensor_tensor(before[:, :], upto[:, :], ident[:, :], ALU.subtract).then_inc(done, 1)
            ve.wait_ge(done, 1)


def layouts(i):
    i = {k: np.asarray(v) for k, v in i.items()}
    c = np.ascontiguousarray
    a = {}
    a["x"] = c(i["L0_attn_hidden_states"].reshape(TOK, D))
    a["norm_w"] = c(i["L0_attn_norm_w"].reshape(KD, P).T)
    a["out_b"] = c(i["L0_attn_out_proj_b"][None])
    a["res_gate"] = c(i["L0_attn_res_gate"][None])
    w = i["L0_attn_in_proj_w"].T.reshape(KD, P, 2, KI, P)
    a["in_w"] = c(w.transpose(3, 1, 2, 0, 4).reshape(KI, P, 2 * KD, P))
    a["in_b"] = c(i["L0_attn_in_proj_b"].reshape(2 * KI, P).T)
    a["conv_w"] = c(i["L0_attn_conv_w"].reshape(KI, P, 4).transpose(1, 0, 2))
    a["conv_b"] = c(i["L0_attn_conv_b"].reshape(KI, P).T)
    xw = i["L0_attn_x_proj_w"].reshape(NH0, 1 + 2 * NS, DI)
    xb = i["L0_attn_x_proj_b"].reshape(NH0, 1 + 2 * NS)
    bc = xw[:, 1:].reshape(PAIRS, 2, 2, NS, KI, P)
    a["bc_w"] = c(bc.transpose(0, 2, 5, 4, 1, 3).reshape(PAIRS * 2, P, KI, P))
    a["bc_b"] = c(xb[:, 1:].reshape(PAIRS, 2, 2, NS).transpose(1, 3, 0, 2).reshape(P, PAIRS, 2))
    means = np.zeros((DI, NH0), np.float32)
    means[np.arange(DI), np.arange(DI) // DH] = 1.0 / DH
    a["dt_w"] = c(np.concatenate([xw[:, 0].T, means], 1).reshape(KI, P, 2 * NH0).transpose(1, 0, 2))
    a["par"] = c(np.concatenate([i["L0_attn_A_log"], i["L0_attn_log2_alpha_base"], i["L0_attn_log2_beta"],
                                 i["L0_attn_surprise_ema"], xb[:, 0], i["L0_attn_res_gate"]])[None])
    a["out_w"] = c(i["L0_attn_out_proj_w"].T.reshape(KI, P, D).transpose(1, 0, 2))
    a["gate0_w"] = c(i["L0_ffn_gate_w"].reshape(KD, P, E0).transpose(1, 0, 2))
    up = np.concatenate([i["L0_ffn_expert_gate_up"], i["L0_ffn_base_gate_up"][None]])
    a["up0_w"] = c(up.reshape(E0 + 1, KD, P, 2 * I0).transpose(0, 2, 1, 3))
    down = np.concatenate([i["L0_ffn_expert_down"], i["L0_ffn_base_down"][None]])
    a["down0_w"] = c(down.reshape(E0 + 1, KH, P, D).transpose(0, 2, 1, 3))
    qkv = i["L1_attn_W_qkv"].reshape(KD, P, 3, QG, 4, DH1)
    strips = np.zeros((P, KD, 2, QG, 4, 2, DH1), np.float32)
    strips[:, :, :, :, :, 0] = qkv[:, :, 0:2].transpose(1, 0, 2, 3, 4, 5)
    a["qk_w"] = c(strips.reshape(P, KD, 2 * QG, P))
    a["v_w"] = c(qkv[:, :, 2].reshape(KD, P, D).transpose(1, 0, 2))
    a["o_w"] = c(i["L1_attn_W_o"].reshape(KD, P, D).transpose(1, 0, 2))
    a["router_w"] = c(i["L1_ffn_router_w"].T.reshape(KD, P, E1).transpose(1, 0, 2))
    a["router_b"] = c(i["L1_ffn_router_bias"][None])
    gu = np.stack([i["L1_ffn_gate_w"], i["L1_ffn_up_w"]], 1).reshape(NG, EG, 2, F1, KD, P)
    a["up1_w"] = c(gu.transpose(0, 5, 4, 1, 2, 3).reshape(NG, P, KD, EG, 2 * F1))
    a["down1_w"] = c(i["L1_ffn_down_w"].reshape(NG, EG, D, F1).transpose(0, 3, 1, 2))
    sh = np.concatenate([i["L1_ffn_sh_gate_w"].reshape(I0, D), i["L1_ffn_sh_up_w"].reshape(I0, D)])
    a["shup_w"] = c(sh.T.reshape(1, KD, P, 2 * I0).transpose(0, 2, 1, 3))
    a["shdown_w"] = c(i["L1_ffn_sh_down_w"].transpose(0, 2, 1).reshape(1, KH, P, D).transpose(0, 2, 1, 3))
    return a


def kernel(**inputs):
    from concourse import bacc
    from concourse.bass_utils import run_bass_kernel_spmd

    arrays = layouts(inputs)
    nc = bacc.Bacc("TRN2", target_bir_lowering=False, num_devices=1)
    A = {n: nc.dram_tensor(f"in_{n}", a.shape, mybir.dt.from_np(a.dtype), kind="ExternalInput").ap()
         for n, a in arrays.items()}
    A["out"] = nc.dram_tensor("out", [TOK, D], F32, kind="ExternalOutput").ap()
    program(nc, A)
    r = run_bass_kernel_spmd(nc, [{f"in_{n}": a for n, a in arrays.items()}], core_ids=[0])
    return r.results[0]["out"].reshape(BATCH, SEQ, D)
```

```python
from contextlib import ExitStack

import numpy as np

import concourse.bass as bass
from concourse import mybir

ACT = mybir.ActivationFunctionType
ALU = mybir.AluOpType
F32 = mybir.dt.float32
F32R = mybir.dt.float32r
I32 = mybir.dt.int32
AX_X = mybir.AxisListType.X

P = 128
D = 256
KD = D // P
BATCH, SEQ = 4, 512
TOK = BATCH * SEQ
NT = TOK // P
CH = SEQ // P
LN_EPS = 1e-5
RMS_EPS = float(np.finfo(np.float32).eps)

NH0, DH, NS = 24, 64, 64
DI = NH0 * DH
KI = DI // P
PAIRS = KI
DTC = 64
HC = 2 * CH
LN2 = float(np.log(2.0))


class Chain:

    def __init__(self, eng, sem):
        self.eng, self.sem, self.n = eng, sem, 0

    def __call__(self, ins):
        self.n += 1
        ins.then_inc(self.sem, 1)
        self.eng.wait_ge(self.sem, self.n)

    def restart(self):
        self.eng.sem_clear(self.sem)
        self.n = 0


def rsqrt(ve, link, out, v, tmp):
    link(ve.tensor_scalar(tmp.bitcast(I32), v.bitcast(I32), 1, None, ALU.logical_shift_right))
    link(ve.tensor_scalar(out.bitcast(I32), tmp.bitcast(I32), -1.0, float(0x5F3759DF), ALU.mult, ALU.add))
    for _ in range(3):
        link(ve.tensor_tensor(tmp, out, out, ALU.mult))
        link(ve.scalar_tensor_tensor(tmp, tmp, -0.5, v, ALU.mult, ALU.mult))
        link(ve.scalar_tensor_tensor(out, tmp, 1.5, out, ALU.add, ALU.mult))


def scope(nc, tag):
    ctx = ExitStack()

    def sb(name, shape, dt=F32):
        return ctx.enter_context(nc.sbuf_tensor(f"{tag}_{name}", shape, dt))

    def ps(name, shape, dt=F32):
        return ctx.enter_context(nc.psum_tensor(f"{tag}_{name}", shape, dt))

    def sem(name):
        USED.append(ctx.enter_context(nc.semaphore(f"{tag}_{name}")))
        return USED[-1]

    return ctx, sb, ps, sem


USED = []


def clear_semaphores(nc):
    with nc.Block() as block:
        @block.gpsimd
        def _(pool):
            for s in USED:
                pool.sem_clear(s)
    USED.clear()


def constants(nc, ident, upto, after, ones):
    ctx, sb, ps, sem = scope(nc, "const")
    with ctx:
        filled = sem("filled")
        made = sem("made")
        block = ctx.enter_context(nc.Block())

        @block.gpsimd
        def _(pool):
            pool.memset(ident[:, :], 0.0).then_inc(filled, 1)
            for m in (upto, after, ones):
                pool.memset(m[:, :], 1.0).then_inc(filled, 1)
            pool.wait_ge(filled, 4)
            sel = pool.affine_select
            sel(out=ident[:, :], in_=ident[:, :], compare_op=ALU.not_equal, fill=1.0, base=0,
                pattern=[[-1, P]], channel_multiplier=1).then_inc(made, 1)
            sel(out=upto[:, :], in_=upto[:, :], compare_op=ALU.is_ge, fill=0.0, base=0,
                pattern=[[1, P]], channel_multiplier=-1).then_inc(made, 1)
            sel(out=after[:, :], in_=after[:, :], compare_op=ALU.is_gt, fill=0.0, base=0,
                pattern=[[-1, P]], channel_multiplier=1).then_inc(made, 1)
            pool.wait_ge(made, 3)


def normalise(nc, tag, x, xT, ident, x_dram=None, rms=None, rows=None):
    ctx, sb, ps, sem = scope(nc, tag)
    with ctx:
        stats = sb("stats", [P, NT, 6])
        mv = sb("mv", [P, NT, 2])
        var = sb("var", [P, NT])
        rstd = sb("rstd", [P, NT])
        rrms = sb("rrms", [P, NT])
        tmp = sb("tmp", [P, NT])
        hrow = sb("hrow", [P, 2, D])
        xrow = sb("xrow", [P, 2, D])
        trans = [ps(f"trans{s}", [P, 512]) for s in range(2)]
        loaded = sem("loaded")
        order = sem("order")
        row_ready = sem("row_ready")
        turned = sem("turned")
        stored = sem("stored")
        block = ctx.enter_context(nc.Block())

        if x_dram is not None:
            @block.sync
            def _(sp):
                for g in range(4):
                    sp.dma_start(x[:, 4 * g:4 * g + 4, :],
                                 x_dram[512 * g:512 * g + 512, :].rearrange("(t p) d -> p t d", p=P)
                                 ).then_inc(loaded, 16)

        @block.vector
        def _(ve):
            link = Chain(ve, order)
            if x_dram is not None:
                ve.wait_ge(loaded, 64)
            with ve.Fori(0, NT) as t:
                ve.bn_stats(stats[:, bass.ds(t, 1), :], x[:, bass.ds(t, 1), :].rearrange("p o d -> p (o d)"))
            link(ve.memset(tmp[:, :], 0.0))
            ve.drain().then_inc(order, 1)
            link.n += 1
            ve.wait_ge(order, link.n)
            for t in range(NT):
                ve.bn_aggr(mv[:, t, :], stats[:, t, :])
            ve.drain().then_inc(order, 1)
            link.n += 1
            ve.wait_ge(order, link.n)
            link(ve.tensor_scalar(var[:, :], mv[:, :, 1], LN_EPS, None, ALU.add))
            rsqrt(ve, link, rstd[:, :], var[:, :], tmp[:, :])
            if rms:
                norm_w, gated_bias = rms
                link(ve.tensor_tensor(var[:, :], mv[:, :, 1], rstd[:, :], ALU.mult))
                link(ve.tensor_tensor(var[:, :], var[:, :], rstd[:, :], ALU.mult))
                link(ve.tensor_scalar(var[:, :], var[:, :], RMS_EPS, None, ALU.add))
                rsqrt(ve, link, rrms[:, :], var[:, :], tmp[:, :])
            with ve.Fori(0, NT // 2) as i:
                link.restart()
                for s in range(2):
                    t = bass.ds(2 * i + s, 1)
                    h = hrow[:, s:s + 1, :]
                    ve.wait_ge(turned, 2 * i + s)
                    if rms:
                        link(ve.tensor_scalar(h, x[:, t, :], mv[:, t, 0:1].rearrange("p o c -> p (o c)"),
                                              rstd[:, t], ALU.subtract, ALU.mult))
                        ve.tensor_scalar(xrow[:, s:s + 1, :], h, rrms[:, t], None, ALU.mult).then_inc(row_ready, 1)
                        link(ve.tensor_tensor(h, h, gated_bias.unsqueeze(1), ALU.add))
                        link(ve.tensor_tensor(x[:, t, :], x[:, t, :], h, ALU.add))
                    else:
                        out = rows[:, t, :] if rows is not None else xrow[:, s:s + 1, :]
                        ve.tensor_scalar(xrow[:, s:s + 1, :], x[:, t, :], mv[:, t, 0:1].rearrange("p o c -> p (o c)"),
                                         rstd[:, t], ALU.subtract, ALU.mult).then_inc(row_ready, 1)
                        if rows is not None:
                            ve.tensor_scalar(rows[:, t, :], x[:, t, :],
                                             mv[:, t, 0:1].rearrange("p o c -> p (o c)"),
                                             rstd[:, t], ALU.subtract, ALU.mult)

        @block.tensor
        def _(pe):
            with pe.Fori(0, NT // 2) as i:
                for s in range(2):
                    pe.wait_ge(row_ready, 2 * i + s + 1)
                    pe.wait_ge(stored, 2 * i + s)
                    for k in range(KD):
                        mm = pe.transpose(trans[s][:, k * P:(k + 1) * P], xrow[:, s, k * P:(k + 1) * P], ident[:, :])
                    mm.then_inc(turned, 1)

        @block.scalar
        def _(act):
            act.preload_act_table_set("natural_log_exp_and_others")
            with act.Fori(0, NT // 2) as i:
                for s in range(2):
                    act.wait_ge(turned, 2 * i + s + 1)
                    for k in range(KD):
                        last = act.activation(xT[:, k, bass.ds((2 * i + s) * P, P)], trans[s][:, k * P:(k + 1) * P],
                                              ACT.Copy, scale=rms[0][:, k:k + 1] if rms else 1.0)
                    last.then_inc(stored, 1)


def mixer(nc, x, xT, ident, upto, after, ones, A):
    ctx, sb, ps, sem = scope(nc, "mix")
    with ctx:
        in_b = sb("in_b", [P, 2 * KI])
        conv_w = sb("conv_w", [P, KI, 4])
        conv_b = sb("conv_b", [P, KI])
        bc_b = sb("bc_b", [P, PAIRS, 2])
        dt_h = sb("dt_h", [P, KI, DTC], F32R)
        dt_l = sb("dt_l", [P, KI, DTC], F32R)
        out_w = sb("out_w", [P, KI, D])
        par = sb("par", [P, 5 * NH0 + 1])
        kpar = sb("kpar", [P, 4, NH0])
        ab = sb("ab", [P, NH0, CH])
        omab = sb("omab", [P, NH0, CH])
        after_r = sb("after_r", [P, P], F32R)
        xTh = sb("xTh", [P, KD, SEQ], F32R)
        xTl = sb("xTl", [P, KD, SEQ], F32R)
        xc_h = sb("xc_h", [P, KI, SEQ], F32R)
        xc_l = sb("xc_l", [P, KI, SEQ], F32R)
        zy = sb("zy", [P, KI, SEQ])
        dt_w = zy[:, :, 0:DTC]
        w_in = [sb(f"w_in{s}", [P, 4, P]) for s in range(2)]
        w_in_h = [sb(f"w_in_h{s}", [P, 4, P], F32R) for s in range(2)]
        w_in_l = [sb(f"w_in_l{s}", [P, 4, P], F32R) for s in range(2)]
        xin = [sb(f"xin{s}", [P, SEQ + 4]) for s in range(2)]
        acc = [sb(f"acc{s}", [P, SEQ]) for s in range(2)]
        gd = sb("gd", [P, NH0, CH])
        ge = sb("ge", [P, NH0, CH])
        gx = sb("gx", [P, NH0, CH])
        gain = sb("gain", [P, NH0, CH])
        w = sb("w", [P, KI, P])
        w_h = {m: sb(f"w_{m}_h", [P, KI, P], F32R) for m in "bc"}
        w_l = {m: sb(f"w_{m}_l", [P, KI, P], F32R) for m in "bc"}
        bT = sb("bT", [P, SEQ])
        cT = sb("cT", [P, SEQ])
        sq_c, sq_b = (t[:, 4:] for t in xin)
        nb = sb("nb", [P, HC])
        rb = sb("rb", [P, HC])
        ncn = sb("ncn", [P, HC])
        rc = sb("rc", [P, HC])
        nt = sb("nt", [P, HC])
        u = sb("u", [P, HC])
        e2 = sb("e2", [P, HC])
        alpha = sb("alpha", [P, HC])
        lna = sb("lna", [P, HC])
        lna_h = sb("lna_h", [P, HC], F32R)
        lna_l = sb("lna_l", [P, HC])
        wj = sb("wj", [P, HC])
        ul_h = sb("ul_h", [P, HC, P], F32R)
        ul_l = sb("ul_l", [P, HC, P], F32R)
        dec = sb("dec", [P, HC, P])
        dtT = acc[0]
        ecum = sb("ecum", [P, 3 * HC])
        ecr = sb("ecr", [P, HC])
        xst = acc[1]
        xw = sb("xw", [P, CH, P])
        bf = sb("bf", [P, CH - 1, P])
        prob = dec
        state = sb("state", [P, CH - 1, P])
        ys = acc[0]
        yi = sq_c

        proj = {"b": ps("proj_b", [P, 512]), "c": ps("proj_c", [P, 512])}
        seg = ps("seg", [P, HC, P])
        bank4, bank5, bank6, bank7 = (ps(f"bank{i}", [P, 512]) for i in range(4, 8))

        names = ("params", "kready", "order", "w_in_ld0", "w_in_ld1", "w_in_hi", "w_in_lo0", "w_in_lo1", "xT_hi", "xT_lo",
                 "inproj0", "inproj1", "inproj2", "inproj3", "xin_ready", "conv_done", "xs_ready", "xc_hi", "xc_ready", "const_hi", "const_lo",
                 "dtT_mm", "dtT_ready", "gate_mm", "gate_d", "gate_e", "gate_l", "gate_a", "a_order",
                 "w_ld", "b_hi", "c_hi", "b_lo", "c_lo", "b_proj", "c_proj", "b_out", "c_out",
                 "bsq_ready", "csq_ready", "tanh_in", "tanh_out", "alpha_ready", "lna_ready", "ul_h_ready",
                 "ul_l_ready", "cum_mm", "cum_out", "seg_mm", "seg_out", "dec_ready", "xst_ready",
                 "xt_mm", "xw_ready", "bt_mm", "bf_ready", "ct_mm", "s_mm", "prob_ready", "ds_mm", "state_ready",
                 "y_mm", "ys_ready", "yt_mm", "zy_ready", "o_mm", "o_out")
        S = {n: sem(n) for n in names}
        block = ctx.enter_context(nc.Block())
        flat = lambda t: t[:, :, :].rearrange("p c q -> p (c q)")

        @block.sync
        def _(sp):
            for dst, src in ((in_b[:, :], "in_b"), (conv_w[:, :, :], "conv_w"), (conv_b[:, :], "conv_b"),
                             (bc_b[:, :, :], "bc_b"), (dt_w, "dt_w"), (out_w[:, :, :], "out_w")):
                sp.dma_start(dst, A[src]).then_inc(S["params"], 16)
            sp.dma_start(par[:, :], A["par"].to_broadcast([P, 5 * NH0 + 1])).then_inc(S["params"], 16)

            with sp.Fori(0, BATCH) as b:
                def load(g, i, n, m):
                    sp.wait_ge(S["bc"[1 - n] + "_lo"], g + n)
                    sp.dma_start(w[:, :, :], A["bc_w"][bass.ds(2 * i + n, 1)].rearrange("o p k m -> p (o k) m")
                                 ).then_inc(S["w_ld"], 16)

                def load_in(j):
                    for q in range(4):
                        s = q % 2
                        sp.wait_ge(S[f"w_in_lo{s}"], 2 * (b * (KI // 4) + j) + q // 2)
                        sp.dma_start(w_in[s][:, :, :], A["in_w"][bass.ds(4 * j + q, 1)].rearrange("o p k m -> p (o k) m")
                                     ).then_inc(S[f"w_in_ld{s}"], 16)

                load_in(0)
                load(b * PAIRS, 0, 0, "b")
                load_in(1)
                load(b * PAIRS, 0, 1, "c")
                load_in(2)
                with sp.Fori(1, PAIRS) as i:
                    load(b * PAIRS + i, i, 0, "b")
                    load(b * PAIRS + i, i, 1, "c")

        @block.tensor
        def _(pe):
            def three(out, a_h, a_l, b_h, b_l, first, last):
                pe.matmul(out, a_h, b_h, start=first, stop=False)
                pe.matmul(out, a_h, b_l, start=False, stop=False)
                return pe.matmul(out, a_l, b_h, start=False, stop=last)

            def project(g, m, ks, b=None):
                if 0 in ks:
                    pe.wait_ge(S[m + "_lo"], g + 1)
                    pe.wait_ge(S[m + "_out"], g)
                for k in ks:
                    if b is not None:
                        pe.wait_ge(S["xc_ready"], b * KI + k + 1)
                    mm = three(proj[m][:, :], w_h[m][:, k, :], w_l[m][:, k, :], xc_h[:, k, :], xc_l[:, k, :],
                               k == 0, k == KI - 1)
                if KI - 1 in ks:
                    mm.then_inc(S[m + "_proj"], 1)

            def out_project(ks):
                for c in range(CH):
                    out = proj["bc"[c // 2]][:, (c % 2) * D:(c % 2 + 1) * D]
                    for k in ks:
                        mm = pe.matmul(out, zy[:, k, c * P:(c + 1) * P], out_w[:, k, :],
                                       start=(k == 0 and c % 2 == 0), stop=(k == KI - 1), skip_group_check=True)
                return mm

            def turn_y(g):
                pe.wait_ge(S["ys_ready"], g)
                for c in range(CH):
                    mm = pe.transpose(bank7[:, c * P:(c + 1) * P], ys[:, c * P:(c + 1) * P], ident[:, :])
                mm.then_inc(S["yt_mm"], 1)

            def scan(b, i, first, last):
                g = b * PAIRS + i
                pe.wait_ge(S["b_out"], g + 1)
                pe.wait_ge(S["state_ready"], g)
                for c in range(CH):
                    mm = pe.transpose(bank5[:, c * P:(c + 1) * P], bT[:, c * P:(c + 1) * P], ident[:, :])
                mm.then_inc(S["bt_mm"], 1)
                pe.wait_ge(S["xst_ready"], g + 1)
                pe.wait_ge(S["csq_ready"], g)
                for c in range(CH):
                    mm = pe.transpose(bank4[:, c * P:(c + 1) * P], xst[:, c * P:(c + 1) * P], ident[:, :])
                mm.then_inc(S["xt_mm"], 1)
                if first:
                    project(g, "c", range(KI))
                else:
                    project(g, "c", range(4))
                    turn_y(g)
                    project(g, "c", range(4, KI))
                pe.wait_ge(S["lna_ready"], g + 1)
                pe.wait_ge(S["cum_out"], g)
                for n, m in enumerate((after, ones, upto)):
                    mm = pe.matmul(bank6[:, n * HC:(n + 1) * HC], m[:, :], lna[:, :], start=True, stop=True)
                mm.then_inc(S["cum_mm"], 1)
                pe.wait_ge(S["ul_h_ready"], g + 1)
                pe.wait_ge(S["ul_l_ready"], g + 1)
                pe.wait_ge(S["prob_ready"], g)
                for h in range(2):
                    r = slice(h * CH, (h + 1) * CH)
                    pe.matmul(seg[:, r, :], after_r[:, :], ul_h[:, r, :], start=True, stop=False)
                    mm = pe.matmul(seg[:, r, :], after_r[:, :], ul_l[:, r, :], start=False, stop=True)
                mm.then_inc(S["seg_mm"], 1)
                pe.wait_ge(S["c_out"], g + 1)
                pe.wait_ge(S["xw_ready"], g + 1)
                for c in range(CH):
                    mm = pe.transpose(bank4[:, c * P:(c + 1) * P], cT[:, c * P:(c + 1) * P], ident[:, :])
                mm.then_inc(S["ct_mm"], 1)
                if last:
                    pe.wait_ge(S["zy_ready"], g)
                    out_project(range(KI - 1))
                else:
                    project(g + 1, "b", range(KI // 2))
                pe.wait_ge(S["seg_out"], g + 1)
                for h in range(2):
                    for c in range(CH):
                        r = slice(h * DH, (h + 1) * DH)
                        mm = pe.matmul(seg[:, h * CH + c, :], bT[r, c * P:(c + 1) * P],
                                       cT[r, c * P:(c + 1) * P], start=True, stop=True)
                mm.then_inc(S["s_mm"], 1)
                pe.wait_ge(S["bf_ready"], g + 1)
                for c in range(CH - 1):
                    mm = pe.matmul(bank5[:, c * P:(c + 1) * P], bf[:, c, :], xw[:, c, :], start=True, stop=True)
                mm.then_inc(S["ds_mm"], 1)
                if not last:
                    project(g + 1, "b", range(KI // 2, KI))
                pe.wait_ge(S["prob_ready"], g + 1)
                pe.wait_ge(S["zy_ready"], g)
                for c in range(CH):
                    for h in range(2):
                        mm = pe.matmul(bank7[:, c * P + h * DH:c * P + (h + 1) * DH], prob[:, h * CH + c, :],
                                       xw[:, c, h * DH:(h + 1) * DH], start=True, stop=True)
                pe.wait_ge(S["state_ready"], g + 1)
                for c in range(1, CH):
                    mm = pe.matmul(bank6[:, c * P:(c + 1) * P], cT[:, c * P:(c + 1) * P], state[:, c - 1, :],
                                   start=True, stop=True)
                mm.then_inc(S["y_mm"], 1)

            pe.wait_ge(S["params"], 16 * 7)
            with pe.Fori(0, BATCH) as b:
                with pe.Fori(0, KI // 4) as j:
                    for q in range(4):
                        n, s = b * KI + 4 * j + q, q % 2
                        pe.wait_ge(S["xT_lo"], b + 1)
                        pe.wait_ge(S[f"w_in_lo{s}"], 2 * (b * (KI // 4) + j) + q // 2 + 1)
                        pe.wait_ge(S["xin_ready"], n - 1 if s else n)
                        for half in range(2):
                            out = (bank4, bank5, bank6, bank7)[2 * s + half]
                            for k in range(KD):
                                mm = three(out[:, :], w_in_h[s][:, 2 * half + k, :], w_in_l[s][:, 2 * half + k, :],
                                           xTh[:, k, :], xTl[:, k, :], k == 0, k == KD - 1)
                        mm.then_inc(S[f"inproj{q}"], 1)
                g0 = b * PAIRS
                pe.wait_ge(S["o_out"], b)
                project(g0, "b", range(KI), b)
                pe.wait_ge(S["const_lo"], 1)
                for k in range(KI):
                    mm = three(bank6[0:DTC, :], dt_h[:, k, :], dt_l[:, k, :], xc_h[:, k, :], xc_l[:, k, :],
                               k == 0, k == KI - 1)
                mm.then_inc(S["dtT_mm"], 1)
                pe.wait_ge(S["dtT_ready"], b + 1)
                for c in range(CH):
                    mm = pe.matmul(bank7[:, c * DTC:(c + 1) * DTC], dtT[0:DTC, c * P:(c + 1) * P],
                                   ident[0:DTC, 0:DTC], start=True, stop=True)
                mm.then_inc(S["gate_mm"], 1)
                scan(b, 0, True, False)
                with pe.Fori(1, PAIRS - 1) as i:
                    scan(b, i, False, False)
                scan(b, PAIRS - 1, False, True)
                turn_y(g0 + PAIRS)
                pe.wait_ge(S["zy_ready"], g0 + PAIRS)
                out_project([KI - 1]).then_inc(S["o_mm"], 1)

        @block.scalar
        def _(act):
            def split(g, m):
                act.wait_ge(S["w_ld"], 32 * g + (16 if m == "b" else 32))
                act.wait_ge(S[m + "_proj"], g)
                act.activation(flat(w_h[m]), flat(w), ACT.Copy).then_inc(S[m + "_hi"], 1)

            def evacuate(g, i, n, m, dst):
                act.wait_ge(S[m + "_proj"], g + 1)
                act.activation(dst[:, :], proj[m][:, :], ACT.Identity, bias=bc_b[:, bass.ds(i, 1), n]
                               ).then_inc(S[m + "_out"], 1)

            def scan(b, i, last):
                g = b * PAIRS + i
                act.wait_ge(S["bt_mm"], g + 1)
                act.activation(sq_b, bank5[:, :], ACT.Square).then_inc(S["bsq_ready"], 1)
                if not last:
                    split(g + 1, "b")
                act.wait_ge(S["tanh_in"], g + 1)
                act.activation(e2[:, :], u[:, :], ACT.Exp).then_inc(S["tanh_out"], 1)
                act.wait_ge(S["alpha_ready"], g + 1)
                act.activation(lna[:, :], alpha[:, :], ACT.Ln).then_inc(S["lna_ready"], 1)
                evacuate(g, i, 1, "c", cT)
                act.wait_ge(S["cum_mm"], g + 1)
                act.activation(ecum[:, :], bank6[:, 0:3 * HC], ACT.Exp).then_inc(S["cum_out"], 1)
                act.wait_ge(S["seg_mm"], g + 1)
                act.activation(dec[:, :, :], seg[:, :, :], ACT.Exp).then_inc(S["seg_out"], 1)
                act.wait_ge(S["ct_mm"], g + 1)
                act.activation(sq_c, bank4[:, :], ACT.Square).then_inc(S["csq_ready"], 1)
                if not last:
                    split(g + 1, "c")
                    act.wait_ge(S["s_mm"], g + 1)
                    evacuate(g + 1, i + 1, 0, "b", bT)

            act.wait_ge(S["params"], 16 * 7)
            act.preload_act_table_set("natural_log_exp_and_others")
            act.activation(dt_h[:, :, :], dt_w, ACT.Copy)
            act.activation(after_r[:, :], after[:, :], ACT.Copy).then_inc(S["const_hi"], 1)
            act.wait_ge(S["kready"], 1)
            act.activation(kpar[:, 1:3, :], kpar[:, 1:3, :], ACT.Exp, scale=LN2).then_inc(S["a_order"], 1)
            with act.Fori(0, BATCH) as b:
                g0 = b * PAIRS
                act.preload_act_table_set("silu_and_others")
                act.activation(xTh[:, :, :], xT[:, :, bass.ds(b * SEQ, SEQ)], ACT.Copy).then_inc(S["xT_hi"], 1)
                def split_in(j, q):
                    act.wait_ge(S[f"w_in_ld{q % 2}"], 32 * (b * (KI // 4) + j) + 16 * (q // 2) + 16)
                    act.wait_ge(S[f"inproj{(q + 2) % 4}"], b * (KI // 4) + j + (q > 1))
                    act.activation(flat(w_in_h[q % 2]), flat(w_in[q % 2]), ACT.Copy).then_inc(S["w_in_hi"], 1)

                def take(j, q):
                    n, f, s = b * KI + 4 * j + q, 4 * j + q, q % 2
                    act.wait_ge(S[f"inproj{q}"], b * (KI // 4) + j + 1)
                    act.wait_ge(S["conv_done"], n - 1 if s else n)
                    act.wait_ge(S["o_mm"], b)
                    act.activation(xin[s][:, 3:3 + SEQ], (bank4, bank6)[s][:, :], ACT.Identity,
                                   bias=in_b[:, bass.ds(f, 1)])
                    act.activation(zy[:, bass.ds(f, 1), :], (bank5, bank7)[s][:, :].unsqueeze(1), ACT.Silu,
                                   bias=in_b[:, bass.ds(f + KI, 1)]).then_inc(S["xin_ready"], 1)

                def convolved(j, q):
                    n, f, s = b * KI + 4 * j + q, 4 * j + q, q % 2
                    act.wait_ge(S["conv_done"], n + 1)
                    act.activation(acc[s][:, :], acc[s][:, :], ACT.Silu, bias=conv_b[:, bass.ds(f, 1)]
                                   ).then_inc(S["xs_ready"], 1)
                    act.wait_ge(S["xs_ready"], n + 1)
                    act.activation(xc_h[:, bass.ds(f, 1), :], acc[s][:, :].unsqueeze(1), ACT.Copy
                                   ).then_inc(S["xc_hi"], 1)

                split_in(0, 0)
                split_in(0, 1)
                split(g0, "b")
                act.wait_ge(S["const_lo"], 1)
                take(0, 0)
                with act.Fori(0, KI // 4 - 1) as j:
                    for q in range(1, 5):
                        split_in(j + (q + 1) // 4, (q + 1) % 4)
                        take(j + q // 4, q % 4)
                        convolved(j, q - 1)
                j = KI // 4 - 1
                for q in range(1, 4):
                    if q < 3:
                        split_in(j, q + 1)
                    take(j, q)
                    convolved(j, q - 1)
                convolved(j, 3)
                split(g0, "c")
                act.preload_act_table_set("natural_log_exp_and_others")
                evacuate(g0, 0, 0, "b", bT)
                act.wait_ge(S["xc_ready"], (b + 1) * KI)
                act.wait_ge(S["dtT_mm"], b + 1)
                act.activation(dtT[0:DTC, :], bank6[0:DTC, :], ACT.Copy).then_inc(S["dtT_ready"], 1)
                act.wait_ge(S["gate_e"], b + 1)
                act.activation(ge[:, :, :], ge[:, :, :], ACT.Exp, scale=-1.0).then_inc(S["a_order"], 1)
                act.wait_ge(S["a_order"], 2 * b + 2)
                act.activation(ge[:, :, :], ge[:, :, :], ACT.Ln, bias=1.0).then_inc(S["gate_l"], 1)
                act.wait_ge(S["gate_a"], b + 1)
                act.activation(gd[:, :, :], gd[:, :, :], ACT.Exp).then_inc(S["a_order"], 1)
                with act.Fori(0, PAIRS - 1) as i:
                    scan(b, i, False)
                scan(b, PAIRS - 1, True)

        @block.gpsimd
        def _(pool):
            def scan(b, i, last):
                g = b * PAIRS + i
                pool.wait_ge(S["xc_ready"], (b + 1) * KI)
                pool.wait_ge(S["xt_mm"], g)
                pool.tensor_tensor(xst[:, :].unsqueeze(1), xc_h[:, bass.ds(i, 1), :].bitcast(F32),
                                   xc_l[:, bass.ds(i, 1), :].bitcast(F32), ALU.add).then_inc(S["xst_ready"], 1)
                if not last:
                    pool.wait_ge(S["b_hi"], g + 2)
                    pool.tensor_tensor(flat(w_l["b"]), flat(w), flat(w_h["b"]).bitcast(F32), ALU.subtract
                                       ).then_inc(S["b_lo"], 1)
                pool.wait_ge(S["lna_ready"], g + 1)
                pool.wait_ge(S["seg_mm"], g)
                pool.tensor_tensor(ul_h[:, :, :], upto[:, :].unsqueeze(1).to_broadcast([P, HC, P]),
                                   lna[:, :].unsqueeze(2).to_broadcast([P, HC, P]), ALU.mult
                                   ).then_inc(S["ul_h_ready"], 1)
                pool.wait_ge(S["seg_out"], g + 1)
                pool.tensor_tensor(dec[:, :, :], dec[:, :, :], upto[:, :].unsqueeze(1).to_broadcast([P, HC, P]),
                                   ALU.mult).then_inc(S["dec_ready"], 1)

            with pool.Fori(0, BATCH) as b:
                def split_in(j, q):
                    pool.wait_ge(S["w_in_hi"], b * KI + 4 * j + q + 1)
                    s = q % 2
                    pool.tensor_tensor(flat(w_in_l[s]), flat(w_in[s]), flat(w_in_h[s]).bitcast(F32), ALU.subtract
                                       ).then_inc(S[f"w_in_lo{s}"], 1)

                def split_x(j, q):
                    f = bass.ds(4 * j + q, 1)
                    pool.wait_ge(S["xc_hi"], b * KI + 4 * j + q + 1)
                    pool.tensor_tensor(xc_l[:, f, :], acc[q % 2][:, :].unsqueeze(1), xc_h[:, f, :].bitcast(F32),
                                       ALU.subtract).then_inc(S["xc_ready"], 1)

                row_cols = bass.ds(b * SEQ, SEQ)
                pool.wait_ge(S["xT_hi"], b + 1)
                pool.tensor_tensor(xTl[:, :, :], xT[:, :, row_cols], xTh[:, :, :].bitcast(F32), ALU.subtract
                                   ).then_inc(S["xT_lo"], 1)
                split_in(0, 0)
                split_in(0, 1)
                with pool.Fori(0, KI // 4 - 1) as j:
                    for q in range(1, 5):
                        split_in(j + (q + 1) // 4, (q + 1) % 4)
                        split_x(j, q - 1)
                j = KI // 4 - 1
                for q in range(1, 4):
                    if q < 3:
                        split_in(j, q + 1)
                    split_x(j, q - 1)
                split_x(j, 3)
                with pool.Fori(0, PAIRS - 1) as i:
                    scan(b, i, False)
                scan(b, PAIRS - 1, True)

        @block.vector
        def _(ve):
            link = Chain(ve, S["order"])
            wide = lambda t, c: t.rearrange("p (h c) -> p c h", h=2)[:, c, :].unsqueeze(3).to_broadcast(
                [P, c.stop - c.start, 2, DH])
            four = lambda t: t.rearrange("p (c h d) -> p c h d", h=2, d=DH)
            by_head = lambda t: t.rearrange("p (h c) -> p h c", h=2)
            squares = lambda t: t.rearrange("p (c h d) -> p h c d", c=CH, h=2)

            def split(g, m):
                ve.wait_ge(S[m + "_hi"], g + 1)
                ve.tensor_tensor(flat(w_l[m]), flat(w), flat(w_h[m]).bitcast(F32), ALU.subtract
                                 ).then_inc(S[m + "_lo"], 1)

            def gate_y(g, i):
                ve.wait_ge(S["yt_mm"], g)
                ve.tensor_tensor(zy[:, bass.ds(i - 1, 1), :], bank7[:, :].unsqueeze(1), zy[:, bass.ds(i - 1, 1), :],
                                 ALU.mult).then_inc(S["zy_ready"], 1)

            def scan(b, i, first, last):
                g = b * PAIRS + i
                heads = bass.ds(2 * i, 2)
                link.restart()
                ve.wait_ge(S["bsq_ready"], g + 1)
                link(ve.tensor_reduce(by_head(u[:, :]), squares(sq_b), AX_X, ALU.add))
                link(ve.tensor_scalar(nb[:, :], u[:, :], 1e-24, None, ALU.max))
                rsqrt(ve, link, rb[:, :], nb[:, :], nt[:, :])
                link(ve.tensor_tensor(u[:, :], u[:, :], rb[:, :], ALU.mult))
                link(ve.tensor_tensor(u[:, :], u[:, :], rb[:, :], ALU.mult))
                link(ve.tensor_tensor(by_head(u[:, :]), by_head(u[:, :]), gain[:, heads, :], ALU.mult))
                ve.tensor_scalar(u[:, :], u[:, :], 60.0, None, ALU.min).then_inc(S["tanh_in"], 1)
                ve.wait_ge(S["tanh_out"], g + 1)
                link(ve.tensor_scalar(e2[:, :], e2[:, :], 1.0, None, ALU.add))
                link(ve.reciprocal(e2[:, :], e2[:, :]))
                link(ve.tensor_scalar(e2[:, :], e2[:, :], -2.0, 1.0, ALU.mult, ALU.add))
                link(ve.scalar_tensor_tensor(by_head(e2[:, :]), by_head(e2[:, :]), 0.0, omab[:, heads, :],
                                             ALU.max, ALU.mult))
                link(ve.tensor_tensor(by_head(e2[:, :]), by_head(e2[:, :]), ab[:, heads, :], ALU.add))
                ve.tensor_scalar(alpha[:, :], e2[:, :], 0.01, 0.999, ALU.max, ALU.min).then_inc(S["alpha_ready"], 1)
                ve.wait_ge(S["alpha_ready"], g + 1)
                link(ve.tensor_scalar(wj[:, :], alpha[:, :], -1.0, 1.0, ALU.mult, ALU.add))
                link(ve.tensor_tensor(wj[:, :], wj[:, :], rb[:, :], ALU.mult))
                ve.wait_ge(S["lna_ready"], g + 1)
                link(ve.tensor_copy(lna_h[:, :], lna[:, :]))
                link(ve.tensor_tensor(lna_l[:, :], lna[:, :], lna_h[:, :].bitcast(F32), ALU.subtract))
                ve.wait_ge(S["seg_mm"], g)
                ve.tensor_tensor(ul_l[:, :, :], upto[:, :].unsqueeze(1).to_broadcast([P, HC, P]),
                                 lna_l[:, :].unsqueeze(2).to_broadcast([P, HC, P]), ALU.mult
                                 ).then_inc(S["ul_l_ready"], 1)
                ve.wait_ge(S["xt_mm"], g + 1)
                ve.tensor_tensor(four(flat(xw)), four(bank4[:, :]), wide(wj[:, :], slice(0, CH)), ALU.mult
                                 ).then_inc(S["xw_ready"], 1)
                if not first:
                    gate_y(g, i)
                ve.wait_ge(S["cum_out"], g + 1)
                ve.tensor_tensor(four(flat(bf)), four(bank5[:, 0:3 * P]), wide(ecum[:, 0:HC], slice(0, CH - 1)),
                                 ALU.mult).then_inc(S["bf_ready"], 1)
                ve.wait_ge(S["csq_ready"], g + 1)
                link(ve.tensor_reduce(by_head(ncn[:, :]), squares(sq_c), AX_X, ALU.add))
                link(ve.tensor_scalar(ncn[:, :], ncn[:, :], 1e-24, None, ALU.max))
                rsqrt(ve, link, rc[:, :], ncn[:, :], nt[:, :])
                link(ve.tensor_tensor(ecr[:, :], rc[:, :], ecum[:, 2 * HC:], ALU.mult))
                ve.wait_ge(S["dec_ready"], g + 1)
                ve.wait_ge(S["s_mm"], g + 1)
                ve.tensor_tensor(prob[:, :, :], seg[:, :, :], dec[:, :, :], ALU.mult).then_inc(S["prob_ready"], 1)
                ve.wait_ge(S["ds_mm"], g + 1)
                for c in range(CH - 1):
                    for h in range(2):
                        r = slice(h * DH, (h + 1) * DH)
                        new = bank5[r, c * P + h * DH:c * P + (h + 1) * DH]
                        if c == 0:
                            ins = ve.tensor_copy(state[r, 0, r], new)
                        else:
                            m = HC + h * CH + c
                            ins = ve.scalar_tensor_tensor(state[r, c, r], state[r, c - 1, r], ecum[r, m:m + 1],
                                                          new, ALU.mult, ALU.add)
                        if c == CH - 2 and h == 1:
                            ins.then_inc(S["state_ready"], 1)
                        elif c < CH - 2:
                            link(ins)
                if not last:
                    split(g + 1, "c")
                ve.wait_ge(S["y_mm"], g + 1)
                link(ve.tensor_tensor(four(ys[:, :]), four(bank7[:, :]), wide(rc[:, :], slice(0, CH)), ALU.mult))
                link(ve.tensor_tensor(four(yi[:, P:]), four(bank6[:, P:]), wide(ecr[:, :], slice(1, CH)), ALU.mult))
                ve.tensor_tensor(ys[:, P:], ys[:, P:], yi[:, P:], ALU.add).then_inc(S["ys_ready"], 1)

            for s in range(2):
                link(ve.memset(xin[s][:, 0:3], 0.0))
            link(ve.memset(state[:, :, :], 0.0))
            ve.wait_ge(S["params"], 16 * 7)
            row = lambda r: par[:, r * NH0:(r + 1) * NH0]
            link(ve.tensor_scalar(kpar[:, 0, :], row(0), -2.3, -0.01, ALU.max, ALU.min))
            link(ve.tensor_scalar(kpar[:, 1, :], row(1), -3.32, -0.015, ALU.max, ALU.min))
            link(ve.tensor_scalar(kpar[:, 3, :], row(3), 1e-6, None, ALU.add))
            link(ve.reciprocal(kpar[:, 3, :], kpar[:, 3, :]))
            ve.tensor_scalar(kpar[:, 2, :], row(2), -2.0, 2.0, ALU.max, ALU.min).then_inc(S["kready"], 1)
            ve.wait_ge(S["a_order"], 1)
            link(ve.tensor_scalar(kpar[:, 1, :], kpar[:, 1, :], -1.0, 1.0, ALU.mult, ALU.add))
            link(ve.tensor_tensor(kpar[:, 2, :], kpar[:, 2, :], kpar[:, 3, :], ALU.mult))
            link(ve.tensor_scalar(kpar[:, 2, :], kpar[:, 2, :], 2.0 / NS, None, ALU.mult))
            for c in range(CH):
                link(ve.tensor_copy(ab[:, :, c], kpar[:, 1, :]))
                link(ve.tensor_scalar(omab[:, :, c], kpar[:, 1, :], -1.0, 1.0, ALU.mult, ALU.add))
            ve.wait_ge(S["const_hi"], 1)
            ve.tensor_tensor(dt_l[:, :, :], dt_w, dt_h[:, :, :].bitcast(F32), ALU.subtract
                             ).then_inc(S["const_lo"], 1)

            with ve.Fori(0, BATCH) as b:
                g0 = b * PAIRS
                split(g0, "b")
                with ve.Fori(0, KI // 2) as i:
                    link.restart()
                    for s in range(2):
                        n = b * (KI // 2) + i
                        f = bass.ds(2 * i + s, 1)
                        ve.wait_ge(S["xin_ready"], 2 * n + s + 1)
                        ve.wait_ge(S["xc_ready"], 2 * n + s - 1 if s else 2 * n)
                        H = SEQ // 2
                        for j in range(4):
                            for h in range(2):
                                out, seen = acc[s][:, h * H:(h + 1) * H], xin[s][:, h * H + j:h * H + j + H]
                                if j == 0:
                                    ins = ve.tensor_scalar(out, seen, conv_w[:, f, 0], None, ALU.mult)
                                else:
                                    ve.wait_ge(S["order"], link.n - (1 if j < 3 or h == 0 else 0))
                                    ins = ve.scalar_tensor_tensor(out, seen, conv_w[:, f, j], out, ALU.mult, ALU.add)
                                if j < 3:
                                    ins.then_inc(S["order"], 1)
                                    link.n += 1
                            if j == 3:
                                ins.then_inc(S["conv_done"], 1)
                split(g0, "c")
                link.restart()
                chunked = bank7[:, 0:CH * DTC].rearrange("p (c q) -> p q c", c=CH)
                ve.wait_ge(S["gate_mm"], b + 1)
                link(ve.tensor_tensor(gd[:, :, :], chunked[:, 0:NH0, :],
                                      row(4).unsqueeze(2).to_broadcast([P, NH0, CH]), ALU.add))
                ve.tensor_copy(gx[:, :, :], chunked[:, NH0:2 * NH0, :]).then_inc(S["gate_d"], 1)
                ve.scalar_tensor_tensor(ge[:, :, :], gd[:, :, :], -1.0, gd[:, :, :], ALU.mult, ALU.max
                                        ).then_inc(S["gate_e"], 1)
                ve.wait_ge(S["gate_l"], b + 1)
                link(ve.scalar_tensor_tensor(gd[:, :, :], gd[:, :, :], 0.0, ge[:, :, :], ALU.max, ALU.add))
                ve.tensor_tensor(gd[:, :, :], gd[:, :, :], kpar[:, 0, :].unsqueeze(2).to_broadcast([P, NH0, CH]),
                                 ALU.mult).then_inc(S["gate_a"], 1)
                ve.wait_ge(S["a_order"], 2 * b + 3)
                ve.wait_ge(S["gate_d"], b + 1)
                link(ve.tensor_scalar(gd[:, :, :], gd[:, :, :], -1.0, 1.0, ALU.mult, ALU.add))
                link(ve.tensor_tensor(gx[:, :, :], gx[:, :, :], gd[:, :, :], ALU.mult))
                link(ve.tensor_tensor(gx[:, :, :], gx[:, :, :], gx[:, :, :], ALU.mult))
                link(ve.tensor_tensor(gain[:, :, :], gx[:, :, :],
                                      kpar[:, 2, :].unsqueeze(2).to_broadcast([P, NH0, CH]), ALU.mult))
                scan(b, 0, True, False)
                with ve.Fori(1, PAIRS - 1) as i:
                    scan(b, i, False, False)
                scan(b, PAIRS - 1, False, True)
                gate_y(g0 + PAIRS, PAIRS)
                ve.wait_ge(S["o_mm"], b + 1)
                for h in range(2):
                    xs = x[:, bass.ds(b * CH + 2 * h, 2), :]
                    ins = ve.scalar_tensor_tensor(xs, proj["bc"[h]][:, :].rearrange("p (c d) -> p c d", c=2),
                                                  par[:, 5 * NH0:], xs, ALU.mult, ALU.add)
                ins.then_inc(S["o_out"], 1)
                ve.wait_ge(S["o_out"], b + 1)


E0, I0 = 8, 512
KH = I0 // P


def gate0(nc, xT, comb, A):
    ctx, sb, ps, sem = scope(nc, "gate0")
    with ctx:
        w = sb("w", [P, KD, E0])
        p = sb("p", [P, NT, E0])
        one = sb("one", [P, NT])
        top = sb("top", [P, NT, 8])
        idx = sb("idx", [P, NT, 8], mybir.dt.uint32)
        idf = sb("idf", [P, NT, 8])
        col = sb("col", [P, E0])
        hit = sb("hit", [P, NT, E0])
        hit2 = sb("hit2", [P, NT, E0])
        logits = ps("logits", [P, NT, E0])
        S = {n: sem(n) for n in ("w", "mm", "order", "shifted", "exp", "col")}
        block = ctx.enter_context(nc.Block())

        @block.sync
        def _(sp):
            sp.dma_start(w[:, :, :], A["gate0_w"]).then_inc(S["w"], 16)

        @block.gpsimd
        def _(pool):
            pool.iota(col[:, :], pattern=[[1, E0]], base=0, channel_multiplier=0,
                      allow_small_or_imprecise_dtypes=True).then_inc(S["col"], 1)

        @block.tensor
        def _(pe):
            pe.wait_ge(S["w"], 16)
            for t in range(NT):
                for k in range(KD):
                    mm = pe.matmul(logits[:, t, :], xT[:, k, t * P:(t + 1) * P], w[:, k, :],
                                   start=(k == 0), stop=(k == KD - 1))
            mm.then_inc(S["mm"], 1)

        @block.scalar
        def _(act):
            act.wait_ge(S["shifted"], 1)
            act.activation(p[:, :, :], p[:, :, :], ACT.Exp).then_inc(S["exp"], 1)

        @block.vector
        def _(ve):
            link = Chain(ve, S["order"])
            wide = lambda t, n: t.unsqueeze(2).to_broadcast([P, NT, n])
            ve.wait_ge(S["mm"], 1)
            link(ve.tensor_reduce(one[:, :], logits[:, :, :], AX_X, ALU.max))
            ve.tensor_tensor(p[:, :, :], logits[:, :, :], wide(one[:, :], E0), ALU.subtract).then_inc(S["shifted"], 1)
            ve.wait_ge(S["exp"], 1)
            link(ve.tensor_reduce(one[:, :], p[:, :, :], AX_X, ALU.add))
            link(ve.reciprocal(one[:, :], one[:, :]))
            link(ve.tensor_tensor(p[:, :, :], p[:, :, :], wide(one[:, :], E0), ALU.mult))
            for t in range(NT):
                ins = ve.max(top[:, t, :], p[:, t, :])
            link(ins)
            for t in range(NT):
                ins = ve.max_index(idx[:, t, :], top[:, t, :], p[:, t, :])
            link(ins)
            link(ve.tensor_tensor(one[:, :], top[:, :, 0], top[:, :, 1], ALU.add))
            link(ve.reciprocal(one[:, :], one[:, :]))
            link(ve.tensor_copy(idf[:, :, :], idx[:, :, :]))
            ve.wait_ge(S["col"], 1)
            cols = col[:, :].unsqueeze(1).to_broadcast([P, NT, E0])
            for n, h in enumerate((hit, hit2)):
                link(ve.tensor_tensor(h[:, :, :], cols, wide(idf[:, :, n], E0), ALU.is_equal))
            link(ve.tensor_tensor(hit[:, :, :], hit[:, :, :], hit2[:, :, :], ALU.add))
            link(ve.tensor_tensor(hit[:, :, :], hit[:, :, :], p[:, :, :], ALU.mult))
            link(ve.memset(comb[:, :, E0:], 1.0))
            link(ve.tensor_tensor(comb[:, :, 0:E0], hit[:, :, :], wide(one[:, :], E0), ALU.mult))


def ffn(nc, tag, x, xT, up_w, down_w, n_exp, comb):
    ctx, sb, ps, sem = scope(nc, tag)
    G = TOK // SEQ
    loops = n_exp // 2
    with ctx:
        wu = [sb(f"wu{s}", [P, KD, 2 * I0]) for s in range(2)]
        wd = [sb(f"wd{s}", [P, KH, D]) for s in range(2)]
        sg = [sb(f"sg{s}", [P, SEQ]) for s in range(2)]
        hT = [sb(f"hT{s}", [P, KH, SEQ]) for s in range(2)]
        gp = [ps(f"g{s}", [P, SEQ]) for s in range(2)]
        up = [ps(f"u{s}", [P, SEQ]) for s in range(2)]
        yp = [ps(f"y{s}", [P, CH, D]) for s in range(2)]
        S = {n: sem(n) for n in ("wu0", "wu1", "wd0", "wd1", "gu_mm", "sg_ready", "h_ready0", "h_ready1",
                                 "y_mm0", "y_mm1", "added0", "added1")}
        block = ctx.enter_context(nc.Block())

        @block.sync
        def _(sp):
            def load(e, s, first):
                if not first:
                    sp.wait_ge(S["gu_mm"], 16 * e - 16)
                sp.dma_start(wu[s][:, :, :], up_w[bass.ds(e, 1)].rearrange("o p k m -> p (o k) m")
                             ).then_inc(S[f"wu{s}"], 16)
                if not first:
                    sp.wait_ge(S["y_mm1"], 2 * e - 2)
                sp.dma_start(wd[s][:, :, :], down_w[bass.ds(e, 1)].rearrange("o p k m -> p (o k) m")
                             ).then_inc(S[f"wd{s}"], 16)

            load(0, 0, True)
            if loops:
                load(1, 1, True)
                with sp.Fori(1, loops) as i:
                    load(2 * i, 0, False)
                    load(2 * i + 1, 1, False)
                load(n_exp - 1, 0, False)

        @block.tensor
        def _(pe):
            def project_up(i, s, j):
                half = 4 * i + 2 * s + j // 2
                q2 = 2 * (8 * i + 4 * s + j)
                if j == 0:
                    pe.wait_ge(S[f"wu{s}"], 16 * i + 16)
                for m in range(KH):
                    pe.wait_ge(S[f"h_ready{m % 2}"], q2 + m // 2)
                    for out, o in ((gp[m % 2], 0), (up[m % 2], I0)):
                        for k in range(KD):
                            mm = pe.matmul(out[:, :], wu[s][:, k, o + m * P:o + (m + 1) * P],
                                           xT[:, k, j * SEQ:(j + 1) * SEQ], start=(k == 0), stop=(k == KD - 1))
                    mm.then_inc(S["gu_mm"], 1)

            def project_down(i, s, j):
                half = 4 * i + 2 * s + j // 2
                q2 = 2 * (8 * i + 4 * s + j)
                if j == 0:
                    pe.wait_ge(S[f"wd{s}"], 16 * i + 16)
                pe.wait_ge(S["h_ready0"], q2 + 2)
                pe.wait_ge(S["h_ready1"], q2 + 2)
                pe.wait_ge(S[f"added{j % 2}"], half)
                for c in range(CH):
                    for k in range(KH):
                        mm = pe.matmul(yp[j % 2][:, c, :], hT[j % 2][:, k, c * P:(c + 1) * P], wd[s][:, k, :],
                                       start=(k == 0), stop=(k == KH - 1))
                mm.then_inc(S[f"y_mm{j % 2}"], 1)

            project_up(0, 0, 0)
            if loops:
                with pe.Fori(0, loops) as i:
                    for n in range(8):
                        project_up(i + (n == 7), (n + 1) // 4 % 2, (n + 1) % 4)
                        project_down(i, n // 4, n % 4)
            for j in range(G):
                if j < G - 1:
                    project_up(loops, 0, j + 1)
                project_down(loops, 0, j)

        @block.scalar
        def _(act):
            def step(i, s, j):
                q = 8 * i + 4 * s + j
                for m in range(KH):
                    act.wait_ge(S["gu_mm"], 4 * q + m + 1)
                    act.wait_ge(S[f"h_ready{m % 2}"], 2 * q + m // 2)
                    act.activation(sg[m % 2][:, :], gp[m % 2][:, :], ACT.Silu).then_inc(S["sg_ready"], 1)

            act.preload_act_table_set("silu_and_others")
            if loops:
                with act.Fori(0, loops) as i:
                    for n in range(8):
                        step(i, n // 4, n % 4)
            for j in range(G):
                step(loops, 0, j)

        @block.vector
        def _(ve):
            def hidden(i, s, j):
                q = 8 * i + 4 * s + j
                ve.wait_ge(S[f"y_mm{j % 2}"], 4 * i + 2 * s + j // 2)
                for m in range(KH):
                    ve.wait_ge(S["sg_ready"], 4 * q + m + 1)
                    ve.tensor_tensor(hT[j % 2][:, m, :], sg[m % 2][:, :], up[m % 2][:, :], ALU.mult
                                     ).then_inc(S[f"h_ready{m % 2}"], 1)

            def add(i, s, j):
                ve.wait_ge(S[f"y_mm{j % 2}"], 4 * i + 2 * s + j // 2 + 1)
                for c in range(CH):
                    t = j * CH + c
                    if comb is None:
                        ins = ve.tensor_tensor(x[:, t, :], yp[j % 2][:, c, :], x[:, t, :], ALU.add)
                    else:
                        ins = ve.scalar_tensor_tensor(x[:, t, :], yp[j % 2][:, c, :],
                                                      comb[:, t, bass.ds(2 * i + s, 1)], x[:, t, :],
                                                      ALU.mult, ALU.add)
                ins.then_inc(S[f"added{j % 2}"], 1)

            hidden(0, 0, 0)
            if loops:
                with ve.Fori(0, loops) as i:
                    for n in range(8):
                        hidden(i + (n == 7), (n + 1) // 4 % 2, (n + 1) % 4)
                        add(i, n // 4, n % 4)
            for j in range(G):
                if j < G - 1:
                    hidden(loops, 0, j + 1)
                add(loops, 0, j)


NH1, DH1 = 16, 16
QG = 4
MASKED = 1e30


def attention(nc, x, xT, ident, A):
    ctx, sb, ps, sem = scope(nc, "attn")
    STEPS = NH1 * CH
    with ctx:
        wqk = sb("wqk", [P, KD, 2 * QG, P])
        wv = sb("wv", [P, KD, D])
        wo = sb("wo", [P, KD, D])
        far = sb("far", [P, SEQ])
        bias = sb("bias", [P, NH1, SEQ])
        xb = sb("xb", [P, KD, SEQ])
        qT = sb("qT", [P, QG, SEQ])
        kT = sb("kT", [P, QG, SEQ])
        v = sb("v", [P, CH, D])
        T = [sb(f"T{i}", [P, SEQ]) for i in range(3)]
        E = [sb(f"E{i}", [P, SEQ]) for i in range(2)]
        ET = [sb(f"ET{i}", [P, SEQ]) for i in range(2)]
        low = sb("low", [P, STEPS])
        rows = sb("rows", [P, QG, CH, 4])
        y = sb("y", [P, CH, D])
        yT = sb("yT", [P, KD, SEQ])
        sc = [ps(f"sc{i}", [P, SEQ]) for i in range(3)]
        tp = [ps(f"tp{i}", [P, SEQ]) for i in range(2)]
        yp = ps("yp", [P, CH, P])
        pj = [ps(f"pj{i}", [P, SEQ]) for i in range(2)]
        names = ("w", "far", "bias", "xb", "pj_mm", "pj_out", "sc_mm", "T_ready", "E_ready", "tp_mm", "ET_ready",
                 "y_mm", "y_out", "yt_mm", "yt_out", "o_mm", "added", "order")
        S = {n: sem(n) for n in names}
        block = ctx.enter_context(nc.Block())

        def step(u):
            g, r, t = u // 16, u % 16 // CH, u % CH
            return g, r, 4 * g + r, t, (t + 1) * P

        NPJ = 2 * QG + CH

        @block.sync
        def _(sp):
            sp.dma_start(wqk[:, :, :, :], A["qk_w"]).then_inc(S["w"], 16)
            sp.dma_start(wv[:, :, :], A["v_w"]).then_inc(S["w"], 16)
            sp.dma_start(wo[:, :, :], A["o_w"]).then_inc(S["w"], 16)

        @block.gpsimd
        def _(pool):
            pool.iota(far[:, :], pattern=[[-1, SEQ]], base=(CH - 1) * P, channel_multiplier=1,
                      allow_small_or_imprecise_dtypes=True).then_inc(S["far"], 1)
            pool.wait_ge(S["far"], 1)
            pool.affine_select(out=far[:, :], in_=far[:, :], compare_op=ALU.is_ge, fill=2 * MASKED * 256.0,
                               base=(CH - 1) * P, pattern=[[-1, SEQ]], channel_multiplier=1).then_inc(S["far"], 1)

        @block.tensor
        def _(pe):
            pe.wait_ge(S["w"], 48)
            with pe.Fori(0, BATCH) as b:
                u0 = b * STEPS

                def project(n):
                    out = pj[n % 2]
                    pe.wait_ge(S[f"pj_out"], b * NPJ + n - 1 if n > 1 else b * NPJ)
                    if n < 2 * QG:
                        for k in range(KD):
                            mm = pe.matmul(out[:, :], wqk[:, k, n, :], xb[:, k, :], start=(k == 0), stop=(k == KD - 1))
                    else:
                        c = n - 2 * QG
                        for k in range(KD):
                            mm = pe.matmul(out[:, 0:D], xb[:, k, c * P:(c + 1) * P], wv[:, k, :],
                                           start=(k == 0), stop=(k == KD - 1))
                    mm.then_inc(S["pj_mm"], 1)

                def scores(u):
                    g, r, h, t, n = step(u)
                    if u > 2:
                        pe.wait_ge(S["T_ready"], u0 + u - 2)
                    rows_ = slice(32 * r, 32 * r + DH1)
                    pe.matmul(sc[u % 3][:, 0:n], qT[rows_, g, t * P:(t + 1) * P], kT[rows_, g, 0:n],
                              start=True, stop=True).then_inc(S["sc_mm"], 1)

                def turn(u):
                    g, r, h, t, n = step(u)
                    pe.wait_ge(S["E_ready"], u0 + u + 1)
                    if u > 1:
                        pe.wait_ge(S["ET_ready"], u0 + u - 1)
                    for j in range(t + 1):
                        mm = pe.transpose(tp[u % 2][:, j * P:(j + 1) * P], E[u % 2][:, j * P:(j + 1) * P], ident[:, :])
                    mm.then_inc(S["tp_mm"], 1)

                def mix(u):
                    g, r, h, t, n = step(u)
                    pe.wait_ge(S["ET_ready"], u0 + u + 1)
                    if u % 16 == 0 and u:
                        pe.wait_ge(S["y_out"], b * QG + g)
                    for j in range(t + 1):
                        mm = pe.matmul(yp[:, t, r * DH1:(r + 1) * DH1], ET[u % 2][:, j * P:(j + 1) * P],
                                       v[:, j, h * DH1:(h + 1) * DH1], start=(j == 0), stop=(j == t))
                    mm.then_inc(S["y_mm"], 1)

                pe.wait_ge(S["xb"], b + 1)
                for n in range(NPJ):
                    project(n)
                pe.wait_ge(S["pj_out"], (b + 1) * NPJ)
                for u in range(3):
                    scores(u)
                for u in range(STEPS):
                    if u + 3 < STEPS:
                        scores(u + 3)
                    turn(u)
                    if u:
                        mix(u - 1)
                mix(STEPS - 1)
                pe.wait_ge(S["y_out"], (b + 1) * QG)
                for k in range(KD):
                    for c in range(CH):
                        mm = pe.transpose(tp[k][:, c * P:(c + 1) * P], y[:, c, k * P:(k + 1) * P], ident[:, :])
                mm.then_inc(S["yt_mm"], 1)
                pe.wait_ge(S["yt_out"], b + 1)
                for c in range(CH):
                    out = pj[c // 2][:, (c % 2) * D:(c % 2 + 1) * D]
                    for k in range(KD):
                        mm = pe.matmul(out, yT[:, k, c * P:(c + 1) * P], wo[:, k, :], start=(k == 0), stop=(k == KD - 1))
                mm.then_inc(S["o_mm"], 1)

        @block.scalar
        def _(act):
            act.preload_act_table_set("natural_log_exp_and_others")
            act.wait_ge(S["w"], 48)
            with act.Fori(0, BATCH) as b:
                u0 = b * STEPS
                act.wait_ge(S["o_mm"], b)
                for n in range(NPJ):
                    act.wait_ge(S["pj_mm"], b * NPJ + n + 1)
                    if n < QG:
                        ins = act.activation(qT[:, n, :], pj[n % 2][:, :], ACT.Copy, scale=-float(DH1) ** -0.5)
                    elif n < 2 * QG:
                        ins = act.activation(kT[:, n - QG, :], pj[n % 2][:, :], ACT.Copy)
                    else:
                        ins = act.activation(v[:, n - 2 * QG, :], pj[n % 2][:, 0:D], ACT.Copy)
                    ins.then_inc(S["pj_out"], 1)
                for u in range(STEPS):
                    g, r, h, t, n = step(u)
                    act.wait_ge(S["T_ready"], u0 + u + 1)
                    if u > 1:
                        act.wait_ge(S["tp_mm"], u0 + u - 1)
                    if u % 16 == 0 and u:
                        act.wait_ge(S["y_out"], b * QG + g - 1 if g > 1 else b * QG)
                    act.activation(E[u % 2][:, 0:n], T[u % 3][:, 0:n], ACT.Exp, bias=low[:, u:u + 1], scale=-1.0,
                                   accum_out=rows[:, g, t, r:r + 1]).then_inc(S["E_ready"], 1)
                act.wait_ge(S["yt_mm"], b + 1)
                for k in range(KD):
                    last = act.activation(yT[:, k, :], tp[k][:, :], ACT.Copy)
                last.then_inc(S["yt_out"], 1)

        @block.vector
        def _(ve):
            link = Chain(ve, S["order"])
            ve.wait_ge(S["far"], 2)
            for h in range(NH1):
                ins = ve.tensor_scalar(bias[:, h, :], far[:, :], 2.0 ** (-8.0 / (h + 1)), None, ALU.mult)
            link(ins)
            with ve.Fori(0, BATCH) as b:
                link.restart()
                u0 = b * STEPS
                ve.wait_ge(S["pj_mm"], b * NPJ)
                ve.tensor_copy(xb[:, :, :], xT[:, :, bass.ds(b * SEQ, SEQ)]).then_inc(S["xb"], 1)

                def negated(u):
                    g, r, h, t, n = step(u)
                    ve.tensor_tensor_reduce(T[u % 3][:, 0:n], sc[u % 3][:, 0:n], bias[:, h, SEQ - n:], 1.0, 3e38,
                                            ALU.add, ALU.min, low[:, u:u + 1]).then_inc(S["T_ready"], 1)

                def copied(u):
                    g, r, h, t, n = step(u)
                    if u + 2 < STEPS:
                        ve.wait_ge(S["sc_mm"], u0 + u + 3)
                    ve.wait_ge(S["tp_mm"], u0 + u + 1)
                    if u > 1:
                        ve.wait_ge(S["y_mm"], u0 + u - 1)
                    ve.tensor_copy(ET[u % 2][:, 0:n], tp[u % 2][:, 0:n]).then_inc(S["ET_ready"], 1)

                def divided(g):
                    ve.wait_ge(S["y_mm"], u0 + 16 * (g + 1))
                    link(ve.reciprocal(rows[:, g, :, :], rows[:, g, :, :]))
                    ve.tensor_tensor(y[:, :, g * 64:(g + 1) * 64].rearrange("p c (r d) -> p c r d", r=4),
                                     yp[:, :, 0:64].rearrange("p c (r d) -> p c r d", r=4),
                                     rows[:, g, :, :].unsqueeze(3).to_broadcast([P, CH, 4, DH1]), ALU.mult
                                     ).then_inc(S["y_out"], 1)

                ve.wait_ge(S["sc_mm"], u0 + 2)
                link(ve.memset(low[:, 0:2], 0.0))
                negated(0)
                negated(1)
                for u in range(STEPS):
                    copied(u)
                    if u + 2 < STEPS:
                        negated(u + 2)
                    if u % 16 == 0 and u:
                        divided(u // 16 - 1)
                divided(QG - 1)
                ve.wait_ge(S["o_mm"], b + 1)
                for c in range(2):
                    xs = x[:, bass.ds(b * CH + 2 * c, 2), :]
                    ins = ve.tensor_tensor(xs, pj[c][:, :].rearrange("p (c d) -> p c d", c=2), xs, ALU.add)
                ins.then_inc(S["added"], 1)


E1, F1, TOP, CAP = 64, 64, 4, 32
SLOTS = E1 * CAP
EG = P // CAP
NG = E1 // EG


def route1(nc, xT, xn, slots, reads, wk, before, ones, xg, A):
    ctx, sb, ps, sem = scope(nc, "route")
    U32 = mybir.dt.uint32
    with ctx:
        w = sb("w", [P, KD, E1])
        rb = sb("rb", [P, E1])
        lg = sb("lg", [P, NT, E1])
        score = sb("score", [P, NT, E1])
        one = sb("one", [P, NT])
        top = sb("top", [P, NT, 8])
        idx = sb("idx", [P, NT, 8], U32)
        idf = sb("idf", [P, NT, 8])
        col = sb("col", [P, E1])
        first = sb("first", [P, E1])
        hit = [sb(f"hit{k}", [P, NT, E1]) for k in range(TOP)]
        mask = sb("mask", [P, NT, E1])
        prior = sb("prior", [P, NT, E1])
        place = sb("place", [P, NT, E1])
        tmp = sb("tmp", [P, NT, E1])
        sf = sb("sf", [P, NT, TOP])
        zero = sb("zero", [P, 4 * D])
        logits = ps("logits", [P, NT, E1])
        rank = ps("rank", [P, NT, E1])
        S = {n: sem(n) for n in ("w", "mm", "order", "shifted", "exp", "col", "zero", "filled", "mask", "rank",
                                 "slots", "sent")}
        block = ctx.enter_context(nc.Block())

        @block.sync
        def _(sp):
            sp.dma_start(w[:, :, :], A["router_w"]).then_inc(S["w"], 16)
            sp.dma_start(rb[:, :], A["router_b"].to_broadcast([P, E1])).then_inc(S["w"], 16)
            sp.wait_ge(S["zero"], 1)
            for g in range(4):
                sp.dma_start(xg[512 * g:512 * g + 512, :].rearrange("(p c) d -> p (c d)", p=P), zero[:, :]
                             ).then_inc(S["filled"], 16)

        @block.gpsimd
        def _(pool):
            pool.memset(zero[:, :], 0.0).then_inc(S["zero"], 1)
            pool.iota(col[:, :], pattern=[[1, E1]], base=0, channel_multiplier=0,
                      allow_small_or_imprecise_dtypes=True).then_inc(S["col"], 1)
            pool.iota(first[:, :], pattern=[[CAP, E1]], base=0, channel_multiplier=0,
                      allow_small_or_imprecise_dtypes=True).then_inc(S["col"], 1)
            pool.wait_ge(S["filled"], 64)
            pool.wait_ge(S["slots"], 1)
            for t in range(NT):
                for k in range(TOP):
                    pool.indirect_dma_start(xg[:, :], bass.IndirectOffsetOnAxis(slots[:, t, k:k + 1], 0), xn[:, t, :], None,
                                            bounds_check=SLOTS - 1, oob_is_err=False).then_inc(S["sent"], 16)
            pool.wait_ge(S["sent"], 16 * NT * TOP)

        @block.tensor
        def _(pe):
            pe.wait_ge(S["w"], 32)
            for t in range(NT):
                for k in range(KD):
                    mm = pe.matmul(logits[:, t, :], xT[:, k, t * P:(t + 1) * P], w[:, k, :],
                                   start=(k == 0), stop=(k == KD - 1))
            mm.then_inc(S["mm"], 1)
            pe.wait_ge(S["mask"], NT - 1)
            for t in range(NT):
                pe.matmul(rank[:, t, :], before[:, :], mask[:, t, :], start=True, stop=False)
                mm = pe.matmul(rank[:, t, :], ones[:, :], prior[:, t, :], start=False, stop=True)
            mm.then_inc(S["rank"], 1)

        @block.scalar
        def _(act):
            act.wait_ge(S["shifted"], 1)
            act.activation(score[:, :, :], score[:, :, :], ACT.Exp).then_inc(S["exp"], 1)

        @block.vector
        def _(ve):
            link = Chain(ve, S["order"])
            wide = lambda t: t.unsqueeze(2).to_broadcast([P, NT, E1])
            tall = lambda t: t[:, :].unsqueeze(1).to_broadcast([P, NT, E1])
            ve.wait_ge(S["mm"], 1)
            ve.wait_ge(S["w"], 32)
            link(ve.tensor_reduce(one[:, :], logits[:, :, :], AX_X, ALU.max))
            ve.tensor_tensor(score[:, :, :], logits[:, :, :], wide(one[:, :]), ALU.subtract).then_inc(S["shifted"], 1)
            link(ve.tensor_tensor(lg[:, :, :], logits[:, :, :], tall(rb), ALU.add))
            for t in range(NT):
                ins = ve.max(top[:, t, :], lg[:, t, :])
            link(ins)
            for t in range(NT):
                ins = ve.max_index(idx[:, t, :], top[:, t, :], lg[:, t, :])
            link(ins)
            link(ve.tensor_copy(idf[:, :, :], idx[:, :, :]))
            ve.wait_ge(S["col"], 2)
            for k in range(TOP):
                link(ve.tensor_tensor(hit[k][:, :, :], tall(col), wide(idf[:, :, k]), ALU.is_equal))
            link(ve.tensor_tensor(mask[:, :, :], hit[0][:, :, :], hit[1][:, :, :], ALU.add))
            link(ve.tensor_tensor(mask[:, :, :], mask[:, :, :], hit[2][:, :, :], ALU.add))
            link(ve.tensor_tensor(mask[:, :, :], mask[:, :, :], hit[3][:, :, :], ALU.add))
            link(ve.memset(prior[:, 0, :], 0.0))
            for t in range(1, NT):
                ve.tensor_tensor(prior[:, t, :], prior[:, t - 1, :], mask[:, t - 1, :], ALU.add
                                 ).then_inc(S["mask"], 1)
                ve.wait_ge(S["mask"], t)
            ve.wait_ge(S["exp"], 1)
            link(ve.tensor_reduce(one[:, :], score[:, :, :], AX_X, ALU.add))
            link(ve.reciprocal(one[:, :], one[:, :]))
            link(ve.tensor_tensor(score[:, :, :], score[:, :, :], wide(one[:, :]), ALU.mult))
            for k in range(TOP):
                link(ve.tensor_tensor(tmp[:, :, :], hit[k][:, :, :], score[:, :, :], ALU.mult))
                link(ve.tensor_reduce(wk[:, :, k], tmp[:, :, :], AX_X, ALU.add))
            link(ve.tensor_reduce(one[:, :], wk[:, :, :], AX_X, ALU.add))
            link(ve.reciprocal(one[:, :], one[:, :]))
            link(ve.tensor_tensor(wk[:, :, :], wk[:, :, :], one[:, :].unsqueeze(2).to_broadcast([P, NT, TOP]), ALU.mult))
            ve.wait_ge(S["rank"], 1)
            link(ve.tensor_scalar(tmp[:, :, :], rank[:, :, :], float(CAP), float(4 * SLOTS), ALU.is_ge, ALU.mult))
            link(ve.tensor_tensor(place[:, :, :], rank[:, :, :], tmp[:, :, :], ALU.add))
            link(ve.tensor_tensor(place[:, :, :], place[:, :, :], tall(first), ALU.add))
            for k in range(TOP):
                link(ve.tensor_tensor(tmp[:, :, :], hit[k][:, :, :], place[:, :, :], ALU.mult))
                link(ve.tensor_reduce(sf[:, :, k], tmp[:, :, :], AX_X, ALU.add))
            ve.tensor_copy(slots[:, :, :], sf[:, :, :]).then_inc(S["slots"], 1)
            kept = tmp[:, :, 0:TOP]
            link(ve.tensor_scalar(kept, sf[:, :, :], float(SLOTS), None, ALU.is_lt))
            link(ve.tensor_tensor(wk[:, :, :], wk[:, :, :], kept, ALU.mult))
            link(ve.tensor_scalar(sf[:, :, :], sf[:, :, :], float(SLOTS - 1), None, ALU.min))
            link(ve.tensor_copy(reads[:, :, :], sf[:, :, :]))


def experts1(nc, ident, xg, yg, A):
    ctx, sb, ps, sem = scope(nc, "exp1")
    with ctx:
        rows = [sb(f"rows{s}", [P, D]) for s in range(2)]
        up_w = [sb(f"up_w{s}", [P, KD, EG, 2 * F1]) for s in range(2)]
        down_w = [sb(f"down_w{s}", [P, EG, D]) for s in range(2)]
        xgT = [sb(f"xgT{s}", [P, D]) for s in range(2)]
        sg = [sb(f"sg{s}", [P, F1]) for s in range(2)]
        h = [sb(f"h{s}", [P, P]) for s in range(2)]
        hT = [sb(f"hT{s}", [P, P]) for s in range(2)]
        y = [sb(f"y{s}", [P, D]) for s in range(2)]
        xtp = [ps(f"xtp{s}", [P, 512]) for s in range(2)]
        gup = [ps(f"gup{s}", [P, 512]) for s in range(2)]
        htp = [ps(f"htp{s}", [P, 512]) for s in range(2)]
        yp = [ps(f"yp{s}", [P, 512]) for s in range(2)]
        names = ("rows", "up_w", "down_w", "xtp", "xgT", "gup", "sg", "h", "htp", "hT", "yp", "y", "stored")
        S = {f"{n}{s}": sem(f"{n}{s}") for n in names for s in range(2)}
        S["padded"] = sem("padded")
        block = ctx.enter_context(nc.Block())

        @block.sync
        def _(sp):
            with sp.Fori(0, NG // 2) as i:
                for s in range(2):
                    g = bass.ds(2 * i + s, 1)
                    sp.wait_ge(S[f"xtp{s}"], i)
                    sp.dma_start(rows[s][:, :], xg[bass.ds((2 * i + s) * P, P), :]).then_inc(S[f"rows{s}"], 16)
                    sp.wait_ge(S[f"gup{s}"], i)
                    sp.dma_start(up_w[s][:, :, :, :], A["up1_w"][g].rearrange("o p k e f -> p (o k) e f")
                                 ).then_inc(S[f"up_w{s}"], 16)
                    sp.wait_ge(S[f"yp{s}"], i)
                    sp.dma_start(down_w[s][0:F1, :, :], A["down1_w"][g].rearrange("o f e d -> f (o e) d")
                                 ).then_inc(S[f"down_w{s}"], 16)

        @block.gpsimd
        def _(pool):
            with pool.Fori(0, NG // 2) as i:
                for s in range(2):
                    pool.wait_ge(S[f"y{s}"], i + 1)
                    pool.wait_ge(S["rows0"], 16)
                    pool.dma_start(yg[bass.ds((2 * i + s) * P, P), :], y[s][:, :]).then_inc(S[f"stored{s}"], 16)
            for s in range(2):
                pool.wait_ge(S[f"stored{s}"], 16 * (NG // 2))

        @block.tensor
        def _(pe):
            def head(n, s):
                pe.wait_ge(S[f"rows{s}"], 16 * n + 16)
                pe.wait_ge(S[f"xgT{s}"], n)
                for k in range(KD):
                    mm = pe.transpose(xtp[s][:, k * P:(k + 1) * P], rows[s][:, k * P:(k + 1) * P], ident[:, :])
                mm.then_inc(S[f"xtp{s}"], 1)
                pe.wait_ge(S[f"up_w{s}"], 16 * n + 16)
                pe.wait_ge(S[f"h{s}"], n)
                pe.wait_ge(S[f"xgT{s}"], n + 1)
                for e in range(EG):
                    r = slice(e * CAP, (e + 1) * CAP)
                    for k in range(KD):
                        mm = pe.matmul(gup[s][r, 0:2 * F1], xgT[s][:, k * P + e * CAP:k * P + (e + 1) * CAP],
                                       up_w[s][:, k, e, :], start=(k == 0), stop=(k == KD - 1))
                mm.then_inc(S[f"gup{s}"], 1)

            def tail(n, s):
                pe.wait_ge(S[f"hT{s}"], n)
                pe.wait_ge(S[f"h{s}"], n + 1)
                pe.transpose(htp[s][:, 0:P], h[s][:, :], ident[:, :]).then_inc(S[f"htp{s}"], 1)
                pe.wait_ge(S[f"hT{s}"], n + 1)
                pe.wait_ge(S[f"y{s}"], n)
                pe.wait_ge(S[f"down_w{s}"], 16 * n + 16)
                for e in range(EG):
                    r = slice(e * CAP, (e + 1) * CAP)
                    mm = pe.matmul(yp[s][r, 0:D], hT[s][:, r], down_w[s][:, e, :], start=True, stop=True)
                mm.then_inc(S[f"yp{s}"], 1)

            pe.wait_ge(S["padded"], 4)
            head(0, 0)
            with pe.Fori(0, NG // 2 - 1) as i:
                head(i, 1)
                tail(i, 0)
                head(i + 1, 0)
                tail(i, 1)
            n = NG // 2 - 1
            head(n, 1)
            tail(n, 0)
            tail(n, 1)

        @block.scalar
        def _(act):
            act.preload_act_table_set("silu_and_others")

            def head(n, s):
                act.wait_ge(S[f"xtp{s}"], n + 1)
                act.wait_ge(S[f"gup{s}"], n)
                act.activation(xgT[s][:, :], xtp[s][:, 0:D], ACT.Copy).then_inc(S[f"xgT{s}"], 1)
                act.wait_ge(S[f"gup{s}"], n + 1)
                act.wait_ge(S[f"h{s}"], n)
                act.activation(sg[s][:, :], gup[s][:, 0:F1], ACT.Silu).then_inc(S[f"sg{s}"], 1)

            with act.Fori(0, NG // 2) as i:
                head(i, 0)
                head(i, 1)

        @block.vector
        def _(ve):
            def head(n, s):
                ve.wait_ge(S[f"htp{s}"], n)
                ve.wait_ge(S[f"sg{s}"], n + 1)
                ve.tensor_tensor(h[s][:, 0:F1], gup[s][:, F1:2 * F1], sg[s][:, :], ALU.mult).then_inc(S[f"h{s}"], 1)

            def tail(n, s):
                ve.wait_ge(S[f"htp{s}"], n + 1)
                ve.wait_ge(S[f"yp{s}"], n)
                ve.tensor_copy(hT[s][:, :], htp[s][:, 0:P]).then_inc(S[f"hT{s}"], 1)
                ve.wait_ge(S[f"yp{s}"], n + 1)
                ve.wait_ge(S[f"stored{s}"], 16 * n)
                ve.tensor_copy(y[s][:, :], yp[s][:, 0:D]).then_inc(S[f"y{s}"], 1)

            for s in range(2):
                ve.memset(h[s][:, F1:], 0.0).then_inc(S["padded"], 1)
                ve.memset(down_w[s][F1:, :, :], 0.0).then_inc(S["padded"], 1)
            ve.wait_ge(S["padded"], 4)
            head(0, 0)
            with ve.Fori(0, NG // 2 - 1) as i:
                head(i, 1)
                tail(i, 0)
                head(i + 1, 0)
                tail(i, 1)
            n = NG // 2 - 1
            head(n, 1)
            tail(n, 0)
            tail(n, 1)


def combine1(nc, x, reads, wk, yg):
    ctx, sb, ps, sem = scope(nc, "comb1")
    R = 8
    with ctx:
        row = [sb(f"row{i}", [P, D]) for i in range(R)]
        come = [sem(f"come{i}") for i in range(R)]
        used = sem("used")
        block = ctx.enter_context(nc.Block())

        @block.gpsimd
        def _(pool):
            for n in range(NT * TOP):
                t, k = n // TOP, n % TOP
                if n >= R:
                    pool.wait_ge(used, n - R + 1)
                pool.indirect_dma_start(row[n % R][:, :], None, yg[:, :], bass.IndirectOffsetOnAxis(reads[:, t, k:k + 1], 0)
                                        ).then_inc(come[n % R], 16)

        @block.vector
        def _(ve):
            for n in range(NT * TOP):
                t, k = n // TOP, n % TOP
                ve.wait_ge(come[n % R], 16 * (n // R) + 16)
                if n:
                    ve.wait_ge(used, n)
                ve.scalar_tensor_tensor(x[:, t, :], row[n % R][:, :], wk[:, t, k:k + 1], x[:, t, :],
                                        ALU.mult, ALU.add).then_inc(used, 1)


def gated_bias_setup(nc, norm_w, gb, gate, A):
    ctx, sb, ps, sem = scope(nc, "gb")
    with ctx:
        ld = sem("ld")
        done = sem("done")
        block = ctx.enter_context(nc.Block())

        @block.sync
        def _(sp):
            sp.dma_start(norm_w[:, :], A["norm_w"]).then_inc(ld, 16)
            sp.dma_start(gb[:, :], A["out_b"].to_broadcast([P, D])).then_inc(ld, 16)
            sp.dma_start(gate[:, :], A["res_gate"].to_broadcast([P, 1])).then_inc(ld, 16)

        @block.vector
        def _(ve):
            ve.wait_ge(ld, 48)
            ve.tensor_scalar(gb[:, :], gb[:, :], gate[:, 0:1], None, ALU.mult).then_inc(done, 1)
            ve.wait_ge(done, 1)


def store(nc, x, out):
    ctx, sb, ps, sem = scope(nc, "st")
    with ctx:
        done = sem("done")
        block = ctx.enter_context(nc.Block())

        @block.sync
        def _(sp):
            sp.dma_start(out.rearrange("(t p) d -> p t d", p=P), x[:, :, :]).then_inc(done, 16)
            sp.wait_ge(done, 16)


def program(nc, A):
    USED.clear()
    with ExitStack() as ctx:
        sb = lambda name, shape: ctx.enter_context(nc.sbuf_tensor(name, shape, F32))
        x = sb("x", [P, NT, D])
        xT = sb("xT", [P, KD, TOK])
        ident, tri, after, ones = (sb(n, [P, P]) for n in ("ident", "upto", "after", "ones"))
        constants(nc, ident, tri, after, ones)
        with ExitStack() as early:
            norm_w, gb, gate = (early.enter_context(nc.sbuf_tensor(n, [P, m], F32))
                                for n, m in (("norm_w", KD), ("gb", D), ("gate", 1)))
            gated_bias_setup(nc, norm_w, gb, gate, A)
            normalise(nc, "n0", x, xT, ident, x_dram=A["x"], rms=(norm_w[:, :], gb[:, :]))
        mixer(nc, x, xT, ident, tri, after, ones, A)
        clear_semaphores(nc)
        normalise(nc, "n1", x, xT, ident)
        with nc.sbuf_tensor("comb", [P, NT, E0 + 1], F32) as comb:
            gate0(nc, xT, comb, A)
            ffn(nc, "exp0", x, xT, A["up0_w"], A["down0_w"], E0 + 1, comb)
        normalise(nc, "n2", x, xT, ident)
        attention(nc, x, xT, ident, A)
        xg = nc.dram_tensor("slot_rows", [SLOTS, D], F32).ap()
        yg = nc.dram_tensor("slot_results", [SLOTS, D], F32).ap()
        xn = sb("xn", [P, NT, D])
        before = sb("before", [P, P])
        slots = ctx.enter_context(nc.sbuf_tensor("slots", [P, NT, TOP], mybir.dt.uint32))
        reads = ctx.enter_context(nc.sbuf_tensor("reads", [P, NT, TOP], mybir.dt.uint32))
        wk = sb("wk", [P, NT, TOP])
        strict(nc, before, tri, ident)
        normalise(nc, "n3", x, xT, ident, rows=xn)
        route1(nc, xT, xn, slots, reads, wk, before, ones, xg, A)
        ffn(nc, "shared", x, xT, A["shup_w"], A["shdown_w"], 1, None)
        experts1(nc, ident, xg, yg, A)
        combine1(nc, x, reads, wk, yg)
        store(nc, x, A["out"])


def strict(nc, before, upto, ident):
    ctx, sb, ps, sem = scope(nc, "strict")
    with ctx:
        done = sem("done")
        block = ctx.enter_context(nc.Block())

        @block.vector
        def _(ve):
            ve.tensor_tensor(before[:, :], upto[:, :], ident[:, :], ALU.subtract).then_inc(done, 1)
            ve.wait_ge(done, 1)


def layouts(i):
    i = {k: np.asarray(v) for k, v in i.items()}
    c = np.ascontiguousarray
    a = {}
    a["x"] = c(i["L0_attn_hidden_states"].reshape(TOK, D))
    a["norm_w"] = c(i["L0_attn_norm_w"].reshape(KD, P).T)
    a["out_b"] = c(i["L0_attn_out_proj_b"][None])
    a["res_gate"] = c(i["L0_attn_res_gate"][None])
    w = i["L0_attn_in_proj_w"].T.reshape(KD, P, 2, KI, P)
    a["in_w"] = c(w.transpose(3, 1, 2, 0, 4).reshape(KI, P, 2 * KD, P))
    a["in_b"] = c(i["L0_attn_in_proj_b"].reshape(2 * KI, P).T)
    a["conv_w"] = c(i["L0_attn_conv_w"].reshape(KI, P, 4).transpose(1, 0, 2))
    a["conv_b"] = c(i["L0_attn_conv_b"].reshape(KI, P).T)
    xw = i["L0_attn_x_proj_w"].reshape(NH0, 1 + 2 * NS, DI)
    xb = i["L0_attn_x_proj_b"].reshape(NH0, 1 + 2 * NS)
    bc = xw[:, 1:].reshape(PAIRS, 2, 2, NS, KI, P)
    a["bc_w"] = c(bc.transpose(0, 2, 5, 4, 1, 3).reshape(PAIRS * 2, P, KI, P))
    a["bc_b"] = c(xb[:, 1:].reshape(PAIRS, 2, 2, NS).transpose(1, 3, 0, 2).reshape(P, PAIRS, 2))
    means = np.zeros((DI, NH0), np.float32)
    means[np.arange(DI), np.arange(DI) // DH] = 1.0 / DH
    pad = np.zeros((DI, DTC - 2 * NH0), np.float32)
    a["dt_w"] = c(np.concatenate([xw[:, 0].T, means, pad], 1).reshape(KI, P, DTC).transpose(1, 0, 2))
    a["par"] = c(np.concatenate([i["L0_attn_A_log"], i["L0_attn_log2_alpha_base"], i["L0_attn_log2_beta"],
                                 i["L0_attn_surprise_ema"], xb[:, 0], i["L0_attn_res_gate"]])[None])
    a["out_w"] = c(i["L0_attn_out_proj_w"].T.reshape(KI, P, D).transpose(1, 0, 2))
    a["gate0_w"] = c(i["L0_ffn_gate_w"].reshape(KD, P, E0).transpose(1, 0, 2))
    up = np.concatenate([i["L0_ffn_expert_gate_up"], i["L0_ffn_base_gate_up"][None]])
    a["up0_w"] = c(up.reshape(E0 + 1, KD, P, 2 * I0).transpose(0, 2, 1, 3))
    down = np.concatenate([i["L0_ffn_expert_down"], i["L0_ffn_base_down"][None]])
    a["down0_w"] = c(down.reshape(E0 + 1, KH, P, D).transpose(0, 2, 1, 3))
    qkv = i["L1_attn_W_qkv"].reshape(KD, P, 3, QG, 4, DH1)
    strips = np.zeros((P, KD, 2, QG, 4, 2, DH1), np.float32)
    strips[:, :, :, :, :, 0] = qkv[:, :, 0:2].transpose(1, 0, 2, 3, 4, 5)
    a["qk_w"] = c(strips.reshape(P, KD, 2 * QG, P))
    a["v_w"] = c(qkv[:, :, 2].reshape(KD, P, D).transpose(1, 0, 2))
    a["o_w"] = c(i["L1_attn_W_o"].reshape(KD, P, D).transpose(1, 0, 2))
    a["router_w"] = c(i["L1_ffn_router_w"].T.reshape(KD, P, E1).transpose(1, 0, 2))
    a["router_b"] = c(i["L1_ffn_router_bias"][None])
    gu = np.stack([i["L1_ffn_gate_w"], i["L1_ffn_up_w"]], 1).reshape(NG, EG, 2, F1, KD, P)
    a["up1_w"] = c(gu.transpose(0, 5, 4, 1, 2, 3).reshape(NG, P, KD, EG, 2 * F1))
    a["down1_w"] = c(i["L1_ffn_down_w"].reshape(NG, EG, D, F1).transpose(0, 3, 1, 2))
    sh = np.concatenate([i["L1_ffn_sh_gate_w"].reshape(I0, D), i["L1_ffn_sh_up_w"].reshape(I0, D)])
    a["shup_w"] = c(sh.T.reshape(1, KD, P, 2 * I0).transpose(0, 2, 1, 3))
    a["shdown_w"] = c(i["L1_ffn_sh_down_w"].transpose(0, 2, 1).reshape(1, KH, P, D).transpose(0, 2, 1, 3))
    return a


def kernel(**inputs):
    from concourse import bacc
    from concourse.bass_utils import run_bass_kernel_spmd

    arrays = layouts(inputs)
    nc = bacc.Bacc("TRN2", target_bir_lowering=False, num_devices=1)
    A = {n: nc.dram_tensor(f"in_{n}", a.shape, mybir.dt.from_np(a.dtype), kind="ExternalInput").ap()
         for n, a in arrays.items()}
    A["out"] = nc.dram_tensor("out", [TOK, D], F32, kind="ExternalOutput").ap()
    program(nc, A)
    r = run_bass_kernel_spmd(nc, [{f"in_{n}": a for n, a in arrays.items()}], core_ids=[0])
    return r.results[0]["out"].reshape(BATCH, SEQ, D)
```

```python
from contextlib import ExitStack

import numpy as np

import concourse.bass as bass
from concourse import mybir

ACT = mybir.ActivationFunctionType
ALU = mybir.AluOpType
F32 = mybir.dt.float32
F32R = mybir.dt.float32r
I32 = mybir.dt.int32
AX_X = mybir.AxisListType.X

P = 128
D = 256
KD = D // P
BATCH, SEQ = 4, 512
TOK = BATCH * SEQ
NT = TOK // P
CH = SEQ // P
LN_EPS = 1e-5
RMS_EPS = float(np.finfo(np.float32).eps)

NH0, DH, NS = 24, 64, 64
DI = NH0 * DH
KI = DI // P
PAIRS = KI
DTC = 64
HC = 2 * CH
LN2 = float(np.log(2.0))


class Chain:

    def __init__(self, eng, sem):
        self.eng, self.sem, self.n = eng, sem, 0

    def __call__(self, ins):
        self.n += 1
        ins.then_inc(self.sem, 1)
        self.eng.wait_ge(self.sem, self.n)

    def restart(self):
        self.eng.sem_clear(self.sem)
        self.n = 0


def rsqrt(ve, link, out, v, tmp):
    link(ve.tensor_scalar(tmp.bitcast(I32), v.bitcast(I32), 1, None, ALU.logical_shift_right))
    link(ve.tensor_scalar(out.bitcast(I32), tmp.bitcast(I32), -1.0, float(0x5F3759DF), ALU.mult, ALU.add))
    for _ in range(3):
        link(ve.tensor_tensor(tmp, out, out, ALU.mult))
        link(ve.scalar_tensor_tensor(tmp, tmp, -0.5, v, ALU.mult, ALU.mult))
        link(ve.scalar_tensor_tensor(out, tmp, 1.5, out, ALU.add, ALU.mult))


def scope(nc, tag):
    ctx = ExitStack()

    def sb(name, shape, dt=F32):
        return ctx.enter_context(nc.sbuf_tensor(f"{tag}_{name}", shape, dt))

    def ps(name, shape, dt=F32):
        return ctx.enter_context(nc.psum_tensor(f"{tag}_{name}", shape, dt))

    def sem(name):
        USED.append(ctx.enter_context(nc.semaphore(f"{tag}_{name}")))
        return USED[-1]

    return ctx, sb, ps, sem


USED = []


def clear_semaphores(nc):
    with nc.Block() as block:
        @block.gpsimd
        def _(pool):
            for s in USED:
                pool.sem_clear(s)
    USED.clear()


def constants(nc, ident, upto, after, ones):
    ctx, sb, ps, sem = scope(nc, "const")
    with ctx:
        filled = sem("filled")
        made = sem("made")
        block = ctx.enter_context(nc.Block())

        @block.gpsimd
        def _(pool):
            pool.memset(ident[:, :], 0.0).then_inc(filled, 1)
            for m in (upto, after, ones):
                pool.memset(m[:, :], 1.0).then_inc(filled, 1)
            pool.wait_ge(filled, 4)
            sel = pool.affine_select
            sel(out=ident[:, :], in_=ident[:, :], compare_op=ALU.not_equal, fill=1.0, base=0,
                pattern=[[-1, P]], channel_multiplier=1).then_inc(made, 1)
            sel(out=upto[:, :], in_=upto[:, :], compare_op=ALU.is_ge, fill=0.0, base=0,
                pattern=[[1, P]], channel_multiplier=-1).then_inc(made, 1)
            sel(out=after[:, :], in_=after[:, :], compare_op=ALU.is_gt, fill=0.0, base=0,
                pattern=[[-1, P]], channel_multiplier=1).then_inc(made, 1)
            pool.wait_ge(made, 3)


def normalise(nc, tag, x, xT, ident, x_dram=None, rms=None, rows=None):
    ctx, sb, ps, sem = scope(nc, tag)
    with ctx:
        stats = sb("stats", [P, NT, 6])
        mv = sb("mv", [P, NT, 2])
        var = sb("var", [P, NT])
        rstd = sb("rstd", [P, NT])
        rrms = sb("rrms", [P, NT])
        tmp = sb("tmp", [P, NT])
        hrow = sb("hrow", [P, 2, D])
        xrow = sb("xrow", [P, 2, D])
        trans = [ps(f"trans{s}", [P, 512]) for s in range(2)]
        loaded = sem("loaded")
        order = sem("order")
        row_ready = sem("row_ready")
        turned = [sem(f"turned{s}") for s in range(2)]
        stored = [sem(f"stored{s}") for s in range(2)]
        block = ctx.enter_context(nc.Block())

        if x_dram is not None:
            @block.sync
            def _(sp):
                for g in range(4):
                    sp.dma_start(x[:, 4 * g:4 * g + 4, :],
                                 x_dram[512 * g:512 * g + 512, :].rearrange("(t p) d -> p t d", p=P)
                                 ).then_inc(loaded, 16)

        @block.vector
        def _(ve):
            link = Chain(ve, order)
            if x_dram is not None:
                ve.wait_ge(loaded, 64)
            for t in range(NT):
                ve.bn_stats(stats[:, t, :], x[:, t, :])
            link(ve.memset(tmp[:, :], 0.0))
            ve.drain().then_inc(order, 1)
            link.n += 1
            ve.wait_ge(order, link.n)
            for t in range(NT):
                ve.bn_aggr(mv[:, t, :], stats[:, t, :])
            ve.drain().then_inc(order, 1)
            link.n += 1
            ve.wait_ge(order, link.n)
            link(ve.tensor_scalar(var[:, :], mv[:, :, 1], LN_EPS, None, ALU.add))
            rsqrt(ve, link, rstd[:, :], var[:, :], tmp[:, :])
            if rms:
                norm_w, gated_bias = rms
                link(ve.tensor_tensor(var[:, :], mv[:, :, 1], rstd[:, :], ALU.mult))
                link(ve.tensor_tensor(var[:, :], var[:, :], rstd[:, :], ALU.mult))
                link(ve.tensor_scalar(var[:, :], var[:, :], RMS_EPS, None, ALU.add))
                rsqrt(ve, link, rrms[:, :], var[:, :], tmp[:, :])
            with ve.Fori(0, NT // 2) as i:
                link.restart()
                for s in range(2):
                    t = bass.ds(2 * i + s, 1)
                    h = hrow[:, s:s + 1, :]
                    ve.wait_ge(turned[s], i)
                    if rms:
                        link(ve.tensor_scalar(h, x[:, t, :], mv[:, t, 0:1].rearrange("p o c -> p (o c)"),
                                              rstd[:, t], ALU.subtract, ALU.mult))
                        ve.tensor_scalar(xrow[:, s:s + 1, :], h, rrms[:, t], None, ALU.mult).then_inc(row_ready, 1)
                        link(ve.tensor_tensor(h, h, gated_bias.unsqueeze(1), ALU.add))
                        link(ve.tensor_tensor(x[:, t, :], x[:, t, :], h, ALU.add))
                    else:
                        ve.tensor_scalar(xrow[:, s:s + 1, :], x[:, t, :], mv[:, t, 0:1].rearrange("p o c -> p (o c)"),
                                         rstd[:, t], ALU.subtract, ALU.mult).then_inc(row_ready, 1)
                        if rows is not None:
                            ve.tensor_scalar(rows[:, t, :], x[:, t, :],
                                             mv[:, t, 0:1].rearrange("p o c -> p (o c)"),
                                             rstd[:, t], ALU.subtract, ALU.mult)

        @block.tensor
        def _(pe):
            with pe.Fori(0, NT // 2) as i:
                for s in range(2):
                    pe.wait_ge(row_ready, 2 * i + s + 1)
                    pe.wait_ge(stored[s], i)
                    for k in range(KD):
                        mm = pe.transpose(trans[s][:, k * P:(k + 1) * P], xrow[:, s, k * P:(k + 1) * P], ident[:, :])
                    mm.then_inc(turned[s], 1)

        @block.scalar
        def _(act):
            act.preload_act_table_set("natural_log_exp_and_others")
            with act.Fori(0, NT // 2) as i:
                for s in range(2):
                    act.wait_ge(turned[s], i + 1)
                    for k in range(KD):
                        last = act.activation(xT[:, k, bass.ds((2 * i + s) * P, P)], trans[s][:, k * P:(k + 1) * P],
                                              ACT.Copy, scale=rms[0][:, k:k + 1] if rms else 1.0)
                    last.then_inc(stored[s], 1)


def mixer(nc, x, xT, ident, upto, after, ones, A):
    ctx, sb, ps, sem = scope(nc, "mix")
    with ctx:
        in_b = sb("in_b", [P, 2 * KI])
        conv_w = sb("conv_w", [P, KI, 4])
        conv_b = sb("conv_b", [P, KI])
        bc_b = sb("bc_b", [P, PAIRS, 2])
        dt_h = sb("dt_h", [P, KI, DTC], F32R)
        dt_l = sb("dt_l", [P, KI, DTC], F32R)
        out_w = sb("out_w", [P, KI, D])
        par = sb("par", [P, 5 * NH0 + 1])
        kpar = sb("kpar", [P, 4, NH0])
        ab = sb("ab", [P, NH0, CH])
        omab = sb("omab", [P, NH0, CH])
        after_r = sb("after_r", [P, P], F32R)
        xTh = sb("xTh", [P, KD, SEQ], F32R)
        xTl = sb("xTl", [P, KD, SEQ], F32R)
        xc_h = sb("xc_h", [P, KI, SEQ], F32R)
        xc_l = sb("xc_l", [P, KI, SEQ], F32R)
        zy = sb("zy", [P, KI, SEQ])
        dt_w = zy[:, :, 0:DTC]
        w_in = [sb(f"w_in{s}", [P, 4, P]) for s in range(2)]
        w_in_h = [sb(f"w_in_h{s}", [P, 4, P], F32R) for s in range(2)]
        w_in_l = [sb(f"w_in_l{s}", [P, 4, P], F32R) for s in range(2)]
        xin = [sb(f"xin{s}", [P, SEQ + 4]) for s in range(2)]
        acc = [sb(f"acc{s}", [P, SEQ]) for s in range(2)]
        gd = sb("gd", [P, NH0, CH])
        ge = sb("ge", [P, NH0, CH])
        gx = sb("gx", [P, NH0, CH])
        gain = sb("gain", [P, NH0, CH])
        w = sb("w", [P, KI, P])
        w_h = {m: sb(f"w_{m}_h", [P, KI, P], F32R) for m in "bc"}
        w_l = {m: sb(f"w_{m}_l", [P, KI, P], F32R) for m in "bc"}
        bT = sb("bT", [P, SEQ])
        cT = sb("cT", [P, SEQ])
        sq_c, sq_b = (t[:, 4:] for t in xin)
        nb = sb("nb", [P, HC])
        rb = sb("rb", [P, HC])
        ncn = sb("ncn", [P, HC])
        rc = sb("rc", [P, HC])
        nt = sb("nt", [P, HC])
        u = sb("u", [P, HC])
        e2 = sb("e2", [P, HC])
        alpha = sb("alpha", [P, HC])
        lna = sb("lna", [P, HC])
        lna_h = sb("lna_h", [P, HC], F32R)
        lna_l = sb("lna_l", [P, HC])
        wj = sb("wj", [P, HC])
        ul_h = sb("ul_h", [P, HC, P], F32R)
        ul_l = sb("ul_l", [P, HC, P], F32R)
        dec = sb("dec", [P, HC, P])
        dtT = acc[0]
        ecum = sb("ecum", [P, 3 * HC])
        ecr = sb("ecr", [P, HC])
        xst = acc[1]
        xw = sb("xw", [P, CH, P])
        bf = sb("bf", [P, CH - 1, P])
        prob = dec
        state = sb("state", [P, CH - 1, P])
        ys = acc[0]
        yi = sq_c

        proj = {"b": ps("proj_b", [P, 512]), "c": ps("proj_c", [P, 512])}
        seg = ps("seg", [P, HC, P])
        bank4, bank5, bank6, bank7 = (ps(f"bank{i}", [P, 512]) for i in range(4, 8))

        names = ("params", "kready", "order", "w_in_ld0", "w_in_ld1", "w_in_hi", "w_in_lo0", "w_in_lo1", "xT_hi", "xT_lo",
                 "inproj0", "inproj1", "inproj2", "inproj3", "xin_ready0", "xin_ready1", "conv_done0", "conv_done1", "xs_ready", "xc_hi", "xc_ready0", "xc_ready1", "const_hi", "const_lo",
                 "dtT_mm", "dtT_ready", "gate_mm", "gate_d", "gate_e", "gate_l", "gate_a", "a_order",
                 "w_ld", "b_hi", "c_hi", "b_lo", "c_lo", "b_proj", "c_proj", "b_out", "c_out",
                 "bsq_ready", "csq_ready", "tanh_in", "tanh_out", "alpha_ready", "lna_ready", "ul_h_ready",
                 "ul_l_ready", "cum_mm", "cum_out", "seg_mm", "seg_out", "dec_ready", "xst_ready",
                 "xt_mm", "xw_ready", "bt_mm", "bf_ready", "ct_mm", "s_mm", "prob_ready", "ds_mm", "state_ready",
                 "y_mm", "ys_ready", "yt_mm", "zy_ready", "o_mm", "o_out")
        S = {n: sem(n) for n in names}
        block = ctx.enter_context(nc.Block())
        flat = lambda t: t[:, :, :].rearrange("p c q -> p (c q)")

        @block.sync
        def _(sp):
            for dst, src in ((in_b[:, :], "in_b"), (conv_w[:, :, :], "conv_w"), (conv_b[:, :], "conv_b"),
                             (bc_b[:, :, :], "bc_b"), (dt_w, "dt_w"), (out_w[:, :, :], "out_w")):
                sp.dma_start(dst, A[src]).then_inc(S["params"], 16)
            sp.dma_start(par[:, :], A["par"].to_broadcast([P, 5 * NH0 + 1])).then_inc(S["params"], 16)

            with sp.Fori(0, BATCH) as b:
                def load(g, i, n, m):
                    sp.wait_ge(S["bc"[1 - n] + "_lo"], g + n)
                    sp.dma_start(w[:, :, :], A["bc_w"][bass.ds(2 * i + n, 1)].rearrange("o p k m -> p (o k) m")
                                 ).then_inc(S["w_ld"], 16)

                def load_in(j):
                    for q in range(4):
                        s = q % 2
                        sp.wait_ge(S[f"w_in_lo{s}"], 2 * (b * (KI // 4) + j) + q // 2)
                        sp.dma_start(w_in[s][:, :, :], A["in_w"][bass.ds(4 * j + q, 1)].rearrange("o p k m -> p (o k) m")
                                     ).then_inc(S[f"w_in_ld{s}"], 16)

                load_in(0)
                load(b * PAIRS, 0, 0, "b")
                load_in(1)
                load(b * PAIRS, 0, 1, "c")
                load_in(2)
                with sp.Fori(1, PAIRS) as i:
                    load(b * PAIRS + i, i, 0, "b")
                    load(b * PAIRS + i, i, 1, "c")

        @block.tensor
        def _(pe):
            def three(out, a_h, a_l, b_h, b_l, first, last):
                pe.matmul(out, a_h, b_h, start=first, stop=False)
                pe.matmul(out, a_h, b_l, start=False, stop=False)
                return pe.matmul(out, a_l, b_h, start=False, stop=last)

            def project(g, m, ks, b=None):
                if 0 in ks:
                    pe.wait_ge(S[m + "_lo"], g + 1)
                    pe.wait_ge(S[m + "_out"], g)
                for k in ks:
                    if b is not None:
                        pe.wait_ge(S[f"xc_ready{k % 2}"], b * (KI // 2) + k // 2 + 1)
                    mm = three(proj[m][:, :], w_h[m][:, k, :], w_l[m][:, k, :], xc_h[:, k, :], xc_l[:, k, :],
                               k == 0, k == KI - 1)
                if KI - 1 in ks:
                    mm.then_inc(S[m + "_proj"], 1)

            def out_project(ks):
                for c in range(CH):
                    out = proj["bc"[c // 2]][:, (c % 2) * D:(c % 2 + 1) * D]
                    for k in ks:
                        mm = pe.matmul(out, zy[:, k, c * P:(c + 1) * P], out_w[:, k, :],
                                       start=(k == 0 and c % 2 == 0), stop=(k == KI - 1), skip_group_check=True)
                return mm

            def turn_y(g):
                pe.wait_ge(S["ys_ready"], g)
                for c in range(CH):
                    mm = pe.transpose(bank7[:, c * P:(c + 1) * P], ys[:, c * P:(c + 1) * P], ident[:, :])
                mm.then_inc(S["yt_mm"], 1)

            def scan(b, i, first, last):
                g = b * PAIRS + i
                pe.wait_ge(S["b_out"], g + 1)
                pe.wait_ge(S["state_ready"], g)
                for c in range(CH):
                    mm = pe.transpose(bank5[:, c * P:(c + 1) * P], bT[:, c * P:(c + 1) * P], ident[:, :])
                mm.then_inc(S["bt_mm"], 1)
                pe.wait_ge(S["xst_ready"], g + 1)
                pe.wait_ge(S["csq_ready"], g)
                for c in range(CH):
                    mm = pe.transpose(bank4[:, c * P:(c + 1) * P], xst[:, c * P:(c + 1) * P], ident[:, :])
                mm.then_inc(S["xt_mm"], 1)
                if first:
                    project(g, "c", range(KI))
                else:
                    project(g, "c", range(4))
                    turn_y(g)
                    project(g, "c", range(4, KI))
                pe.wait_ge(S["lna_ready"], g + 1)
                pe.wait_ge(S["cum_out"], g)
                for n, m in enumerate((after, ones, upto)):
                    mm = pe.matmul(bank6[:, n * HC:(n + 1) * HC], m[:, :], lna[:, :], start=True, stop=True)
                mm.then_inc(S["cum_mm"], 1)
                pe.wait_ge(S["ul_h_ready"], g + 1)
                pe.wait_ge(S["ul_l_ready"], g + 1)
                pe.wait_ge(S["prob_ready"], g)
                for h in range(2):
                    r = slice(h * CH, (h + 1) * CH)
                    pe.matmul(seg[:, r, :], after_r[:, :], ul_h[:, r, :], start=True, stop=False)
                    mm = pe.matmul(seg[:, r, :], after_r[:, :], ul_l[:, r, :], start=False, stop=True)
                mm.then_inc(S["seg_mm"], 1)
                pe.wait_ge(S["c_out"], g + 1)
                pe.wait_ge(S["xw_ready"], g + 1)
                for c in range(CH):
                    mm = pe.transpose(bank4[:, c * P:(c + 1) * P], cT[:, c * P:(c + 1) * P], ident[:, :])
                mm.then_inc(S["ct_mm"], 1)
                if last:
                    pe.wait_ge(S["zy_ready"], g)
                    out_project(range(KI - 1))
                else:
                    project(g + 1, "b", range(KI // 2))
                pe.wait_ge(S["seg_out"], g + 1)
                for h in range(2):
                    for c in range(CH):
                        r = slice(h * DH, (h + 1) * DH)
                        mm = pe.matmul(seg[:, h * CH + c, :], bT[r, c * P:(c + 1) * P],
                                       cT[r, c * P:(c + 1) * P], start=True, stop=True)
                mm.then_inc(S["s_mm"], 1)
                pe.wait_ge(S["bf_ready"], g + 1)
                for c in range(CH - 1):
                    mm = pe.matmul(bank5[:, c * P:(c + 1) * P], bf[:, c, :], xw[:, c, :], start=True, stop=True)
                mm.then_inc(S["ds_mm"], 1)
                if not last:
                    project(g + 1, "b", range(KI // 2, KI))
                pe.wait_ge(S["prob_ready"], g + 1)
                pe.wait_ge(S["zy_ready"], g)
                for c in range(CH):
                    for h in range(2):
                        mm = pe.matmul(bank7[:, c * P + h * DH:c * P + (h + 1) * DH], prob[:, h * CH + c, :],
                                       xw[:, c, h * DH:(h + 1) * DH], start=True, stop=True)
                pe.wait_ge(S["state_ready"], g + 1)
                for c in range(1, CH):
                    mm = pe.matmul(bank6[:, c * P:(c + 1) * P], cT[:, c * P:(c + 1) * P], state[:, c - 1, :],
                                   start=True, stop=True)
                mm.then_inc(S["y_mm"], 1)

            pe.wait_ge(S["params"], 16 * 7)
            with pe.Fori(0, BATCH) as b:
                with pe.Fori(0, KI // 4) as j:
                    for q in range(4):
                        s = q % 2
                        pe.wait_ge(S["xT_lo"], b + 1)
                        pe.wait_ge(S[f"w_in_lo{s}"], 2 * (b * (KI // 4) + j) + q // 2 + 1)
                        pe.wait_ge(S[f"xin_ready{s}"], 2 * (b * (KI // 4) + j) + q // 2)
                        for half in range(2):
                            out = (bank4, bank5, bank6, bank7)[2 * s + half]
                            for k in range(KD):
                                mm = three(out[:, :], w_in_h[s][:, 2 * half + k, :], w_in_l[s][:, 2 * half + k, :],
                                           xTh[:, k, :], xTl[:, k, :], k == 0, k == KD - 1)
                        mm.then_inc(S[f"inproj{q}"], 1)
                g0 = b * PAIRS
                pe.wait_ge(S["o_out"], b)
                project(g0, "b", range(KI), b)
                pe.wait_ge(S["const_lo"], 1)
                for k in range(KI):
                    mm = three(bank6[0:DTC, :], dt_h[:, k, :], dt_l[:, k, :], xc_h[:, k, :], xc_l[:, k, :],
                               k == 0, k == KI - 1)
                mm.then_inc(S["dtT_mm"], 1)
                pe.wait_ge(S["dtT_ready"], b + 1)
                for c in range(CH):
                    mm = pe.matmul(bank7[:, c * DTC:(c + 1) * DTC], dtT[0:DTC, c * P:(c + 1) * P],
                                   ident[0:DTC, 0:DTC], start=True, stop=True)
                mm.then_inc(S["gate_mm"], 1)
                scan(b, 0, True, False)
                with pe.Fori(1, PAIRS - 1) as i:
                    scan(b, i, False, False)
                scan(b, PAIRS - 1, False, True)
                turn_y(g0 + PAIRS)
                pe.wait_ge(S["zy_ready"], g0 + PAIRS)
                out_project([KI - 1]).then_inc(S["o_mm"], 1)

        @block.scalar
        def _(act):
            def split(g, m):
                act.wait_ge(S["w_ld"], 32 * g + (16 if m == "b" else 32))
                act.wait_ge(S[m + "_proj"], g)
                act.activation(flat(w_h[m]), flat(w), ACT.Copy).then_inc(S[m + "_hi"], 1)

            def evacuate(g, i, n, m, dst):
                act.wait_ge(S[m + "_proj"], g + 1)
                act.activation(dst[:, :], proj[m][:, :], ACT.Identity, bias=bc_b[:, bass.ds(i, 1), n]
                               ).then_inc(S[m + "_out"], 1)

            def scan(b, i, last):
                g = b * PAIRS + i
                act.wait_ge(S["bt_mm"], g + 1)
                act.activation(sq_b, bank5[:, :], ACT.Square).then_inc(S["bsq_ready"], 1)
                if not last:
                    split(g + 1, "b")
                act.wait_ge(S["tanh_in"], g + 1)
                act.activation(e2[:, :], u[:, :], ACT.Exp).then_inc(S["tanh_out"], 1)
                act.wait_ge(S["alpha_ready"], g + 1)
                act.activation(lna[:, :], alpha[:, :], ACT.Ln).then_inc(S["lna_ready"], 1)
                evacuate(g, i, 1, "c", cT)
                act.wait_ge(S["cum_mm"], g + 1)
                act.activation(ecum[:, :], bank6[:, 0:3 * HC], ACT.Exp).then_inc(S["cum_out"], 1)
                act.wait_ge(S["seg_mm"], g + 1)
                act.activation(dec[:, :, :], seg[:, :, :], ACT.Exp).then_inc(S["seg_out"], 1)
                act.wait_ge(S["ct_mm"], g + 1)
                act.activation(sq_c, bank4[:, :], ACT.Square).then_inc(S["csq_ready"], 1)
                if not last:
                    split(g + 1, "c")
                    act.wait_ge(S["s_mm"], g + 1)
                    evacuate(g + 1, i + 1, 0, "b", bT)

            act.wait_ge(S["params"], 16 * 7)
            act.preload_act_table_set("natural_log_exp_and_others")
            act.activation(dt_h[:, :, :], dt_w, ACT.Copy)
            act.activation(after_r[:, :], after[:, :], ACT.Copy).then_inc(S["const_hi"], 1)
            act.wait_ge(S["kready"], 1)
            act.activation(kpar[:, 1:3, :], kpar[:, 1:3, :], ACT.Exp, scale=LN2).then_inc(S["a_order"], 1)
            with act.Fori(0, BATCH) as b:
                g0 = b * PAIRS
                act.preload_act_table_set("silu_and_others")
                act.activation(xTh[:, :, :], xT[:, :, bass.ds(b * SEQ, SEQ)], ACT.Copy).then_inc(S["xT_hi"], 1)
                def split_in(j, q):
                    act.wait_ge(S[f"w_in_ld{q % 2}"], 32 * (b * (KI // 4) + j) + 16 * (q // 2) + 16)
                    act.wait_ge(S[f"inproj{(q + 2) % 4}"], b * (KI // 4) + j + (q > 1))
                    act.activation(flat(w_in_h[q % 2]), flat(w_in[q % 2]), ACT.Copy).then_inc(S["w_in_hi"], 1)

                def take(j, q):
                    f, s = 4 * j + q, q % 2
                    act.wait_ge(S[f"inproj{q}"], b * (KI // 4) + j + 1)
                    act.wait_ge(S[f"conv_done{s}"], 2 * (b * (KI // 4) + j) + q // 2)
                    act.wait_ge(S["o_mm"], b)
                    act.activation(xin[s][:, 3:3 + SEQ], (bank4, bank6)[s][:, :], ACT.Identity,
                                   bias=in_b[:, bass.ds(f, 1)])
                    act.activation(zy[:, bass.ds(f, 1), :], (bank5, bank7)[s][:, :].unsqueeze(1), ACT.Silu,
                                   bias=in_b[:, bass.ds(f + KI, 1)]).then_inc(S[f"xin_ready{s}"], 1)

                def convolved(j, q):
                    n, f, s = b * KI + 4 * j + q, 4 * j + q, q % 2
                    act.wait_ge(S[f"conv_done{s}"], 2 * (b * (KI // 4) + j) + q // 2 + 1)
                    act.activation(acc[s][:, :], acc[s][:, :], ACT.Silu, bias=conv_b[:, bass.ds(f, 1)]
                                   ).then_inc(S["xs_ready"], 1)
                    act.wait_ge(S["xs_ready"], n + 1)
                    act.activation(xc_h[:, bass.ds(f, 1), :], acc[s][:, :].unsqueeze(1), ACT.Copy
                                   ).then_inc(S["xc_hi"], 1)

                split_in(0, 0)
                split_in(0, 1)
                split(g0, "b")
                split_in(0, 2)
                act.wait_ge(S["const_lo"], 1)
                take(0, 0)
                with act.Fori(0, KI // 4 - 1) as j:
                    for q in range(1, 5):
                        split_in(j + (q + 2) // 4, (q + 2) % 4)
                        take(j + q // 4, q % 4)
                        convolved(j, q - 1)
                j = KI // 4 - 1
                for q in range(1, 4):
                    if q == 1:
                        split_in(j, q + 2)
                    take(j, q)
                    convolved(j, q - 1)
                convolved(j, 3)
                split(g0, "c")
                act.preload_act_table_set("natural_log_exp_and_others")
                evacuate(g0, 0, 0, "b", bT)
                for s in range(2):
                    act.wait_ge(S[f"xc_ready{s}"], (b + 1) * (KI // 2))
                act.wait_ge(S["dtT_mm"], b + 1)
                act.activation(dtT[0:DTC, :], bank6[0:DTC, :], ACT.Copy).then_inc(S["dtT_ready"], 1)
                act.wait_ge(S["gate_e"], b + 1)
                act.activation(ge[:, :, :], ge[:, :, :], ACT.Exp, scale=-1.0).then_inc(S["a_order"], 1)
                act.wait_ge(S["a_order"], 2 * b + 2)
                act.activation(ge[:, :, :], ge[:, :, :], ACT.Ln, bias=1.0).then_inc(S["gate_l"], 1)
                act.wait_ge(S["gate_a"], b + 1)
                act.activation(gd[:, :, :], gd[:, :, :], ACT.Exp).then_inc(S["a_order"], 1)
                with act.Fori(0, PAIRS - 1) as i:
                    scan(b, i, False)
                scan(b, PAIRS - 1, True)

        @block.gpsimd
        def _(pool):
            def scan(b, i, last):
                g = b * PAIRS + i
                for s in range(2):
                    pool.wait_ge(S[f"xc_ready{s}"], (b + 1) * (KI // 2))
                pool.wait_ge(S["xt_mm"], g)
                pool.tensor_tensor(xst[:, :].unsqueeze(1), xc_h[:, bass.ds(i, 1), :].bitcast(F32),
                                   xc_l[:, bass.ds(i, 1), :].bitcast(F32), ALU.add).then_inc(S["xst_ready"], 1)
                if not last:
                    pool.wait_ge(S["b_hi"], g + 2)
                    pool.tensor_tensor(flat(w_l["b"]), flat(w), flat(w_h["b"]).bitcast(F32), ALU.subtract
                                       ).then_inc(S["b_lo"], 1)
                pool.wait_ge(S["lna_ready"], g + 1)
                pool.wait_ge(S["seg_mm"], g)
                pool.tensor_tensor(ul_h[:, :, :], upto[:, :].unsqueeze(1).to_broadcast([P, HC, P]),
                                   lna[:, :].unsqueeze(2).to_broadcast([P, HC, P]), ALU.mult
                                   ).then_inc(S["ul_h_ready"], 1)
                pool.wait_ge(S["seg_out"], g + 1)
                pool.tensor_tensor(dec[:, :, :], dec[:, :, :], upto[:, :].unsqueeze(1).to_broadcast([P, HC, P]),
                                   ALU.mult).then_inc(S["dec_ready"], 1)

            with pool.Fori(0, BATCH) as b:
                def split_in(j, q):
                    pool.wait_ge(S["w_in_hi"], b * KI + 4 * j + q + 1)
                    s = q % 2
                    pool.tensor_tensor(flat(w_in_l[s]), flat(w_in[s]), flat(w_in_h[s]).bitcast(F32), ALU.subtract
                                       ).then_inc(S[f"w_in_lo{s}"], 1)

                def split_x(j, q):
                    f = bass.ds(4 * j + q, 1)
                    pool.wait_ge(S["xc_hi"], b * KI + 4 * j + q + 1)
                    pool.tensor_tensor(xc_l[:, f, :], acc[q % 2][:, :].unsqueeze(1), xc_h[:, f, :].bitcast(F32),
                                       ALU.subtract).then_inc(S[f"xc_ready{q % 2}"], 1)

                row_cols = bass.ds(b * SEQ, SEQ)
                pool.wait_ge(S["xT_hi"], b + 1)
                pool.tensor_tensor(xTl[:, :, :], xT[:, :, row_cols], xTh[:, :, :].bitcast(F32), ALU.subtract
                                   ).then_inc(S["xT_lo"], 1)
                for q in range(3):
                    split_in(0, q)
                with pool.Fori(0, KI // 4 - 1) as j:
                    for q in range(1, 5):
                        split_in(j + (q + 2) // 4, (q + 2) % 4)
                        split_x(j, q - 1)
                j = KI // 4 - 1
                for q in range(1, 4):
                    if q == 1:
                        split_in(j, q + 2)
                    split_x(j, q - 1)
                split_x(j, 3)
                with pool.Fori(0, PAIRS - 1) as i:
                    scan(b, i, False)
                scan(b, PAIRS - 1, True)

        @block.vector
        def _(ve):
            link = Chain(ve, S["order"])
            wide = lambda t, c: t.rearrange("p (h c) -> p c h", h=2)[:, c, :].unsqueeze(3).to_broadcast(
                [P, c.stop - c.start, 2, DH])
            four = lambda t: t.rearrange("p (c h d) -> p c h d", h=2, d=DH)
            by_head = lambda t: t.rearrange("p (h c) -> p h c", h=2)
            squares = lambda t: t.rearrange("p (c h d) -> p h c d", c=CH, h=2)

            def split(g, m):
                ve.wait_ge(S[m + "_hi"], g + 1)
                ve.tensor_tensor(flat(w_l[m]), flat(w), flat(w_h[m]).bitcast(F32), ALU.subtract
                                 ).then_inc(S[m + "_lo"], 1)

            def gate_y(g, i):
                ve.wait_ge(S["yt_mm"], g)
                ve.tensor_tensor(zy[:, bass.ds(i - 1, 1), :], bank7[:, :].unsqueeze(1), zy[:, bass.ds(i - 1, 1), :],
                                 ALU.mult).then_inc(S["zy_ready"], 1)

            def scan(b, i, first, last):
                g = b * PAIRS + i
                heads = bass.ds(2 * i, 2)
                link.restart()
                ve.wait_ge(S["bsq_ready"], g + 1)
                link(ve.tensor_reduce(by_head(u[:, :]), squares(sq_b), AX_X, ALU.add))
                link(ve.tensor_scalar(nb[:, :], u[:, :], 1e-24, None, ALU.max))
                rsqrt(ve, link, rb[:, :], nb[:, :], nt[:, :])
                link(ve.tensor_tensor(u[:, :], u[:, :], rb[:, :], ALU.mult))
                link(ve.tensor_tensor(u[:, :], u[:, :], rb[:, :], ALU.mult))
                link(ve.tensor_tensor(by_head(u[:, :]), by_head(u[:, :]), gain[:, heads, :], ALU.mult))
                ve.tensor_scalar(u[:, :], u[:, :], 60.0, None, ALU.min).then_inc(S["tanh_in"], 1)
                ve.wait_ge(S["tanh_out"], g + 1)
                link(ve.tensor_scalar(e2[:, :], e2[:, :], 1.0, None, ALU.add))
                link(ve.reciprocal(e2[:, :], e2[:, :]))
                link(ve.tensor_scalar(e2[:, :], e2[:, :], -2.0, 1.0, ALU.mult, ALU.add))
                link(ve.scalar_tensor_tensor(by_head(e2[:, :]), by_head(e2[:, :]), 0.0, omab[:, heads, :],
                                             ALU.max, ALU.mult))
                link(ve.tensor_tensor(by_head(e2[:, :]), by_head(e2[:, :]), ab[:, heads, :], ALU.add))
                ve.tensor_scalar(alpha[:, :], e2[:, :], 0.01, 0.999, ALU.max, ALU.min).then_inc(S["alpha_ready"], 1)
                ve.wait_ge(S["alpha_ready"], g + 1)
                link(ve.tensor_scalar(wj[:, :], alpha[:, :], -1.0, 1.0, ALU.mult, ALU.add))
                link(ve.tensor_tensor(wj[:, :], wj[:, :], rb[:, :], ALU.mult))
                ve.wait_ge(S["lna_ready"], g + 1)
                link(ve.tensor_copy(lna_h[:, :], lna[:, :]))
                link(ve.tensor_tensor(lna_l[:, :], lna[:, :], lna_h[:, :].bitcast(F32), ALU.subtract))
                ve.wait_ge(S["seg_mm"], g)
                ve.tensor_tensor(ul_l[:, :, :], upto[:, :].unsqueeze(1).to_broadcast([P, HC, P]),
                                 lna_l[:, :].unsqueeze(2).to_broadcast([P, HC, P]), ALU.mult
                                 ).then_inc(S["ul_l_ready"], 1)
                ve.wait_ge(S["xt_mm"], g + 1)
                ve.tensor_tensor(four(flat(xw)), four(bank4[:, :]), wide(wj[:, :], slice(0, CH)), ALU.mult
                                 ).then_inc(S["xw_ready"], 1)
                if not first:
                    gate_y(g, i)
                ve.wait_ge(S["cum_out"], g + 1)
                ve.tensor_tensor(four(flat(bf)), four(bank5[:, 0:3 * P]), wide(ecum[:, 0:HC], slice(0, CH - 1)),
                                 ALU.mult).then_inc(S["bf_ready"], 1)
                ve.wait_ge(S["csq_ready"], g + 1)
                link(ve.tensor_reduce(by_head(ncn[:, :]), squares(sq_c), AX_X, ALU.add))
                link(ve.tensor_scalar(ncn[:, :], ncn[:, :], 1e-24, None, ALU.max))
                rsqrt(ve, link, rc[:, :], ncn[:, :], nt[:, :])
                link(ve.tensor_tensor(ecr[:, :], rc[:, :], ecum[:, 2 * HC:], ALU.mult))
                ve.wait_ge(S["dec_ready"], g + 1)
                ve.wait_ge(S["s_mm"], g + 1)
                ve.tensor_tensor(prob[:, :, :], seg[:, :, :], dec[:, :, :], ALU.mult).then_inc(S["prob_ready"], 1)
                ve.wait_ge(S["ds_mm"], g + 1)
                for c in range(CH - 1):
                    for h in range(2):
                        r = slice(h * DH, (h + 1) * DH)
                        new = bank5[r, c * P + h * DH:c * P + (h + 1) * DH]
                        if c == 0:
                            ins = ve.tensor_copy(state[r, 0, r], new)
                        else:
                            m = HC + h * CH + c
                            ins = ve.scalar_tensor_tensor(state[r, c, r], state[r, c - 1, r], ecum[r, m:m + 1],
                                                          new, ALU.mult, ALU.add)
                        if c == CH - 2 and h == 1:
                            ins.then_inc(S["state_ready"], 1)
                        elif c < CH - 2:
                            link(ins)
                if not last:
                    split(g + 1, "c")
                ve.wait_ge(S["y_mm"], g + 1)
                link(ve.tensor_tensor(four(ys[:, :]), four(bank7[:, :]), wide(rc[:, :], slice(0, CH)), ALU.mult))
                link(ve.tensor_tensor(four(yi[:, P:]), four(bank6[:, P:]), wide(ecr[:, :], slice(1, CH)), ALU.mult))
                ve.tensor_tensor(ys[:, P:], ys[:, P:], yi[:, P:], ALU.add).then_inc(S["ys_ready"], 1)

            for s in range(2):
                link(ve.memset(xin[s][:, 0:3], 0.0))
            link(ve.memset(state[:, :, :], 0.0))
            ve.wait_ge(S["params"], 16 * 7)
            row = lambda r: par[:, r * NH0:(r + 1) * NH0]
            link(ve.tensor_scalar(kpar[:, 0, :], row(0), -2.3, -0.01, ALU.max, ALU.min))
            link(ve.tensor_scalar(kpar[:, 1, :], row(1), -3.32, -0.015, ALU.max, ALU.min))
            link(ve.tensor_scalar(kpar[:, 3, :], row(3), 1e-6, None, ALU.add))
            link(ve.reciprocal(kpar[:, 3, :], kpar[:, 3, :]))
            ve.tensor_scalar(kpar[:, 2, :], row(2), -2.0, 2.0, ALU.max, ALU.min).then_inc(S["kready"], 1)
            ve.wait_ge(S["a_order"], 1)
            link(ve.tensor_scalar(kpar[:, 1, :], kpar[:, 1, :], -1.0, 1.0, ALU.mult, ALU.add))
            link(ve.tensor_tensor(kpar[:, 2, :], kpar[:, 2, :], kpar[:, 3, :], ALU.mult))
            link(ve.tensor_scalar(kpar[:, 2, :], kpar[:, 2, :], 2.0 / NS, None, ALU.mult))
            for c in range(CH):
                link(ve.tensor_copy(ab[:, :, c], kpar[:, 1, :]))
                link(ve.tensor_scalar(omab[:, :, c], kpar[:, 1, :], -1.0, 1.0, ALU.mult, ALU.add))
            ve.wait_ge(S["const_hi"], 1)
            ve.tensor_tensor(dt_l[:, :, :], dt_w, dt_h[:, :, :].bitcast(F32), ALU.subtract
                             ).then_inc(S["const_lo"], 1)

            with ve.Fori(0, BATCH) as b:
                g0 = b * PAIRS
                split(g0, "b")
                with ve.Fori(0, KI // 2) as i:
                    link.restart()
                    for s in range(2):
                        n = b * (KI // 2) + i
                        f = bass.ds(2 * i + s, 1)
                        ve.wait_ge(S[f"xin_ready{s}"], n + 1)
                        ve.wait_ge(S[f"xc_ready{s}"], n)
                        H = SEQ // 2
                        for j in range(4):
                            for h in range(2):
                                out, seen = acc[s][:, h * H:(h + 1) * H], xin[s][:, h * H + j:h * H + j + H]
                                if j == 0:
                                    ins = ve.tensor_scalar(out, seen, conv_w[:, f, 0], None, ALU.mult)
                                else:
                                    ve.wait_ge(S["order"], link.n - (1 if j < 3 or h == 0 else 0))
                                    ins = ve.scalar_tensor_tensor(out, seen, conv_w[:, f, j], out, ALU.mult, ALU.add)
                                if j < 3:
                                    ins.then_inc(S["order"], 1)
                                    link.n += 1
                            if j == 3:
                                ins.then_inc(S[f"conv_done{s}"], 1)
                split(g0, "c")
                link.restart()
                chunked = bank7[:, 0:CH * DTC].rearrange("p (c q) -> p q c", c=CH)
                ve.wait_ge(S["gate_mm"], b + 1)
                link(ve.tensor_tensor(gd[:, :, :], chunked[:, 0:NH0, :],
                                      row(4).unsqueeze(2).to_broadcast([P, NH0, CH]), ALU.add))
                ve.tensor_copy(gx[:, :, :], chunked[:, NH0:2 * NH0, :]).then_inc(S["gate_d"], 1)
                ve.scalar_tensor_tensor(ge[:, :, :], gd[:, :, :], -1.0, gd[:, :, :], ALU.mult, ALU.max
                                        ).then_inc(S["gate_e"], 1)
                ve.wait_ge(S["gate_l"], b + 1)
                link(ve.scalar_tensor_tensor(gd[:, :, :], gd[:, :, :], 0.0, ge[:, :, :], ALU.max, ALU.add))
                ve.tensor_tensor(gd[:, :, :], gd[:, :, :], kpar[:, 0, :].unsqueeze(2).to_broadcast([P, NH0, CH]),
                                 ALU.mult).then_inc(S["gate_a"], 1)
                ve.wait_ge(S["a_order"], 2 * b + 3)
                ve.wait_ge(S["gate_d"], b + 1)
                link(ve.tensor_scalar(gd[:, :, :], gd[:, :, :], -1.0, 1.0, ALU.mult, ALU.add))
                link(ve.tensor_tensor(gx[:, :, :], gx[:, :, :], gd[:, :, :], ALU.mult))
                link(ve.tensor_tensor(gx[:, :, :], gx[:, :, :], gx[:, :, :], ALU.mult))
                link(ve.tensor_tensor(gain[:, :, :], gx[:, :, :],
                                      kpar[:, 2, :].unsqueeze(2).to_broadcast([P, NH0, CH]), ALU.mult))
                scan(b, 0, True, False)
                with ve.Fori(1, PAIRS - 1) as i:
                    scan(b, i, False, False)
                scan(b, PAIRS - 1, False, True)
                gate_y(g0 + PAIRS, PAIRS)
                ve.wait_ge(S["o_mm"], b + 1)
                for h in range(2):
                    xs = x[:, bass.ds(b * CH + 2 * h, 2), :]
                    ins = ve.scalar_tensor_tensor(xs, proj["bc"[h]][:, :].rearrange("p (c d) -> p c d", c=2),
                                                  par[:, 5 * NH0:], xs, ALU.mult, ALU.add)
                ins.then_inc(S["o_out"], 1)
                ve.wait_ge(S["o_out"], b + 1)


E0, I0, TOP0 = 8, 512, 2
KH = I0 // P
TILES0 = TOK * TOP0 // P + E0


def route0(nc, xT, slots, wk, tile_expert, before, ones, xg, A):
    ctx, sb, ps, sem = scope(nc, "route0")
    with ctx:
        w = sb("w", [P, KD, E0])
        p = sb("p", [P, NT, E0])
        one = sb("one", [P, NT])
        top = sb("top", [P, NT, 8])
        idx = sb("idx", [P, NT, 8], mybir.dt.uint32)
        idf = sb("idf", [P, NT, 8])
        col = sb("col", [P, E0])
        tile = sb("tile", [P, TILES0, E0])
        hit = [sb(f"hit{k}", [P, NT, E0]) for k in range(TOP0)]
        mask = sb("mask", [P, NT, E0])
        prior = sb("prior", [P, NT + 1, E0])
        place = sb("place", [P, NT, E0])
        count = sb("count", [P, E0])
        whole = sb("whole", [P, E0], I32)
        tiles = sb("tiles", [P, E0])
        first = sb("first", [P, E0])
        end = sb("end", [P, E0])
        past = sb("past", [P, TILES0, E0])
        te = sb("te", [P, TILES0])
        sf = sb("sf", [P, NT, TOP0])
        zero = sb("zero", [P, 4 * D])
        logits = ps("logits", [P, NT, E0])
        rank = ps("rank", [P, NT, E0])
        total = ps("total", [P, E0])
        S = {n: sem(n) for n in ("w", "mm", "order", "shifted", "exp", "iota", "zero", "filled", "mask", "rank")}
        block = ctx.enter_context(nc.Block())

        @block.sync
        def _(sp):
            sp.dma_start(w[:, :, :], A["gate0_w"]).then_inc(S["w"], 16)
            sp.wait_ge(S["zero"], 1)
            for g in range(TILES0 // 4):
                sp.dma_start(xg[4 * P * g:4 * P * (g + 1), :].rearrange("(p c) d -> p (c d)", p=P), zero[:, :]
                             ).then_inc(S["filled"], 16)
            sp.wait_ge(S["filled"], 16 * (TILES0 // 4))

        @block.gpsimd
        def _(pool):
            pool.memset(zero[:, :], 0.0).then_inc(S["zero"], 1)
            pool.iota(col[:, :], pattern=[[1, E0]], base=0, channel_multiplier=0,
                      allow_small_or_imprecise_dtypes=True).then_inc(S["iota"], 1)
            pool.iota(tile[:, :, :], pattern=[[1, TILES0], [0, E0]], base=0, channel_multiplier=0,
                      allow_small_or_imprecise_dtypes=True).then_inc(S["iota"], 1)

        @block.tensor
        def _(pe):
            pe.wait_ge(S["w"], 16)
            for t in range(NT):
                for k in range(KD):
                    mm = pe.matmul(logits[:, t, :], xT[:, k, t * P:(t + 1) * P], w[:, k, :],
                                   start=(k == 0), stop=(k == KD - 1))
            mm.then_inc(S["mm"], 1)
            pe.wait_ge(S["mask"], NT)
            for t in range(NT):
                pe.matmul(rank[:, t, :], before[:, :], mask[:, t, :], start=True, stop=False)
                pe.matmul(rank[:, t, :], ones[:, :], prior[:, t, :], start=False, stop=True)
            pe.matmul(total[:, :], ones[:, :], prior[:, NT, :], start=True, stop=True).then_inc(S["rank"], 1)

        @block.scalar
        def _(act):
            act.wait_ge(S["shifted"], 1)
            act.activation(p[:, :, :], p[:, :, :], ACT.Exp).then_inc(S["exp"], 1)

        @block.vector
        def _(ve):
            link = Chain(ve, S["order"])
            wide = lambda t, n: t.unsqueeze(2).to_broadcast([P, NT, n])
            ve.wait_ge(S["mm"], 1)
            link(ve.tensor_reduce(one[:, :], logits[:, :, :], AX_X, ALU.max))
            ve.tensor_tensor(p[:, :, :], logits[:, :, :], wide(one[:, :], E0), ALU.subtract).then_inc(S["shifted"], 1)
            ve.wait_ge(S["exp"], 1)
            link(ve.tensor_reduce(one[:, :], p[:, :, :], AX_X, ALU.add))
            link(ve.reciprocal(one[:, :], one[:, :]))
            link(ve.tensor_tensor(p[:, :, :], p[:, :, :], wide(one[:, :], E0), ALU.mult))
            for t in range(NT):
                ins = ve.max(top[:, t, :], p[:, t, :])
            link(ins)
            for t in range(NT):
                ins = ve.max_index(idx[:, t, :], top[:, t, :], p[:, t, :])
            link(ins)
            link(ve.tensor_copy(idf[:, :, :], idx[:, :, :]))
            ve.wait_ge(S["iota"], 2)
            cols = col[:, :].unsqueeze(1).to_broadcast([P, NT, E0])
            for k in range(TOP0):
                link(ve.tensor_tensor(hit[k][:, :, :], cols, wide(idf[:, :, k], E0), ALU.is_equal))
            link(ve.tensor_tensor(mask[:, :, :], hit[0][:, :, :], hit[1][:, :, :], ALU.add))
            link(ve.memset(prior[:, 0, :], 0.0))
            for t in range(NT):
                ve.tensor_tensor(prior[:, t + 1, :], prior[:, t, :], mask[:, t, :], ALU.add).then_inc(S["mask"], 1)
                ve.wait_ge(S["mask"], t + 1)
            link(ve.tensor_tensor(one[:, :], top[:, :, 0], top[:, :, 1], ALU.add))
            link(ve.reciprocal(one[:, :], one[:, :]))
            link(ve.tensor_tensor(wk[:, :, :], top[:, :, 0:TOP0], wide(one[:, :], TOP0), ALU.mult))
            ve.wait_ge(S["rank"], 1)
            link(ve.tensor_scalar(count[:, :], total[:, :], float(P - 1), None, ALU.add))
            link(ve.tensor_copy(whole[:, :], count[:, :]))
            link(ve.tensor_scalar(whole[:, :], whole[:, :], P.bit_length() - 1, None, ALU.logical_shift_right))
            link(ve.tensor_copy(tiles[:, :], whole[:, :]))
            link(ve.memset(first[:, 0:1], 0.0))
            for e in range(1, E0):
                link(ve.tensor_tensor(first[:, e:e + 1], first[:, e - 1:e], tiles[:, e - 1:e], ALU.add))
            link(ve.tensor_tensor(end[:, :], first[:, :], tiles[:, :], ALU.add))
            link(ve.tensor_tensor(past[:, :, :], end[:, :].unsqueeze(1).to_broadcast([P, TILES0, E0]), tile[:, :, :],
                                  ALU.is_le))
            link(ve.tensor_reduce(te[:, :], past[:, :, :], AX_X, ALU.add))
            link(ve.tensor_scalar(te[:, :], te[:, :], float(E0 - 1), None, ALU.min))
            link(ve.tensor_copy(tile_expert[:, :], te[:, :]))
            link(ve.tensor_scalar(first[:, :], first[:, :], float(P), None, ALU.mult))
            link(ve.tensor_tensor(place[:, :, :], rank[:, :, :], first[:, :].unsqueeze(1).to_broadcast([P, NT, E0]),
                                  ALU.add))
            for k in range(TOP0):
                link(ve.tensor_tensor(hit[k][:, :, :], hit[k][:, :, :], place[:, :, :], ALU.mult))
                link(ve.tensor_reduce(sf[:, :, k], hit[k][:, :, :], AX_X, ALU.add))
            link(ve.tensor_copy(slots[:, :, :], sf[:, :, :]))


def moe0(nc, x, xT, ident, before, ones, A):
    xg = nc.dram_tensor("slot_rows0", [TILES0 * P, D], F32).ap()
    yg = nc.dram_tensor("slot_results0", [TILES0 * P, D], F32).ap()
    ctx, sb, ps, sem = scope(nc, "moe0")
    with ctx:
        xn = sb("xn", [P, NT, D])
        wk = sb("wk", [P, NT, TOP0])
        slots = sb("slots", [P, NT, TOP0], mybir.dt.uint32)
        tile_expert = sb("tile_expert", [P, TILES0], I32)
        wu = sb("wu", [P, E0, KD, 2 * I0])
        wd = sb("wd", [P, E0, KH, D])
        weights_loaded, sent = sem("weights_loaded"), sem("sent")

        def load_experts(sp):
            for e in range(E0):
                sp.dma_start(wu[:, e, :, :], A["up0_w"][e]).then_inc(weights_loaded, 16)
                sp.dma_start(wd[:, e, :, :], A["down0_w"][e]).then_inc(weights_loaded, 16)

        normalise(nc, "n1", x, xT, ident, rows=xn)
        route0(nc, xT, slots, wk, tile_expert, before, ones, xg, A)
        ffn(nc, "base", x, xT, A["up0_w"][E0], A["down0_w"][E0],
            lambda pool: scatter_rows(pool, xn, slots, xg, TOP0, sent, TILES0 * P - 1), load_experts)
        experts0(nc, ident, xg, yg, wu, wd, weights_loaded, tile_expert)
        combine(nc, "comb0", x, slots, wk, yg, TOP0)


def experts0(nc, ident, xg, yg, wu, wd, weights_loaded, tile_expert):
    ctx, sb, ps, sem = scope(nc, "exp0")
    with ctx:
        rows = [sb(f"rows{s}", [P, D]) for s in range(2)]
        xgT = [sb(f"xgT{s}", [P, D]) for s in range(2)]
        sg = [sb(f"sg{s}", [P, I0]) for s in range(2)]
        h = [sb(f"h{s}", [P, I0]) for s in range(2)]
        hT = [sb(f"hT{s}", [P, I0]) for s in range(2)]
        y = [sb(f"y{s}", [P, D]) for s in range(2)]
        xtp = ps("xtp", [P, 2, D])
        gp = [ps(f"gp{s}", [P, I0]) for s in range(2)]
        up = [ps(f"up{s}", [P, I0]) for s in range(2)]
        htp = [ps(f"htp{s}", [P, I0]) for s in range(2)]
        yp = ps("yp", [P, 2, D])
        names = ("rows", "xtp", "xgT", "gup", "sg", "h", "htp", "hT", "yp", "y", "stored")
        S = {f"{n}{s}": sem(f"{n}{s}") for n in names for s in range(2)}
        block = ctx.enter_context(nc.Block())
        LAST = TILES0 // 2

        def steps(eng, step):
            step(0, 0, True, False)
            step(0, 1, False, False)
            with eng.Fori(1, LAST - 1) as i:
                step(i, 0, False, False)
                step(i, 1, False, False)
            step(LAST - 1, 0, False, False, False)
            step(LAST - 1, 1, False, True, False)

        @block.sync
        def _(sp):
            with sp.Fori(0, LAST) as i:
                for s in range(2):
                    sp.wait_ge(S[f"xtp{s}"], i)
                    sp.dma_start(rows[s][:, :], xg[bass.ds((2 * i + s) * P, P), :]).then_inc(S[f"rows{s}"], 16)

        @block.gpsimd
        def _(pool):
            with pool.Fori(0, LAST) as i:
                for s in range(2):
                    pool.wait_ge(S[f"y{s}"], i + 1)
                    pool.wait_ge(S["rows0"], 16)
                    pool.dma_start(yg[bass.ds((2 * i + s) * P, P), :], y[s][:, :]).then_inc(S[f"stored{s}"], 16)
            for s in range(2):
                pool.wait_ge(S[f"stored{s}"], 16 * LAST)

        @block.tensor
        def _(pe):
            def turn_x(n, s):
                pe.wait_ge(S[f"rows{s}"], 16 * n + 16)
                pe.wait_ge(S[f"xgT{1 - s}"], n + s)
                for k in range(KD):
                    mm = pe.transpose(xtp[:, s, k * P:(k + 1) * P], rows[s][:, k * P:(k + 1) * P], ident[:, :])
                mm.then_inc(S[f"xtp{s}"], 1)

            def project_up(n, s):
                e = pe.value_load(tile_expert[0:1, bass.ds(2 * n + s, 1)], min_val=0, max_val=E0 - 1)
                pe.wait_ge(S[f"xgT{s}"], n + 1)
                pe.wait_ge(S[f"h{s}"], n)
                for o, out in ((0, gp[s]), (I0, up[s])):
                    for k in range(KD):
                        mm = pe.matmul(out[:, :], xgT[s][:, k * P:(k + 1) * P],
                                       wu[:, bass.ds(e, 1), k, o:o + I0].rearrange("p o m -> p (o m)"),
                                       start=(k == 0), stop=(k == KD - 1))
                mm.then_inc(S[f"gup{s}"], 1)

            def turn_h(n, s):
                pe.wait_ge(S[f"hT{s}"], n)
                pe.wait_ge(S[f"h{s}"], n + 1)
                for k in range(KH):
                    mm = pe.transpose(htp[s][:, k * P:(k + 1) * P], h[s][:, k * P:(k + 1) * P], ident[:, :])
                mm.then_inc(S[f"htp{s}"], 1)

            def project_down(n, s):
                e = pe.value_load(tile_expert[0:1, bass.ds(2 * n + s, 1)], min_val=0, max_val=E0 - 1)
                pe.wait_ge(S[f"hT{s}"], n + 1)
                pe.wait_ge(S[f"y{1 - s}"], n + s)
                for k in range(KH):
                    mm = pe.matmul(yp[:, s, :], hT[s][:, k * P:(k + 1) * P],
                                   wd[:, bass.ds(e, 1), k, :].rearrange("p o m -> p (o m)"),
                                   start=(k == 0), stop=(k == KH - 1))
                mm.then_inc(S[f"yp{s}"], 1)

            def step(i, s, first, last, more=True):
                if not last:
                    project_up(i + s, 1 - s)
                turn_h(i, s)
                if more:
                    turn_x(i + 1, s)
                if not first:
                    project_down(i - 1 + s, 1 - s)

            turn_x(0, 0)
            pe.wait_ge(weights_loaded, 16 * 2 * E0)
            project_up(0, 0)
            turn_x(0, 1)
            steps(pe, step)
            project_down(LAST - 1, 1)

        @block.scalar
        def _(act):
            act.preload_act_table_set("silu_and_others")

            def copy_x(n, s):
                act.wait_ge(S[f"xtp{s}"], n + 1)
                act.wait_ge(S[f"gup{s}"], n)
                act.activation(xgT[s][:, :], xtp[:, s, :], ACT.Copy).then_inc(S[f"xgT{s}"], 1)

            def silu(n, s):
                act.wait_ge(S[f"gup{s}"], n + 1)
                act.wait_ge(S[f"h{s}"], n)
                act.activation(sg[s][:, :], gp[s][:, :], ACT.Silu).then_inc(S[f"sg{s}"], 1)

            def copy_y(n, s):
                act.wait_ge(S[f"yp{s}"], n + 1)
                act.wait_ge(S[f"stored{s}"], 16 * n)
                act.activation(y[s][:, :], yp[:, s, :], ACT.Copy).then_inc(S[f"y{s}"], 1)

            def step(i, s, first, last, more=True):
                if not last:
                    silu(i + s, 1 - s)
                if more:
                    copy_x(i + 1, s)
                if not first:
                    copy_y(i - 1 + s, 1 - s)

            copy_x(0, 0)
            silu(0, 0)
            copy_x(0, 1)
            steps(act, step)
            copy_y(LAST - 1, 1)

        @block.vector
        def _(ve):
            def hidden(n, s):
                ve.wait_ge(S[f"sg{s}"], n + 1)
                ve.wait_ge(S[f"htp{s}"], n)
                ve.tensor_tensor(h[s][:, :], up[s][:, :], sg[s][:, :], ALU.mult).then_inc(S[f"h{s}"], 1)

            def copy_h(n, s):
                ve.wait_ge(S[f"htp{s}"], n + 1)
                ve.wait_ge(S[f"yp{s}"], n)
                ve.tensor_copy(hT[s][:, :], htp[s][:, :]).then_inc(S[f"hT{s}"], 1)

            def step(i, s, first, last, more=True):
                copy_h(i, s)
                if not last:
                    hidden(i + s, 1 - s)

            hidden(0, 0)
            steps(ve, step)


def ffn(nc, tag, x, xT, up_w, down_w, scatter, prefetch=None):
    ctx, sb, ps, sem = scope(nc, tag)
    G = TOK // SEQ
    with ctx:
        wu = sb("wu", [P, KD, 2 * I0])
        wd = sb("wd", [P, KH, D])
        sg = [sb(f"sg{s}", [P, SEQ]) for s in range(2)]
        hT = [sb(f"hT{s}", [P, KH, SEQ]) for s in range(2)]
        gp = [ps(f"g{s}", [P, SEQ]) for s in range(2)]
        up = [ps(f"u{s}", [P, SEQ]) for s in range(2)]
        yp = [ps(f"y{s}", [P, CH, D]) for s in range(2)]
        S = {n: sem(n) for n in ("wu", "wd", "gu_mm", "sg_ready", "h_ready0", "h_ready1",
                                 "y_mm0", "y_mm1", "added0", "added1")}
        block = ctx.enter_context(nc.Block())

        @block.sync
        def _(sp):
            sp.dma_start(wu[:, :, :], up_w).then_inc(S["wu"], 16)
            sp.dma_start(wd[:, :, :], down_w).then_inc(S["wd"], 16)
            if prefetch:
                prefetch(sp)

        @block.gpsimd
        def _(pool):
            scatter(pool)

        @block.tensor
        def _(pe):
            def project_up(j):
                for m in range(KH):
                    pe.wait_ge(S[f"h_ready{m % 2}"], 2 * j + m // 2)
                    for out, o in ((gp[m % 2], 0), (up[m % 2], I0)):
                        for k in range(KD):
                            mm = pe.matmul(out[:, :], wu[:, k, o + m * P:o + (m + 1) * P],
                                           xT[:, k, j * SEQ:(j + 1) * SEQ], start=(k == 0), stop=(k == KD - 1))
                    mm.then_inc(S["gu_mm"], 1)

            def project_down(j):
                pe.wait_ge(S["h_ready0"], 2 * j + 2)
                pe.wait_ge(S["h_ready1"], 2 * j + 2)
                pe.wait_ge(S[f"added{j % 2}"], j // 2)
                for c in range(CH):
                    for k in range(KH):
                        mm = pe.matmul(yp[j % 2][:, c, :], hT[j % 2][:, k, c * P:(c + 1) * P], wd[:, k, :],
                                       start=(k == 0), stop=(k == KH - 1))
                mm.then_inc(S[f"y_mm{j % 2}"], 1)

            pe.wait_ge(S["wu"], 16)
            project_up(0)
            pe.wait_ge(S["wd"], 16)
            for j in range(G):
                if j < G - 1:
                    project_up(j + 1)
                project_down(j)

        @block.scalar
        def _(act):
            act.preload_act_table_set("silu_and_others")
            for j in range(G):
                for m in range(KH):
                    act.wait_ge(S["gu_mm"], 4 * j + m + 1)
                    act.wait_ge(S[f"h_ready{m % 2}"], 2 * j + m // 2)
                    act.activation(sg[m % 2][:, :], gp[m % 2][:, :], ACT.Silu).then_inc(S["sg_ready"], 1)

        @block.vector
        def _(ve):
            def hidden(j):
                ve.wait_ge(S[f"y_mm{j % 2}"], j // 2)
                for m in range(KH):
                    ve.wait_ge(S["sg_ready"], 4 * j + m + 1)
                    ve.tensor_tensor(hT[j % 2][:, m, :], sg[m % 2][:, :], up[m % 2][:, :], ALU.mult
                                     ).then_inc(S[f"h_ready{m % 2}"], 1)

            def add(j):
                ve.wait_ge(S[f"y_mm{j % 2}"], j // 2 + 1)
                for c in range(CH):
                    t = j * CH + c
                    ins = ve.tensor_tensor(x[:, t, :], yp[j % 2][:, c, :], x[:, t, :], ALU.add)
                ins.then_inc(S[f"added{j % 2}"], 1)

            hidden(0)
            for j in range(G):
                if j < G - 1:
                    hidden(j + 1)
                add(j)


def scatter_rows(pool, xn, slots, xg, top, sent, last):
    for t in range(NT):
        for k in range(top):
            pool.indirect_dma_start(xg[:, :], bass.IndirectOffsetOnAxis(slots[:, t, k:k + 1], 0), xn[:, t, :], None,
                                    bounds_check=last, oob_is_err=False).then_inc(sent, 16)
    pool.wait_ge(sent, 16 * NT * top)


NH1, DH1 = 16, 16
QG = 4
MASKED = 1e30


def attention(nc, x, xT, ident, A):
    ctx, sb, ps, sem = scope(nc, "attn")
    STEPS = NH1 * CH
    with ctx:
        wqk = sb("wqk", [P, KD, 2 * QG, P])
        wv = sb("wv", [P, KD, D])
        wo = sb("wo", [P, QG, D])
        far = sb("far", [P, SEQ])
        bias = sb("bias", [P, NH1, SEQ])
        xb = sb("xb", [P, KD, SEQ])
        qT = sb("qT", [P, QG, SEQ])
        kT = sb("kT", [P, QG, SEQ])
        v = sb("v", [P, CH, NH1, 2 * DH1])
        T = [sb(f"T{i}", [P, SEQ]) for i in range(3)]
        E = [sb(f"E{i}", [P, SEQ]) for i in range(3)]
        ET = [sb(f"ET{i}", [P, SEQ]) for i in range(2)]
        low = sb("low", [P, STEPS])
        rows = sb("rows", [P, QG, CH, 4])
        diag = [sb(f"diag{i}", [P, P]) for i in range(2)]
        yT = sb("yT", [P, QG, SEQ])
        sc = [ps(f"sc{i}", [P, SEQ]) for i in range(3)]
        tp = [ps(f"tp{i}", [P, SEQ]) for i in range(2)]
        yp = ps("yp", [P, SEQ])
        pj = [ps(f"pj{i}", [P, SEQ]) for i in range(2)]
        yb = (yp, pj[0], pj[1], yp)
        names = ("w", "far", "bias", "xb", "pj_mm", "pj_out", "sc_mm", "T_ready", "E_ready", "inverse_ready", "diag_ready",
                 "tp_mm", "ET_ready", "y_mm", "y_out", "o_mm", "added", "order")
        S = {n: sem(n) for n in names}
        block = ctx.enter_context(nc.Block())

        def step(u):
            g, r, t = u // 16, u % 16 // CH, u % CH
            return g, r, 4 * g + r, t, (t + 1) * P

        NPJ = 2 * QG + CH

        @block.sync
        def _(sp):
            sp.dma_start(wqk[:, :, :, :], A["qk_w"]).then_inc(S["w"], 16)
            sp.dma_start(wv[:, :, :], A["v_w"]).then_inc(S["w"], 16)
            sp.dma_start(wo[:, :, :], A["o_w"]).then_inc(S["w"], 16)

        @block.gpsimd
        def _(pool):
            pool.iota(far[:, :], pattern=[[-1, SEQ]], base=(CH - 1) * P, channel_multiplier=1,
                      allow_small_or_imprecise_dtypes=True).then_inc(S["far"], 1)
            pool.wait_ge(S["far"], 1)
            pool.affine_select(out=far[:, :], in_=far[:, :], compare_op=ALU.is_ge, fill=2 * MASKED * 256.0,
                               base=(CH - 1) * P, pattern=[[-1, SEQ]], channel_multiplier=1).then_inc(S["far"], 1)
            with pool.Fori(0, BATCH) as b:
                for u in range(STEPS):
                    g, r, h, t, n = step(u)
                    pool.wait_ge(S["inverse_ready"], b * STEPS + u + 1)
                    if u > 1:
                        pool.wait_ge(S["tp_mm"], b * STEPS + u - 1)
                    pool.tensor_tensor(diag[u % 2][:, :], ident[:, :], rows[:, g, t, r:r + 1].to_broadcast([P, P]),
                                       ALU.mult).then_inc(S["diag_ready"], 1)

        @block.tensor
        def _(pe):
            pe.wait_ge(S["w"], 48)
            with pe.Fori(0, BATCH) as b:
                u0 = b * STEPS

                def project(n):
                    out = pj[n % 2]
                    pe.wait_ge(S[f"pj_out"], b * NPJ + n - 1 if n > 1 else b * NPJ)
                    if n < 2 * QG:
                        for k in range(KD):
                            mm = pe.matmul(out[:, :], wqk[:, k, n, :], xb[:, k, :], start=(k == 0), stop=(k == KD - 1))
                    else:
                        c = n - 2 * QG
                        for k in range(KD):
                            mm = pe.matmul(out[:, 0:D], xb[:, k, c * P:(c + 1) * P], wv[:, k, :],
                                           start=(k == 0), stop=(k == KD - 1))
                    mm.then_inc(S["pj_mm"], 1)

                def scores(u):
                    g, r, h, t, n = step(u)
                    if u > 2:
                        pe.wait_ge(S["T_ready"], u0 + u - 2)
                    rows_ = slice(32 * r, 32 * r + DH1)
                    pe.matmul(sc[u % 3][:, 0:n], qT[rows_, g, t * P:(t + 1) * P], kT[rows_, g, 0:n],
                              start=True, stop=True).then_inc(S["sc_mm"], 1)

                def turn(u):
                    g, r, h, t, n = step(u)
                    pe.wait_ge(S["diag_ready"], u0 + u + 1)
                    if u > 1:
                        pe.wait_ge(S["ET_ready"], u0 + u - 1)
                    for j in range(t + 1):
                        mm = pe.matmul(tp[u % 2][:, j * P:(j + 1) * P], E[u % 3][:, j * P:(j + 1) * P],
                                       diag[u % 2][:, :], start=True, stop=True)
                    mm.then_inc(S["tp_mm"], 1)

                def mix(u):
                    g, r, h, t, n = step(u)
                    pe.wait_ge(S["ET_ready"], u0 + u + 1)
                    if u == 16 * (QG - 1):
                        pe.wait_ge(S["y_out"], b * QG + 1)
                    for j in range(t + 1):
                        mm = pe.matmul(yb[g][32 * r:32 * r + 32, t * P:(t + 1) * P], v[:, j, h, :],
                                       ET[u % 2][:, j * P:(j + 1) * P], start=(j == 0), stop=(j == t))
                    mm.then_inc(S["y_mm"], 1)

                pe.wait_ge(S["xb"], b + 1)
                for n in range(NPJ):
                    project(n)
                pe.wait_ge(S["pj_out"], (b + 1) * NPJ)
                for u in range(3):
                    scores(u)
                for u in range(STEPS):
                    if u + 3 < STEPS:
                        scores(u + 3)
                    turn(u)
                    if u:
                        mix(u - 1)
                mix(STEPS - 1)
                pe.wait_ge(S["y_out"], (b + 1) * QG)
                for c in range(CH):
                    out = pj[c // 2][:, (c % 2) * D:(c % 2 + 1) * D]
                    for g in range(QG):
                        mm = pe.matmul(out, yT[:, g, c * P:(c + 1) * P], wo[:, g, :], start=(g == 0), stop=(g == QG - 1))
                mm.then_inc(S["o_mm"], 1)

        @block.scalar
        def _(act):
            act.preload_act_table_set("natural_log_exp_and_others")
            act.wait_ge(S["w"], 48)
            with act.Fori(0, BATCH) as b:
                u0 = b * STEPS
                act.wait_ge(S["o_mm"], b)
                for n in range(NPJ):
                    act.wait_ge(S["pj_mm"], b * NPJ + n + 1)
                    if n < QG:
                        ins = act.activation(qT[:, n, :], pj[n % 2][:, :], ACT.Copy, scale=-float(DH1) ** -0.5)
                    elif n < 2 * QG:
                        ins = act.activation(kT[:, n - QG, :], pj[n % 2][:, :], ACT.Copy)
                    else:
                        ins = act.activation(v[:, n - 2 * QG, :, 0:DH1],
                                             pj[n % 2][:, 0:D].rearrange("p (h d) -> p h d", h=NH1), ACT.Copy)
                    ins.then_inc(S["pj_out"], 1)

                def take_y(g):
                    act.wait_ge(S["y_mm"], u0 + 16 * (g + 1))
                    act.activation(yT[:, g, :], yb[g][:, :], ACT.Copy).then_inc(S["y_out"], 1)

                for u in range(STEPS):
                    g, r, h, t, n = step(u)
                    act.wait_ge(S["T_ready"], u0 + u + 1)
                    if u > 2:
                        act.wait_ge(S["tp_mm"], u0 + u - 2)
                    act.activation(E[u % 3][:, 0:n], T[u % 3][:, 0:n], ACT.Exp, bias=low[:, u:u + 1], scale=-1.0,
                                   accum_out=rows[:, g, t, r:r + 1]).then_inc(S["E_ready"], 1)
                    if u % 16 == 3 and u > 3:
                        take_y(u // 16 - 1)
                take_y(QG - 1)

        @block.vector
        def _(ve):
            link = Chain(ve, S["order"])
            link(ve.memset(v[:, :, :, :], 0.0))
            ve.wait_ge(S["far"], 2)
            for h in range(NH1):
                ins = ve.tensor_scalar(bias[:, h, :], far[:, :], 2.0 ** (-8.0 / (h + 1)), None, ALU.mult)
            link(ins)
            with ve.Fori(0, BATCH) as b:
                link.restart()
                u0 = b * STEPS
                ve.wait_ge(S["pj_mm"], b * NPJ)
                ve.tensor_copy(xb[:, :, :], xT[:, :, bass.ds(b * SEQ, SEQ)]).then_inc(S["xb"], 1)

                def negated(u):
                    g, r, h, t, n = step(u)
                    ve.tensor_tensor_reduce(T[u % 3][:, 0:n], sc[u % 3][:, 0:n], bias[:, h, SEQ - n:], 1.0, 3e38,
                                            ALU.add, ALU.min, low[:, u:u + 1]).then_inc(S["T_ready"], 1)

                def copied(u):
                    g, r, h, t, n = step(u)
                    if u + 3 < STEPS:
                        ve.wait_ge(S["sc_mm"], u0 + u + 4)
                    ve.wait_ge(S["tp_mm"], u0 + u + 1)
                    if u > 1:
                        ve.wait_ge(S["y_mm"], u0 + u - 1)
                    ve.tensor_copy(ET[u % 2][:, 0:n], tp[u % 2][:, 0:n]).then_inc(S["ET_ready"], 1)

                def inverse(u):
                    g, r, h, t, n = step(u)
                    ve.wait_ge(S["E_ready"], u0 + u + 1)
                    ve.reciprocal(rows[:, g, t, r:r + 1], rows[:, g, t, r:r + 1]).then_inc(S["inverse_ready"], 1)

                ve.wait_ge(S["sc_mm"], u0 + 3)
                link(ve.memset(low[:, 0:2], 0.0))
                for u in range(3):
                    negated(u)
                inverse(0)
                for u in range(STEPS):
                    if u + 1 < STEPS:
                        inverse(u + 1)
                    copied(u)
                    if u + 3 < STEPS:
                        negated(u + 3)
                ve.wait_ge(S["o_mm"], b + 1)
                for c in range(2):
                    xs = x[:, bass.ds(b * CH + 2 * c, 2), :]
                    ins = ve.tensor_tensor(xs, pj[c][:, :].rearrange("p (c d) -> p c d", c=2), xs, ALU.add)
                ins.then_inc(S["added"], 1)


E1, F1, TOP, CAP = 64, 64, 4, 32
SLOTS = E1 * CAP
EG = P // CAP
NG = E1 // EG


def route1(nc, xT, slots, reads, wk, before, ones, xg, A):
    ctx, sb, ps, sem = scope(nc, "route")
    U32 = mybir.dt.uint32
    with ctx:
        w = sb("w", [P, KD, E1])
        rb = sb("rb", [P, E1])
        lg = sb("lg", [P, NT, E1])
        score = sb("score", [P, NT, E1])
        one = sb("one", [P, NT])
        top = sb("top", [P, NT, 8])
        idx = sb("idx", [P, NT, 8], U32)
        idf = sb("idf", [P, NT, 8])
        col = sb("col", [P, E1])
        first = sb("first", [P, E1])
        hit = [sb(f"hit{k}", [P, NT, E1]) for k in range(TOP)]
        mask = sb("mask", [P, NT, E1])
        prior = sb("prior", [P, NT, E1])
        place = sb("place", [P, NT, E1])
        tmp = sb("tmp", [P, NT, E1])
        sf = sb("sf", [P, NT, TOP])
        zero = sb("zero", [P, 4 * D])
        logits = ps("logits", [P, NT, E1])
        rank = ps("rank", [P, NT, E1])
        S = {n: sem(n) for n in ("w", "mm", "order", "shifted", "exp", "col", "zero", "filled", "mask", "rank")}
        block = ctx.enter_context(nc.Block())

        @block.sync
        def _(sp):
            sp.dma_start(w[:, :, :], A["router_w"]).then_inc(S["w"], 16)
            sp.dma_start(rb[:, :], A["router_b"].to_broadcast([P, E1])).then_inc(S["w"], 16)
            sp.wait_ge(S["zero"], 1)
            for g in range(4):
                sp.dma_start(xg[512 * g:512 * g + 512, :].rearrange("(p c) d -> p (c d)", p=P), zero[:, :]
                             ).then_inc(S["filled"], 16)

        @block.gpsimd
        def _(pool):
            pool.memset(zero[:, :], 0.0).then_inc(S["zero"], 1)
            pool.iota(col[:, :], pattern=[[1, E1]], base=0, channel_multiplier=0,
                      allow_small_or_imprecise_dtypes=True).then_inc(S["col"], 1)
            pool.iota(first[:, :], pattern=[[CAP, E1]], base=0, channel_multiplier=0,
                      allow_small_or_imprecise_dtypes=True).then_inc(S["col"], 1)
            pool.wait_ge(S["filled"], 64)

        @block.tensor
        def _(pe):
            pe.wait_ge(S["w"], 32)
            for t in range(NT):
                for k in range(KD):
                    mm = pe.matmul(logits[:, t, :], xT[:, k, t * P:(t + 1) * P], w[:, k, :],
                                   start=(k == 0), stop=(k == KD - 1))
            mm.then_inc(S["mm"], 1)
            pe.wait_ge(S["mask"], NT - 1)
            for t in range(NT):
                pe.matmul(rank[:, t, :], before[:, :], mask[:, t, :], start=True, stop=False)
                mm = pe.matmul(rank[:, t, :], ones[:, :], prior[:, t, :], start=False, stop=True)
            mm.then_inc(S["rank"], 1)

        @block.scalar
        def _(act):
            act.wait_ge(S["shifted"], 1)
            act.activation(score[:, :, :], score[:, :, :], ACT.Exp).then_inc(S["exp"], 1)

        @block.vector
        def _(ve):
            link = Chain(ve, S["order"])
            wide = lambda t: t.unsqueeze(2).to_broadcast([P, NT, E1])
            tall = lambda t: t[:, :].unsqueeze(1).to_broadcast([P, NT, E1])
            ve.wait_ge(S["mm"], 1)
            ve.wait_ge(S["w"], 32)
            link(ve.tensor_reduce(one[:, :], logits[:, :, :], AX_X, ALU.max))
            ve.tensor_tensor(score[:, :, :], logits[:, :, :], wide(one[:, :]), ALU.subtract).then_inc(S["shifted"], 1)
            link(ve.tensor_tensor(lg[:, :, :], logits[:, :, :], tall(rb), ALU.add))
            for t in range(NT):
                ins = ve.max(top[:, t, :], lg[:, t, :])
            link(ins)
            for t in range(NT):
                ins = ve.max_index(idx[:, t, :], top[:, t, :], lg[:, t, :])
            link(ins)
            link(ve.tensor_copy(idf[:, :, :], idx[:, :, :]))
            ve.wait_ge(S["col"], 2)
            for k in range(TOP):
                link(ve.tensor_tensor(hit[k][:, :, :], tall(col), wide(idf[:, :, k]), ALU.is_equal))
            link(ve.tensor_tensor(mask[:, :, :], hit[0][:, :, :], hit[1][:, :, :], ALU.add))
            link(ve.tensor_tensor(mask[:, :, :], mask[:, :, :], hit[2][:, :, :], ALU.add))
            link(ve.tensor_tensor(mask[:, :, :], mask[:, :, :], hit[3][:, :, :], ALU.add))
            link(ve.memset(prior[:, 0, :], 0.0))
            for t in range(1, NT):
                ve.tensor_tensor(prior[:, t, :], prior[:, t - 1, :], mask[:, t - 1, :], ALU.add
                                 ).then_inc(S["mask"], 1)
                ve.wait_ge(S["mask"], t)
            ve.wait_ge(S["exp"], 1)
            link(ve.tensor_reduce(one[:, :], score[:, :, :], AX_X, ALU.add))
            link(ve.reciprocal(one[:, :], one[:, :]))
            link(ve.tensor_tensor(score[:, :, :], score[:, :, :], wide(one[:, :]), ALU.mult))
            for k in range(TOP):
                link(ve.tensor_tensor(tmp[:, :, :], hit[k][:, :, :], score[:, :, :], ALU.mult))
                link(ve.tensor_reduce(wk[:, :, k], tmp[:, :, :], AX_X, ALU.add))
            link(ve.tensor_reduce(one[:, :], wk[:, :, :], AX_X, ALU.add))
            link(ve.reciprocal(one[:, :], one[:, :]))
            link(ve.tensor_tensor(wk[:, :, :], wk[:, :, :], one[:, :].unsqueeze(2).to_broadcast([P, NT, TOP]), ALU.mult))
            ve.wait_ge(S["rank"], 1)
            link(ve.tensor_scalar(tmp[:, :, :], rank[:, :, :], float(CAP), float(4 * SLOTS), ALU.is_ge, ALU.mult))
            link(ve.tensor_tensor(place[:, :, :], rank[:, :, :], tmp[:, :, :], ALU.add))
            link(ve.tensor_tensor(place[:, :, :], place[:, :, :], tall(first), ALU.add))
            for k in range(TOP):
                link(ve.tensor_tensor(tmp[:, :, :], hit[k][:, :, :], place[:, :, :], ALU.mult))
                link(ve.tensor_reduce(sf[:, :, k], tmp[:, :, :], AX_X, ALU.add))
            ve.tensor_copy(slots[:, :, :], sf[:, :, :])
            kept = tmp[:, :, 0:TOP]
            link(ve.tensor_scalar(kept, sf[:, :, :], float(SLOTS), None, ALU.is_lt))
            link(ve.tensor_tensor(wk[:, :, :], wk[:, :, :], kept, ALU.mult))
            link(ve.tensor_scalar(sf[:, :, :], sf[:, :, :], float(SLOTS - 1), None, ALU.min))
            link(ve.tensor_copy(reads[:, :, :], sf[:, :, :]))


def experts1(nc, ident, xg, yg, A):
    ctx, sb, ps, sem = scope(nc, "exp1")
    with ctx:
        rows = [sb(f"rows{s}", [P, D]) for s in range(2)]
        up_w = [sb(f"up_w{s}", [P, KD, EG, 2 * F1]) for s in range(2)]
        down_w = [sb(f"down_w{s}", [P, EG, D]) for s in range(2)]
        xgT = [sb(f"xgT{s}", [P, D]) for s in range(2)]
        sg = [sb(f"sg{s}", [P, F1]) for s in range(2)]
        h = [sb(f"h{s}", [P, P]) for s in range(2)]
        hT = [sb(f"hT{s}", [P, P]) for s in range(2)]
        y = [sb(f"y{s}", [P, D]) for s in range(2)]
        xtp = [ps(f"xtp{s}", [P, 512]) for s in range(2)]
        gup = [ps(f"gup{s}", [P, 512]) for s in range(2)]
        htp = [ps(f"htp{s}", [P, 512]) for s in range(2)]
        yp = [ps(f"yp{s}", [P, 512]) for s in range(2)]
        names = ("rows", "up_w", "down_w", "xtp", "xgT", "gup", "sg", "h", "htp", "hT", "yp", "y", "stored")
        S = {f"{n}{s}": sem(f"{n}{s}") for n in names for s in range(2)}
        S["padded"] = sem("padded")
        block = ctx.enter_context(nc.Block())

        @block.sync
        def _(sp):
            with sp.Fori(0, NG // 2) as i:
                for s in range(2):
                    g = bass.ds(2 * i + s, 1)
                    sp.wait_ge(S[f"xtp{s}"], i)
                    sp.dma_start(rows[s][:, :], xg[bass.ds((2 * i + s) * P, P), :]).then_inc(S[f"rows{s}"], 16)
                    sp.wait_ge(S[f"gup{s}"], i)
                    sp.dma_start(up_w[s][:, :, :, :], A["up1_w"][g].rearrange("o p k e f -> p (o k) e f")
                                 ).then_inc(S[f"up_w{s}"], 16)
                    sp.wait_ge(S[f"yp{s}"], i)
                    sp.dma_start(down_w[s][0:F1, :, :], A["down1_w"][g].rearrange("o f e d -> f (o e) d")
                                 ).then_inc(S[f"down_w{s}"], 16)

        @block.gpsimd
        def _(pool):
            with pool.Fori(0, NG // 2) as i:
                for s in range(2):
                    pool.wait_ge(S[f"y{s}"], i + 1)
                    pool.wait_ge(S["rows0"], 16)
                    pool.dma_start(yg[bass.ds((2 * i + s) * P, P), :], y[s][:, :]).then_inc(S[f"stored{s}"], 16)
            for s in range(2):
                pool.wait_ge(S[f"stored{s}"], 16 * (NG // 2))

        @block.tensor
        def _(pe):
            def head(n, s):
                pe.wait_ge(S[f"rows{s}"], 16 * n + 16)
                pe.wait_ge(S[f"xgT{s}"], n)
                for k in range(KD):
                    mm = pe.transpose(xtp[s][:, k * P:(k + 1) * P], rows[s][:, k * P:(k + 1) * P], ident[:, :])
                mm.then_inc(S[f"xtp{s}"], 1)
                pe.wait_ge(S[f"up_w{s}"], 16 * n + 16)
                pe.wait_ge(S[f"h{s}"], n)
                pe.wait_ge(S[f"xgT{s}"], n + 1)
                for e in range(EG):
                    r = slice(e * CAP, (e + 1) * CAP)
                    for k in range(KD):
                        mm = pe.matmul(gup[s][r, 0:2 * F1], xgT[s][:, k * P + e * CAP:k * P + (e + 1) * CAP],
                                       up_w[s][:, k, e, :], start=(k == 0), stop=(k == KD - 1))
                mm.then_inc(S[f"gup{s}"], 1)

            def tail(n, s):
                pe.wait_ge(S[f"hT{s}"], n)
                pe.wait_ge(S[f"h{s}"], n + 1)
                pe.transpose(htp[s][:, 0:P], h[s][:, :], ident[:, :]).then_inc(S[f"htp{s}"], 1)
                pe.wait_ge(S[f"hT{s}"], n + 1)
                pe.wait_ge(S[f"y{s}"], n)
                pe.wait_ge(S[f"down_w{s}"], 16 * n + 16)
                for e in range(EG):
                    r = slice(e * CAP, (e + 1) * CAP)
                    mm = pe.matmul(yp[s][r, 0:D], hT[s][:, r], down_w[s][:, e, :], start=True, stop=True)
                mm.then_inc(S[f"yp{s}"], 1)

            pe.wait_ge(S["padded"], 4)
            head(0, 0)
            with pe.Fori(0, NG // 2 - 1) as i:
                head(i, 1)
                tail(i, 0)
                head(i + 1, 0)
                tail(i, 1)
            n = NG // 2 - 1
            head(n, 1)
            tail(n, 0)
            tail(n, 1)

        @block.scalar
        def _(act):
            act.preload_act_table_set("silu_and_others")

            def head(n, s):
                act.wait_ge(S[f"xtp{s}"], n + 1)
                act.wait_ge(S[f"gup{s}"], n)
                act.activation(xgT[s][:, :], xtp[s][:, 0:D], ACT.Copy).then_inc(S[f"xgT{s}"], 1)
                act.wait_ge(S[f"gup{s}"], n + 1)
                act.wait_ge(S[f"h{s}"], n)
                act.activation(sg[s][:, :], gup[s][:, 0:F1], ACT.Silu).then_inc(S[f"sg{s}"], 1)

            with act.Fori(0, NG // 2) as i:
                head(i, 0)
                head(i, 1)

        @block.vector
        def _(ve):
            def head(n, s):
                ve.wait_ge(S[f"htp{s}"], n)
                ve.wait_ge(S[f"sg{s}"], n + 1)
                ve.tensor_tensor(h[s][:, 0:F1], gup[s][:, F1:2 * F1], sg[s][:, :], ALU.mult).then_inc(S[f"h{s}"], 1)

            def tail(n, s):
                ve.wait_ge(S[f"htp{s}"], n + 1)
                ve.wait_ge(S[f"yp{s}"], n)
                ve.tensor_copy(hT[s][:, :], htp[s][:, 0:P]).then_inc(S[f"hT{s}"], 1)
                ve.wait_ge(S[f"yp{s}"], n + 1)
                ve.wait_ge(S[f"stored{s}"], 16 * n)
                ve.tensor_copy(y[s][:, :], yp[s][:, 0:D]).then_inc(S[f"y{s}"], 1)

            for s in range(2):
                ve.memset(h[s][:, F1:], 0.0).then_inc(S["padded"], 1)
                ve.memset(down_w[s][F1:, :, :], 0.0).then_inc(S["padded"], 1)
            ve.wait_ge(S["padded"], 4)
            head(0, 0)
            with ve.Fori(0, NG // 2 - 1) as i:
                head(i, 1)
                tail(i, 0)
                head(i + 1, 0)
                tail(i, 1)
            n = NG // 2 - 1
            head(n, 1)
            tail(n, 0)
            tail(n, 1)


def combine(nc, tag, x, reads, wk, yg, top):
    ctx, sb, ps, sem = scope(nc, tag)
    R = 8
    with ctx:
        row = [sb(f"row{i}", [P, D]) for i in range(R)]
        come = [sem(f"come{i}") for i in range(R)]
        used = sem("used")
        block = ctx.enter_context(nc.Block())

        @block.gpsimd
        def _(pool):
            for n in range(NT * top):
                t, k = n // top, n % top
                if n >= R:
                    pool.wait_ge(used, n - R + 1)
                pool.indirect_dma_start(row[n % R][:, :], None, yg[:, :], bass.IndirectOffsetOnAxis(reads[:, t, k:k + 1], 0)
                                        ).then_inc(come[n % R], 16)

        @block.vector
        def _(ve):
            for n in range(NT * top):
                t, k = n // top, n % top
                ve.wait_ge(come[n % R], 16 * (n // R) + 16)
                if n:
                    ve.wait_ge(used, n)
                ve.scalar_tensor_tensor(x[:, t, :], row[n % R][:, :], wk[:, t, k:k + 1], x[:, t, :],
                                        ALU.mult, ALU.add).then_inc(used, 1)


def gated_bias_setup(nc, norm_w, gb, gate, A):
    ctx, sb, ps, sem = scope(nc, "gb")
    with ctx:
        ld = sem("ld")
        done = sem("done")
        block = ctx.enter_context(nc.Block())

        @block.sync
        def _(sp):
            sp.dma_start(norm_w[:, :], A["norm_w"]).then_inc(ld, 16)
            sp.dma_start(gb[:, :], A["out_b"].to_broadcast([P, D])).then_inc(ld, 16)
            sp.dma_start(gate[:, :], A["res_gate"].to_broadcast([P, 1])).then_inc(ld, 16)

        @block.vector
        def _(ve):
            ve.wait_ge(ld, 48)
            ve.tensor_scalar(gb[:, :], gb[:, :], gate[:, 0:1], None, ALU.mult).then_inc(done, 1)
            ve.wait_ge(done, 1)


def store(nc, x, out):
    ctx, sb, ps, sem = scope(nc, "st")
    with ctx:
        done = sem("done")
        block = ctx.enter_context(nc.Block())

        @block.sync
        def _(sp):
            sp.dma_start(out.rearrange("(t p) d -> p t d", p=P), x[:, :, :]).then_inc(done, 16)
            sp.wait_ge(done, 16)


def program(nc, A):
    USED.clear()
    with ExitStack() as ctx:
        sb = lambda name, shape: ctx.enter_context(nc.sbuf_tensor(name, shape, F32))
        x = sb("x", [P, NT, D])
        xT = sb("xT", [P, KD, TOK])
        ident, tri, after, ones = (sb(n, [P, P]) for n in ("ident", "upto", "after", "ones"))
        constants(nc, ident, tri, after, ones)
        with ExitStack() as early:
            norm_w, gb, gate = (early.enter_context(nc.sbuf_tensor(n, [P, m], F32))
                                for n, m in (("norm_w", KD), ("gb", D), ("gate", 1)))
            gated_bias_setup(nc, norm_w, gb, gate, A)
            normalise(nc, "n0", x, xT, ident, x_dram=A["x"], rms=(norm_w[:, :], gb[:, :]))
        mixer(nc, x, xT, ident, tri, after, ones, A)
        before = sb("before", [P, P])
        clear_semaphores(nc)
        strict(nc, before, tri, ident)
        moe0(nc, x, xT, ident, before, ones, A)
        normalise(nc, "n2", x, xT, ident)
        attention(nc, x, xT, ident, A)
        xg = nc.dram_tensor("slot_rows", [SLOTS, D], F32).ap()
        yg = nc.dram_tensor("slot_results", [SLOTS, D], F32).ap()
        xn = sb("xn", [P, NT, D])
        slots = ctx.enter_context(nc.sbuf_tensor("slots", [P, NT, TOP], mybir.dt.uint32))
        reads = ctx.enter_context(nc.sbuf_tensor("reads", [P, NT, TOP], mybir.dt.uint32))
        wk = sb("wk", [P, NT, TOP])
        normalise(nc, "n3", x, xT, ident, rows=xn)
        route1(nc, xT, slots, reads, wk, before, ones, xg, A)
        sent = ctx.enter_context(nc.semaphore("sent1"))
        ffn(nc, "shared", x, xT, A["shup_w"][0], A["shdown_w"][0],
            lambda pool: scatter_rows(pool, xn, slots, xg, TOP, sent, SLOTS - 1))
        experts1(nc, ident, xg, yg, A)
        combine(nc, "comb1", x, reads, wk, yg, TOP)
        store(nc, x, A["out"])


def strict(nc, before, upto, ident):
    ctx, sb, ps, sem = scope(nc, "strict")
    with ctx:
        done = sem("done")
        block = ctx.enter_context(nc.Block())

        @block.vector
        def _(ve):
            ve.tensor_tensor(before[:, :], upto[:, :], ident[:, :], ALU.subtract).then_inc(done, 1)
            ve.wait_ge(done, 1)


def layouts(i):
    i = {k: np.asarray(v) for k, v in i.items()}
    c = np.ascontiguousarray
    a = {}
    a["x"] = c(i["L0_attn_hidden_states"].reshape(TOK, D))
    a["norm_w"] = c(i["L0_attn_norm_w"].reshape(KD, P).T)
    a["out_b"] = c(i["L0_attn_out_proj_b"][None])
    a["res_gate"] = c(i["L0_attn_res_gate"][None])
    w = i["L0_attn_in_proj_w"].T.reshape(KD, P, 2, KI, P)
    a["in_w"] = c(w.transpose(3, 1, 2, 0, 4).reshape(KI, P, 2 * KD, P))
    a["in_b"] = c(i["L0_attn_in_proj_b"].reshape(2 * KI, P).T)
    a["conv_w"] = c(i["L0_attn_conv_w"].reshape(KI, P, 4).transpose(1, 0, 2))
    a["conv_b"] = c(i["L0_attn_conv_b"].reshape(KI, P).T)
    xw = i["L0_attn_x_proj_w"].reshape(NH0, 1 + 2 * NS, DI)
    xb = i["L0_attn_x_proj_b"].reshape(NH0, 1 + 2 * NS)
    bc = xw[:, 1:].reshape(PAIRS, 2, 2, NS, KI, P)
    a["bc_w"] = c(bc.transpose(0, 2, 5, 4, 1, 3).reshape(PAIRS * 2, P, KI, P))
    a["bc_b"] = c(xb[:, 1:].reshape(PAIRS, 2, 2, NS).transpose(1, 3, 0, 2).reshape(P, PAIRS, 2))
    means = np.zeros((DI, NH0), np.float32)
    means[np.arange(DI), np.arange(DI) // DH] = 1.0 / DH
    pad = np.zeros((DI, DTC - 2 * NH0), np.float32)
    a["dt_w"] = c(np.concatenate([xw[:, 0].T, means, pad], 1).reshape(KI, P, DTC).transpose(1, 0, 2))
    a["par"] = c(np.concatenate([i["L0_attn_A_log"], i["L0_attn_log2_alpha_base"], i["L0_attn_log2_beta"],
                                 i["L0_attn_surprise_ema"], xb[:, 0], i["L0_attn_res_gate"]])[None])
    a["out_w"] = c(i["L0_attn_out_proj_w"].T.reshape(KI, P, D).transpose(1, 0, 2))
    a["gate0_w"] = c(i["L0_ffn_gate_w"].reshape(KD, P, E0).transpose(1, 0, 2))
    up = np.concatenate([i["L0_ffn_expert_gate_up"], i["L0_ffn_base_gate_up"][None]])
    a["up0_w"] = c(up.reshape(E0 + 1, KD, P, 2 * I0).transpose(0, 2, 1, 3))
    down = np.concatenate([i["L0_ffn_expert_down"], i["L0_ffn_base_down"][None]])
    a["down0_w"] = c(down.reshape(E0 + 1, KH, P, D).transpose(0, 2, 1, 3))
    qkv = i["L1_attn_W_qkv"].reshape(KD, P, 3, QG, 4, DH1)
    strips = np.zeros((P, KD, 2, QG, 4, 2, DH1), np.float32)
    strips[:, :, :, :, :, 0] = qkv[:, :, 0:2].transpose(1, 0, 2, 3, 4, 5)
    a["qk_w"] = c(strips.reshape(P, KD, 2 * QG, P))
    a["v_w"] = c(qkv[:, :, 2].reshape(KD, P, D).transpose(1, 0, 2))
    strips = np.zeros((4, 2, DH1, QG, D), np.float32)
    strips[:, 0] = i["L1_attn_W_o"].reshape(QG, 4, DH1, D).transpose(1, 2, 0, 3)
    a["o_w"] = c(strips.reshape(P, QG, D))
    a["router_w"] = c(i["L1_ffn_router_w"].T.reshape(KD, P, E1).transpose(1, 0, 2))
    a["router_b"] = c(i["L1_ffn_router_bias"][None])
    gu = np.stack([i["L1_ffn_gate_w"], i["L1_ffn_up_w"]], 1).reshape(NG, EG, 2, F1, KD, P)
    a["up1_w"] = c(gu.transpose(0, 5, 4, 1, 2, 3).reshape(NG, P, KD, EG, 2 * F1))
    a["down1_w"] = c(i["L1_ffn_down_w"].reshape(NG, EG, D, F1).transpose(0, 3, 1, 2))
    sh = np.concatenate([i["L1_ffn_sh_gate_w"].reshape(I0, D), i["L1_ffn_sh_up_w"].reshape(I0, D)])
    a["shup_w"] = c(sh.T.reshape(1, KD, P, 2 * I0).transpose(0, 2, 1, 3))
    a["shdown_w"] = c(i["L1_ffn_sh_down_w"].transpose(0, 2, 1).reshape(1, KH, P, D).transpose(0, 2, 1, 3))
    return a


def kernel(**inputs):
    from concourse import bacc
    from concourse.bass_utils import run_bass_kernel_spmd

    arrays = layouts(inputs)
    nc = bacc.Bacc("TRN2", target_bir_lowering=False, num_devices=1)
    A = {n: nc.dram_tensor(f"in_{n}", a.shape, mybir.dt.from_np(a.dtype), kind="ExternalInput").ap()
         for n, a in arrays.items()}
    A["out"] = nc.dram_tensor("out", [TOK, D], F32, kind="ExternalOutput").ap()
    program(nc, A)
    r = run_bass_kernel_spmd(nc, [{f"in_{n}": a for n, a in arrays.items()}], core_ids=[0])
    return r.results[0]["out"].reshape(BATCH, SEQ, D)
```
